# Optimizing a Trainium2 kernel written in Bass

```python
import numpy as np
import jax
import jax.numpy as jnp

def _softmax(x, axis=-1):
    return jax.nn.softmax(x, axis=axis)

def _gelu(x):
    return jax.nn.gelu(x, approximate=True)

def _silu(x):
    return jax.nn.silu(x)

def _sigmoid(x):
    return jax.nn.sigmoid(x)

def _layernorm(x, axis=-1, eps=1e-05):
    m = jnp.mean(x, axis=axis, keepdims=True)
    v = jnp.var(x, axis=axis, keepdims=True)
    return (x - m) / jnp.sqrt(v + eps)

def _scatter_add(tgt, idx, src, axis=0):
    return tgt.at[idx].add(src)

def _segment_sum(src, seg, n):
    return jax.ops.segment_sum(src, seg, n)
kernel_name = 'mk_xattn_seq_d4_seqx_r8_dc0552'

def setup_inputs(seed: int=0):
    np.random.seed(seed)
    _w = jnp.asarray

    def _rec_inputs():
        import jax
        import jax.numpy as jnp
        _rk = jax.random.key(seed)
        x = 7.22e-05 + 1 * jax.random.normal(jax.random.fold_in(_rk, 1), (16, 128, 256), jnp.float32)
        _lenS = 128 - jax.random.randint(jax.random.fold_in(_rk, 7), (16,), 0, max(1, 128 // 4) + 1, jnp.int32)
        _lenS2 = 128 - jax.random.randint(jax.random.fold_in(_rk, 8), (16,), 0, max(1, 128 // 4) + 1, jnp.int32)
        _ctx_2048P = jax.random.normal(jax.random.fold_in(_rk, 11), (16, 16, 256), jnp.float32)
        _ctx_2048c = jax.random.dirichlet(jax.random.fold_in(_rk, 511), 0.3 * jnp.ones((16,), jnp.float32), (16, 128))
        _ctx_2048t = jnp.einsum('bsk,bkd->bsd', _ctx_2048c, _ctx_2048P)
        _ctx_2048t = _ctx_2048t * jax.lax.rsqrt(jnp.mean(jnp.square(_ctx_2048t)) + 1e-12) * 0.953939
        ctx_2048 = 2.81802e-05 + 1.00001 * (_ctx_2048t + 0.3 * jax.random.normal(jax.random.fold_in(_rk, 611), (16, 128, 256), jnp.float32))
        _validS = jnp.arange(128)[None, :] < _lenS[:, None]
        _validS2 = jnp.arange(128)[None, :] < _lenS2[:, None]
        _causal = jnp.tril(jnp.ones((128, 128), dtype=bool))
        mask_BxS2_bf1 = jnp.ones((16, 128), dtype=bool)
        mask_Bx1xSxS2_ff0 = jnp.where(jnp.ones((16, 1, 128, 128), dtype=bool), 0.0, -1000000000.0).astype(jnp.float32)
        mask_BxS2_ik0 = jnp.where(jnp.broadcast_to(_validS2[:, :], (16, 128)), 0, 1).astype(jnp.int32)
        return (x, ctx_2048, mask_BxS2_bf1, mask_Bx1xSxS2_ff0, mask_BxS2_ik0)
    x, ctx_2048, mask_BxS2_bf1, mask_Bx1xSxS2_ff0, mask_BxS2_ik0 = _rec_inputs()

    def _L0_xattn_setup():
        import jax, jax.numpy as jnp
        import numpy as np
        D = 256
        H = 16
        HD = D // H
        INNER = 4 * D
        EPS = 1e-05

        def layer_norm(x, w, b):
            mu = jnp.mean(x, axis=-1, keepdims=True)
            var = jnp.mean(jnp.square(x - mu), axis=-1, keepdims=True)
            return (x - mu) * jax.lax.rsqrt(var + EPS) * w + b
        key = jax.random.key(seed)
        ks = jax.random.split(key, 12)
        B, LQ, LK = (4, 128, 256)
        std = 0.02
        inp = {'hidden_states': jax.random.normal(ks[0], (B, LQ, D), jnp.float32), 'encoder_hidden_states': jax.random.normal(ks[1], (B, LK, D), jnp.float32), 'encoder_attention_mask': jnp.ones((B, LK), dtype=bool), 'ln1_w': jnp.ones((D,), jnp.float32), 'ln1_b': jnp.zeros((D,), jnp.float32), 'q_w': jax.random.normal(ks[2], (D, D), jnp.float32) * std, 'q_b': jnp.zeros((D,), jnp.float32), 'k_w': jax.random.normal(ks[3], (D, D), jnp.float32) * std, 'k_b': jnp.zeros((D,), jnp.float32), 'v_w': jax.random.normal(ks[4], (D, D), jnp.float32) * std, 'v_b': jnp.zeros((D,), jnp.float32), 'cproj_w': jax.random.normal(ks[5], (D, D), jnp.float32) * std, 'cproj_b': jnp.zeros((D,), jnp.float32), 'ln2_w': jnp.ones((D,), jnp.float32), 'ln2_b': jnp.zeros((D,), jnp.float32), 'fc_w': jax.random.normal(ks[6], (D, INNER), jnp.float32) * std, 'fc_b': jnp.zeros((INNER,), jnp.float32), 'proj_w': jax.random.normal(ks[7], (INNER, D), jnp.float32) * std, 'proj_b': jnp.zeros((D,), jnp.float32)}
        return inp
    _L0_xattn_all = _L0_xattn_setup()
    _L0_xattn_in = {k: v for k, v in _L0_xattn_all.items() if k in ('ln1_w', 'ln1_b', 'q_w', 'q_b', 'k_w', 'k_b', 'v_w', 'v_b', 'cproj_w', 'cproj_b', 'ln2_w', 'ln2_b', 'fc_w', 'fc_b', 'proj_w', 'proj_b')}
    del _L0_xattn_all

    def _L1_xattn_setup():
        import jax, jax.numpy as jnp
        import numpy as np
        H = 256
        NH = 32
        KVH = 8
        HD = H // NH
        GROUPS = NH // KVH
        EPS = 1e-06
        B, L, S = (4, 128, 128)

        def _gqa_forward(hidden_state, encoder_hidden_state, encoder_attention_mask, Wq, bq, Wk, bk, Wv, bv, Wo, bo, gamma, beta):
            b, l, _ = hidden_state.shape
            s = encoder_hidden_state.shape[1]
            q = hidden_state @ Wq + bq
            k = encoder_hidden_state @ Wk + bk
            v = encoder_hidden_state @ Wv + bv
            q = q.reshape(b, l, KVH, GROUPS, HD).transpose(0, 2, 3, 1, 4)
            k = k.reshape(b, s, KVH, HD).transpose(0, 2, 1, 3)
            v = v.reshape(b, s, KVH, HD).transpose(0, 2, 1, 3)
            scale = 1.0 / jnp.sqrt(jnp.asarray(HD, q.dtype))
            scores = jnp.einsum('bkgld,bksd->bkgls', q, k) * scale
            scores = scores + encoder_attention_mask[:, :, None, :, :]
            attn = jax.nn.softmax(scores, axis=-1)
            out = jnp.einsum('bkgls,bksd->bkgld', attn, v)
            out = out.transpose(0, 3, 1, 2, 4).reshape(b, l, H)
            out = out @ Wo + bo
            x = out + hidden_state
            mu = jnp.mean(x, axis=-1, keepdims=True)
            var = jnp.var(x, axis=-1, keepdims=True)
            return (x - mu) * jax.lax.rsqrt(var + EPS) * gamma + beta
        key = jax.random.key(seed)
        ks = jax.random.split(key, 12)
        sd = 0.02
        return {'hidden_state': jax.random.normal(ks[0], (B, L, H), jnp.float32), 'encoder_hidden_state': jax.random.normal(ks[1], (B, S, H), jnp.float32), 'encoder_attention_mask': jnp.zeros((B, 1, L, S), jnp.float32), 'Wq': jax.random.normal(ks[2], (H, H), jnp.float32) * sd, 'bq': jnp.zeros((H,), jnp.float32), 'Wk': jax.random.normal(ks[3], (H, KVH * HD), jnp.float32) * sd, 'bk': jnp.zeros((KVH * HD,), jnp.float32), 'Wv': jax.random.normal(ks[4], (H, KVH * HD), jnp.float32) * sd, 'bv': jnp.zeros((KVH * HD,), jnp.float32), 'Wo': jax.random.normal(ks[5], (H, H), jnp.float32) * sd, 'bo': jnp.zeros((H,), jnp.float32), 'gamma': jnp.ones((H,), jnp.float32), 'beta': jnp.zeros((H,), jnp.float32)}
    _L1_xattn_all = _L1_xattn_setup()
    _L1_xattn_in = {k: v for k, v in _L1_xattn_all.items() if k in ('Wq', 'bq', 'Wk', 'bk', 'Wv', 'bv', 'Wo', 'bo', 'gamma', 'beta')}
    del _L1_xattn_all

    def _L2_xattn_setup():
        import jax, jax.numpy as jnp
        import numpy as np
        B, P, K, H, NH = (4, 256, 32, 256, 16)
        DH = H // NH
        EPS = 1e-06

        def rmsnorm(x, w):
            var = jnp.mean(jnp.square(x), axis=-1, keepdims=True)
            return x * jax.lax.rsqrt(var + EPS) * w
        key = jax.random.key(seed)
        ks = jax.random.split(key, 12)
        s = 0.02
        return {'x': jax.random.normal(ks[0], (B, P, H), jnp.float32), 'latents': jax.random.normal(ks[1], (B, K, H), jnp.float32), 'attention_mask': jax.random.randint(ks[2], (B, P), 0, 2, jnp.int32), 'q_w': s * jax.random.normal(ks[3], (H, H), jnp.float32), 'q_b': jnp.zeros((H,), jnp.float32), 'kv_w': s * jax.random.normal(ks[4], (H, 2 * H), jnp.float32), 'kv_b': jnp.zeros((2 * H,), jnp.float32), 'out_w': s * jax.random.normal(ks[5], (H, H), jnp.float32), 'out_b': jnp.zeros((H,), jnp.float32), 'postnorm_w': jnp.ones((H,), jnp.float32), 'mlp_w1': s * jax.random.normal(ks[6], (H, 4 * H), jnp.float32), 'mlp_b1': jnp.zeros((4 * H,), jnp.float32), 'mlp_w2': s * jax.random.normal(ks[7], (4 * H, H), jnp.float32), 'mlp_b2': jnp.zeros((H,), jnp.float32)}
    _L2_xattn_all = _L2_xattn_setup()
    _L2_xattn_in = {k: v for k, v in _L2_xattn_all.items() if k in ('q_w', 'q_b', 'kv_w', 'kv_b', 'out_w', 'out_b', 'postnorm_w', 'mlp_w1', 'mlp_b1', 'mlp_w2', 'mlp_b2')}
    del _L2_xattn_all

    def _L3_xattn_setup():
        import jax, jax.numpy as jnp
        import numpy as np
        HIDDEN = 256
        HEADS = 16
        HEAD_DIM = HIDDEN // HEADS
        LN_EPS = 1e-05
        GATE_INIT = 0.5

        def _layer_norm(x, gamma, beta):
            mu = jnp.mean(x, axis=-1, keepdims=True)
            var = jnp.mean(jnp.square(x - mu), axis=-1, keepdims=True)
            return (x - mu) * jax.lax.rsqrt(var + LN_EPS) * gamma + beta
        key = jax.random.key(seed)
        ks = jax.random.split(key, 8)
        B, T_TEXT, T_AUDIO = (4, 256, 1500)
        s = 0.02
        return {'hidden_states': jax.random.normal(ks[0], (B, T_TEXT, HIDDEN), jnp.float32), 'audio_kv': jax.random.normal(ks[1], (B, T_AUDIO, HIDDEN), jnp.float32), 'audio_attention_mask': jnp.ones((B, T_AUDIO), dtype=bool), 'Wq': jax.random.normal(ks[2], (HIDDEN, HIDDEN), jnp.float32) * s, 'Wk': jax.random.normal(ks[3], (HIDDEN, HIDDEN), jnp.float32) * s, 'Wv': jax.random.normal(ks[4], (HIDDEN, HIDDEN), jnp.float32) * s, 'Wo': jax.random.normal(ks[5], (HIDDEN, HIDDEN), jnp.float32) * s, 'ln_gamma': jnp.ones((HIDDEN,), jnp.float32), 'ln_beta': jnp.zeros((HIDDEN,), jnp.float32), 'gate': jnp.array([GATE_INIT], jnp.float32)}
    _L3_xattn_all = _L3_xattn_setup()
    _L3_xattn_in = {k: v for k, v in _L3_xattn_all.items() if k in ('Wq', 'Wk', 'Wv', 'Wo', 'ln_gamma', 'ln_beta', 'gate')}
    del _L3_xattn_all
    return {'x': x, 'ctx_2048': ctx_2048, 'mask_BxS2_bf1': mask_BxS2_bf1, 'mask_Bx1xSxS2_ff0': mask_Bx1xSxS2_ff0, 'mask_BxS2_ik0': mask_BxS2_ik0, 'L0_xattn_ln1_w': _L0_xattn_in['ln1_w'], 'L0_xattn_ln1_b': _L0_xattn_in['ln1_b'], 'L0_xattn_q_w': _L0_xattn_in['q_w'], 'L0_xattn_q_b': _L0_xattn_in['q_b'], 'L0_xattn_k_w': _L0_xattn_in['k_w'], 'L0_xattn_k_b': _L0_xattn_in['k_b'], 'L0_xattn_v_w': _L0_xattn_in['v_w'], 'L0_xattn_v_b': _L0_xattn_in['v_b'], 'L0_xattn_cproj_w': _L0_xattn_in['cproj_w'], 'L0_xattn_cproj_b': _L0_xattn_in['cproj_b'], 'L0_xattn_ln2_w': _L0_xattn_in['ln2_w'], 'L0_xattn_ln2_b': _L0_xattn_in['ln2_b'], 'L0_xattn_fc_w': _L0_xattn_in['fc_w'], 'L0_xattn_fc_b': _L0_xattn_in['fc_b'], 'L0_xattn_proj_w': _L0_xattn_in['proj_w'], 'L0_xattn_proj_b': _L0_xattn_in['proj_b'], 'L1_xattn_Wq': _L1_xattn_in['Wq'], 'L1_xattn_bq': _L1_xattn_in['bq'], 'L1_xattn_Wk': _L1_xattn_in['Wk'], 'L1_xattn_bk': _L1_xattn_in['bk'], 'L1_xattn_Wv': _L1_xattn_in['Wv'], 'L1_xattn_bv': _L1_xattn_in['bv'], 'L1_xattn_Wo': _L1_xattn_in['Wo'], 'L1_xattn_bo': _L1_xattn_in['bo'], 'L1_xattn_gamma': _L1_xattn_in['gamma'], 'L1_xattn_beta': _L1_xattn_in['beta'], 'L2_xattn_q_w': _L2_xattn_in['q_w'], 'L2_xattn_q_b': _L2_xattn_in['q_b'], 'L2_xattn_kv_w': _L2_xattn_in['kv_w'], 'L2_xattn_kv_b': _L2_xattn_in['kv_b'], 'L2_xattn_out_w': _L2_xattn_in['out_w'], 'L2_xattn_out_b': _L2_xattn_in['out_b'], 'L2_xattn_postnorm_w': _L2_xattn_in['postnorm_w'], 'L2_xattn_mlp_w1': _L2_xattn_in['mlp_w1'], 'L2_xattn_mlp_b1': _L2_xattn_in['mlp_b1'], 'L2_xattn_mlp_w2': _L2_xattn_in['mlp_w2'], 'L2_xattn_mlp_b2': _L2_xattn_in['mlp_b2'], 'L3_xattn_Wq': _L3_xattn_in['Wq'], 'L3_xattn_Wk': _L3_xattn_in['Wk'], 'L3_xattn_Wv': _L3_xattn_in['Wv'], 'L3_xattn_Wo': _L3_xattn_in['Wo'], 'L3_xattn_ln_gamma': _L3_xattn_in['ln_gamma'], 'L3_xattn_ln_beta': _L3_xattn_in['ln_beta'], 'L3_xattn_gate': _L3_xattn_in['gate']}

def reference(x, ctx_2048, mask_BxS2_bf1, mask_Bx1xSxS2_ff0, mask_BxS2_ik0, L0_xattn_ln1_w, L0_xattn_ln1_b, L0_xattn_q_w, L0_xattn_q_b, L0_xattn_k_w, L0_xattn_k_b, L0_xattn_v_w, L0_xattn_v_b, L0_xattn_cproj_w, L0_xattn_cproj_b, L0_xattn_ln2_w, L0_xattn_ln2_b, L0_xattn_fc_w, L0_xattn_fc_b, L0_xattn_proj_w, L0_xattn_proj_b, L1_xattn_Wq, L1_xattn_bq, L1_xattn_Wk, L1_xattn_bk, L1_xattn_Wv, L1_xattn_bv, L1_xattn_Wo, L1_xattn_bo, L1_xattn_gamma, L1_xattn_beta, L2_xattn_q_w, L2_xattn_q_b, L2_xattn_kv_w, L2_xattn_kv_b, L2_xattn_out_w, L2_xattn_out_b, L2_xattn_postnorm_w, L2_xattn_mlp_w1, L2_xattn_mlp_b1, L2_xattn_mlp_w2, L2_xattn_mlp_b2, L3_xattn_Wq, L3_xattn_Wk, L3_xattn_Wv, L3_xattn_Wo, L3_xattn_ln_gamma, L3_xattn_ln_beta, L3_xattn_gate):
    import jax
    import jax.numpy as jnp

    def _L0_xattn_ref(hidden_states, encoder_hidden_states, encoder_attention_mask, ln1_w, ln1_b, q_w, q_b, k_w, k_b, v_w, v_b, cproj_w, cproj_b, ln2_w, ln2_b, fc_w, fc_b, proj_w, proj_b):
        import jax, jax.numpy as jnp
        import numpy as np
        D = 256
        H = 16
        HD = D // H
        INNER = 4 * D
        EPS = 1e-05

        def layer_norm(x, w, b):
            mu = jnp.mean(x, axis=-1, keepdims=True)
            var = jnp.mean(jnp.square(x - mu), axis=-1, keepdims=True)
            return (x - mu) * jax.lax.rsqrt(var + EPS) * w + b
        B, LQ, _ = hidden_states.shape
        LK = encoder_hidden_states.shape[1]
        residual = hidden_states
        x = layer_norm(hidden_states, ln1_w, ln1_b)
        q = (x @ q_w + q_b).reshape(B, LQ, H, HD).transpose(0, 2, 1, 3)
        k = (encoder_hidden_states @ k_w + k_b).reshape(B, LK, H, HD).transpose(0, 2, 1, 3)
        v = (encoder_hidden_states @ v_w + v_b).reshape(B, LK, H, HD).transpose(0, 2, 1, 3)
        scale = 1.0 / np.sqrt(HD).astype(np.float32)
        scores = jnp.einsum('bhqd,bhkd->bhqk', q, k) * scale
        mask = encoder_attention_mask[:, None, None, :]
        mask_value = jnp.finfo(scores.dtype).min
        scores = jnp.where(mask, scores, mask_value)
        attn = jax.nn.softmax(scores, axis=-1)
        out = jnp.einsum('bhqk,bhkd->bhqd', attn, v)
        out = out.transpose(0, 2, 1, 3).reshape(B, LQ, D)
        out = out @ cproj_w + cproj_b
        hidden = out + residual
        residual = hidden
        y = layer_norm(hidden, ln2_w, ln2_b)
        y = jax.nn.gelu(y @ fc_w + fc_b, approximate=True)
        y = y @ proj_w + proj_b
        return residual + y

    def _L1_xattn_ref(hidden_state, encoder_hidden_state, encoder_attention_mask, Wq, bq, Wk, bk, Wv, bv, Wo, bo, gamma, beta):
        import jax, jax.numpy as jnp
        import numpy as np
        H = 256
        NH = 32
        KVH = 8
        HD = H // NH
        GROUPS = NH // KVH
        EPS = 1e-06
        B, L, S = (4, 128, 128)

        def _gqa_forward(hidden_state, encoder_hidden_state, encoder_attention_mask, Wq, bq, Wk, bk, Wv, bv, Wo, bo, gamma, beta):
            b, l, _ = hidden_state.shape
            s = encoder_hidden_state.shape[1]
            q = hidden_state @ Wq + bq
            k = encoder_hidden_state @ Wk + bk
            v = encoder_hidden_state @ Wv + bv
            q = q.reshape(b, l, KVH, GROUPS, HD).transpose(0, 2, 3, 1, 4)
            k = k.reshape(b, s, KVH, HD).transpose(0, 2, 1, 3)
            v = v.reshape(b, s, KVH, HD).transpose(0, 2, 1, 3)
            scale = 1.0 / jnp.sqrt(jnp.asarray(HD, q.dtype))
            scores = jnp.einsum('bkgld,bksd->bkgls', q, k) * scale
            scores = scores + encoder_attention_mask[:, :, None, :, :]
            attn = jax.nn.softmax(scores, axis=-1)
            out = jnp.einsum('bkgls,bksd->bkgld', attn, v)
            out = out.transpose(0, 3, 1, 2, 4).reshape(b, l, H)
            out = out @ Wo + bo
            x = out + hidden_state
            mu = jnp.mean(x, axis=-1, keepdims=True)
            var = jnp.var(x, axis=-1, keepdims=True)
            return (x - mu) * jax.lax.rsqrt(var + EPS) * gamma + beta
        return _gqa_forward(hidden_state, encoder_hidden_state, encoder_attention_mask, Wq, bq, Wk, bk, Wv, bv, Wo, bo, gamma, beta)

    def _L2_xattn_ref(x, latents, attention_mask, q_w, q_b, kv_w, kv_b, out_w, out_b, postnorm_w, mlp_w1, mlp_b1, mlp_w2, mlp_b2):
        import jax, jax.numpy as jnp
        import numpy as np
        B, P, K, H, NH = (4, 256, 32, 256, 16)
        DH = H // NH
        EPS = 1e-06

        def rmsnorm(x, w):
            var = jnp.mean(jnp.square(x), axis=-1, keepdims=True)
            return x * jax.lax.rsqrt(var + EPS) * w
        b, p, _ = x.shape
        k_len = latents.shape[1]
        residual = latents
        h = jnp.concatenate([x, latents], axis=1)
        q = (latents @ q_w + q_b).reshape(b, k_len, NH, DH)
        kv = (h @ kv_w + kv_b).reshape(b, p + k_len, NH, DH, 2)
        kmat, v = (kv[..., 0], kv[..., 1])
        attn = jnp.einsum('bkhd,bnhd->bhkn', q, kmat) / DH
        full_mask = jnp.concatenate([attention_mask.astype(bool), jnp.ones((b, k_len), bool)], axis=-1)
        attn = jnp.where(full_mask[:, None, None, :], attn, -jnp.inf)
        attn = jax.nn.softmax(attn.astype(jnp.float32), axis=-1).astype(q.dtype)
        attn_out = jnp.einsum('bhkn,bnhd->bkhd', attn, v).reshape(b, k_len, H)
        attn_out = attn_out @ out_w + out_b + residual
        out = rmsnorm(attn_out, postnorm_w)
        out = jax.nn.gelu(out @ mlp_w1 + mlp_b1) @ mlp_w2 + mlp_b2
        return out + residual

    def _L3_xattn_ref(hidden_states, audio_kv, audio_attention_mask, Wq, Wk, Wv, Wo, ln_gamma, ln_beta, gate):
        import jax, jax.numpy as jnp
        import numpy as np
        HIDDEN = 256
        HEADS = 16
        HEAD_DIM = HIDDEN // HEADS
        LN_EPS = 1e-05
        GATE_INIT = 0.5

        def _layer_norm(x, gamma, beta):
            mu = jnp.mean(x, axis=-1, keepdims=True)
            var = jnp.mean(jnp.square(x - mu), axis=-1, keepdims=True)
            return (x - mu) * jax.lax.rsqrt(var + LN_EPS) * gamma + beta
        B, Tt, D = hidden_states.shape
        Ta = audio_kv.shape[1]
        scale = HEAD_DIM ** (-0.5)
        a = _layer_norm(audio_kv, ln_gamma, ln_beta)
        Q = (hidden_states @ Wq.T).reshape(B, Tt, HEADS, HEAD_DIM).transpose(0, 2, 1, 3)
        K = (a @ Wk.T).reshape(B, Ta, HEADS, HEAD_DIM).transpose(0, 2, 1, 3)
        V = (a @ Wv.T).reshape(B, Ta, HEADS, HEAD_DIM).transpose(0, 2, 1, 3)
        scores = jnp.einsum('bhtd,bhsd->bhts', Q, K) * scale
        mask = audio_attention_mask[:, None, None, :]
        scores = jnp.where(mask, scores, jnp.float32(-jnp.inf))
        attn = jax.nn.softmax(scores, axis=-1)
        out = jnp.einsum('bhts,bhsd->bhtd', attn, V)
        out = out.transpose(0, 2, 1, 3).reshape(B, Tt, D)
        out = out @ Wo.T
        return hidden_states + jnp.tanh(gate) * out
    x = _L0_xattn_ref(x, ctx_2048, mask_BxS2_bf1, L0_xattn_ln1_w, L0_xattn_ln1_b, L0_xattn_q_w, L0_xattn_q_b, L0_xattn_k_w, L0_xattn_k_b, L0_xattn_v_w, L0_xattn_v_b, L0_xattn_cproj_w, L0_xattn_cproj_b, L0_xattn_ln2_w, L0_xattn_ln2_b, L0_xattn_fc_w, L0_xattn_fc_b, L0_xattn_proj_w, L0_xattn_proj_b)
    x = _L1_xattn_ref(x, ctx_2048, mask_Bx1xSxS2_ff0, L1_xattn_Wq, L1_xattn_bq, L1_xattn_Wk, L1_xattn_bk, L1_xattn_Wv, L1_xattn_bv, L1_xattn_Wo, L1_xattn_bo, L1_xattn_gamma, L1_xattn_beta)
    x = _L2_xattn_ref(ctx_2048, x, mask_BxS2_ik0, L2_xattn_q_w, L2_xattn_q_b, L2_xattn_kv_w, L2_xattn_kv_b, L2_xattn_out_w, L2_xattn_out_b, L2_xattn_postnorm_w, L2_xattn_mlp_w1, L2_xattn_mlp_b1, L2_xattn_mlp_w2, L2_xattn_mlp_b2)
    x = _L3_xattn_ref(x, ctx_2048, mask_BxS2_bf1, L3_xattn_Wq, L3_xattn_Wk, L3_xattn_Wv, L3_xattn_Wo, L3_xattn_ln_gamma, L3_xattn_ln_beta, L3_xattn_gate)
    return x

_drawn_inputs = setup_inputs


def setup_inputs(seed=0):
    import zlib

    import numpy as np

    out = dict(_drawn_inputs(seed))
    spreads = {'L0_xattn_ln1_w': (1.0, 0.6),
     'L0_xattn_ln1_b': (0.0, 0.8),
     'L0_xattn_q_b': (0.0, 0.8),
     'L0_xattn_k_b': (0.0, 0.8),
     'L0_xattn_v_b': (0.0, 0.1),
     'L0_xattn_cproj_b': (0.0, 0.1),
     'L0_xattn_ln2_w': (1.0, 0.6),
     'L0_xattn_ln2_b': (0.0, 0.761),
     'L0_xattn_fc_b': (0.0, 0.1),
     'L0_xattn_proj_b': (0.0, 0.1),
     'L1_xattn_bq': (0.0, 0.8),
     'L1_xattn_bk': (0.0, 0.8),
     'L1_xattn_bv': (0.0, 0.1),
     'L1_xattn_bo': (0.0, 0.1),
     'L1_xattn_gamma': (1.0, 0.2),
     'L1_xattn_beta': (0.0, 0.1),
     'L2_xattn_q_b': (0.0, 0.8),
     'L2_xattn_kv_b': (0.0, 0.8),
     'L2_xattn_out_b': (0.0, 0.693),
     'L2_xattn_postnorm_w': (1.0, 0.6),
     'L2_xattn_mlp_b1': (0.0, 0.1),
     'L2_xattn_mlp_b2': (0.0, 0.1),
     'L3_xattn_ln_gamma': (1.0, 0.6),
     'L3_xattn_ln_beta': (0.0, 0.8)}
    factors = {'L0_xattn_q_w': 8.0,
     'L0_xattn_k_w': 8.0,
     'L1_xattn_Wq': 8.0,
     'L1_xattn_Wk': 8.0,
     'L2_xattn_q_w': 8.0,
     'L2_xattn_kv_w': 8.0,
     'L2_xattn_out_w': 8.0,
     'L3_xattn_Wq': 8.0,
     'L3_xattn_Wk': 8.0}
    for name, (base, spread) in spreads.items():
        noise = np.random.default_rng([zlib.crc32(name.encode()), seed]).standard_normal(out[name].shape)
        drawn = base * np.exp(spread * noise) if base else spread * noise
        out[name] = jnp.asarray(drawn.astype(out[name].dtype))
    for name, factor in factors.items():
        out[name] = (out[name] * factor).astype(out[name].dtype)
    return out
```

```python
from contextlib import ExitStack

import concourse.bass as bass
from concourse import mybir

B = 16
T = 128
D = 256
DT = D // 128
INNER = 4 * D
FT = INNER // 128
G = 2
S = 2
GT = G * T
PASSES = B // (G * S)
BIG = 3.0e38
CREDIT = 256
PR = 96

Q_SLOTS = ((0, 0, 3, 1), (0, 3, 2, 1), (0, 5, 1, 1))
K_SLOTS = ((0, 0, 1, 3), (1, 3, 1, 2), (2, 5, 1, 1))


class Layer:
    def __init__(self, name, heads, head, kv_heads, key_tiles, unit, scale, eps, ln_x=False, ln_c=False,
                 load_ct=False, store_ct=False, mlp=None, float_mask=False, slot=0):
        self.name, self.heads, self.head, self.kv_heads = name, heads, head, kv_heads
        self.key_tiles, self.unit, self.scale, self.eps = key_tiles, unit, scale, eps
        self.ln_x, self.ln_c, self.load_ct, self.store_ct = ln_x, ln_c, load_ct, store_ct
        self.mlp, self.float_mask, self.slot = mlp, float_mask, slot
        self.group = heads // kv_heads
        self.kcols = kv_heads * head
        self.units = [(s, b, h) for s in range(S) for b in range(G) for h in range(0, heads, unit)]


LAYERS = [
    Layer("L0", 16, 16, 16, 1, 8, 0.25, 1e-5, ln_x=True, store_ct=True, mlp="L0"),
    Layer("L1", 32, 8, 8, 1, 8, float(8.0 ** -0.5), 1e-6, load_ct=True, float_mask=True, slot=1),
    Layer("L2", 16, 16, 16, 2, 4, 1.0 / 16, 1e-6, load_ct=True, mlp="L2"),
    Layer("L3", 16, 16, 16, 1, 8, 0.25, 1e-5, ln_c=True, slot=1),
]


class Signal:

    def __init__(self, sem, step=1):
        self.sem, self.step, self.total, self.keys, self.risen = sem, step, CREDIT, [], set()

    def plan(self, keys):
        self.keys, self.risen = list(keys), set()
        assert self.step * len(self.keys) < CREDIT, (self.sem, len(self.keys))

    def rise(self, key):
        assert key in self.keys and key not in self.risen, (self.sem, key)
        self.risen.add(key)
        return self.sem, self.step

    def at(self, it, key):
        return self.total + self.step * (it * len(self.keys) + self.keys.index(key) + 1)

    def prev(self, it, key):
        return self.total + self.step * ((it - 1) * len(self.keys) + self.keys.index(key) + 1)

    def back(self, it, key, n):
        return self.total + self.step * (it * len(self.keys) + self.keys.index(key) + 1 - n)

    def finish(self, passes):
        assert len(self.risen) == len(self.keys), (self.sem, set(self.keys) - self.risen)
        self.total += self.step * len(self.keys) * passes
        self.keys, self.risen = [], set()


class Steps:

    def __init__(self, sem):
        self.sem, self.total, self.per, self.n = sem, CREDIT, 0, 0

    def plan(self, layer):
        self.layer, self.per, self.n = layer, STEPS[layer], 0

    def tick(self):
        self.n += 1
        return self.sem, 1

    def now(self, it):
        return self.total + it * self.per + self.n

    def finish(self, passes):
        assert passes == 1 or self.n == self.per, f"STEPS {self.layer} {self.n}"
        self.total += self.n * passes
        self.n = 0


STEPS = {"L0": 46, "L1": 54, "L2": 62, "L3": 36}


def xattn_program(nc, ins, out):
    F32, F32R, BF16 = mybir.dt.float32, mybir.dt.float32r, mybir.dt.bfloat16
    ALU, ACT, AX = mybir.AluOpType, mybir.ActivationFunctionType, mybir.AxisListType

    ctx = ExitStack()
    with ctx:
        def sb(name, shape, dt=F32):
            return ctx.enter_context(nc.sbuf_tensor(name, shape, dt))

        def dram(name, shape, dt=F32):
            return nc.dram_tensor(name, shape, dt, kind="Internal").ap()

        signals = []

        def signal(name, step=1):
            signals.append(Signal(ctx.enter_context(nc.semaphore(name)), step))
            return signals[-1]

        W_COLS = (6144, 2048)
        w_hi = [sb(f"w_hi{i}", [128, W_COLS[i]], F32R) for i in range(2)]
        w_lo = [sb(f"w_lo{i}", [128, W_COLS[i]], F32R) for i in range(2)]
        ARENA = 48 * GT
        arena = [sb(f"stacks{s}", [128, ARENA], BF16) for s in range(S)]
        values = [sb(f"values{s}", [128, G * 2 * 16 * 32]) for s in range(S)]
        probs = sb("probs", [128, 4, 512])
        x_tok = [sb(f"x_tok{s}", [128, G, D]) for s in range(S)]
        c_tok = [sb(f"c_tok{s}", [128, G, D]) for s in range(S)]
        norm = [sb(f"norm{s}", [128, G, D]) for s in range(S)]
        heads_out = [sb(f"heads_out{s}", [128, G, D]) for s in range(S)]
        t32 = [sb(f"t32_{i}", [128, DT, GT]) for i in range(2)]
        x_hi = [sb(f"x_hi{s}", [128, DT, GT], F32R) for s in range(S)]
        x_lo = [sb(f"x_lo{s}", [128, DT, GT], F32R) for s in range(S)]
        c_hi = [sb(f"c_hi{s}", [128, DT, GT], F32R) for s in range(S)]
        c_lo = [sb(f"c_lo{s}", [128, DT, GT], F32R) for s in range(S)]
        qk32 = [sb(f"qk32_{i}", [128, DT, GT]) for i in range(2)]
        parts = [sb(f"parts{i}", [128, 3, DT, GT], BF16) for i in range(2)]
        hid32 = [sb(f"hid32_{i}", [128, 2, GT]) for i in range(2)]
        hid_hi = [sb(f"hid_hi{i}", [128, 2, GT], F32R) for i in range(2)]
        hid_lo = [sb(f"hid_lo{i}", [128, 2, GT], F32R) for i in range(2)]
        o_t = sb("o_t", [128, 256])
        m_neg = sb("m_neg", [128, 2, 8])
        m_parts = sb("m_parts", [128, 2, 128], BF16)
        m_rows = sb("m_rows", [128, 2, 128], BF16)
        r_inv = sb("r_inv", [128, 2, 8])
        stats = sb("stats", [128, S, G, 6])
        moments = sb("moments", [128, S, G, 2])
        spread = sb("spread", [128, S, G])
        rstd = sb("rstd", [128, S, G])
        minus_half = sb("minus_half", [128, G])
        spare = sb("spare", [128, 1])
        ident = sb("ident", [128, 128])
        ident_r = sb("ident_r", [128, 128], F32R)
        ident_b = sb("ident_b", [128, 128], BF16)
        select = sb("select", [128, 8, 128], BF16)
        rows = sb("rows", [128, 5, D])
        V_BIAS, O_BIAS, M_BIAS, GAMMA, BETA = range(5)
        cols = sb("cols", [128, 12 + FT])
        Q_COL, K_COL, W1_COL, B1_COL, W2_COL, B2_COL, F_COL = 0, 2, 4, 6, 8, 10, 12
        mask_f = sb("mask_f", [B, T])
        mask_u8 = sb("mask_u8", [B, T], mybir.dt.uint8)
        mask_i32 = sb("mask_i32", [B, T], mybir.dt.int32)
        mask_b = sb("mask_b", [B, 2, T], BF16)
        key_ok = sb("key_ok", [B, 3])
        gate = sb("gate", [128, 2 + B])

        ps_a = [ctx.enter_context(nc.psum_tensor(f"ps_a{i}", [128, 1024], F32)) for i in range(2)]
        ps_b = [ctx.enter_context(nc.psum_tensor(f"ps_b{i}", [128, 512], F32)) for i in range(2)]
        ps_d = [ctx.enter_context(nc.psum_tensor(f"ps_d{i}", [128, 512], F32)) for i in range(2)]

        x_dram = [ins["x"]] + [dram(f"x_after{i}", [B, T, D]) for i in range(3)] + [out]
        ct_dram = dram("ct", [PASSES, S, 2, 128, DT * GT])
        bias_dram = dram("key_bias", [2, B * T], BF16)
        ok_dram = dram("key_ok_rows", [B])
        q_dram = [dram(f"q_parts{s}", [3 * D * GT], BF16) for s in range(S)]
        k_dram = [[dram(f"k_parts{s}_{k}", [3 * D * GT], BF16) for k in range(2)] for s in range(S)]

        eye_ready = signal("eye_ready")
        const_ready = signal("const_ready")
        tanh_ready = signal("tanh_ready")
        const_loaded = signal("const_loaded", 16)
        bias_stored = signal("bias_stored", 16)
        factor_loaded = signal("factor_loaded", 16)
        raw_loaded = [signal(f"raw_loaded{i}", 16) for i in range(4)]
        raw_split = signal("raw_split")
        raw_turned = signal("raw_turned")
        vectors_loaded = signal("vectors_loaded", 16)
        vectors_ready = signal("vectors_ready")
        stacks_clear = signal("stacks_clear")
        x_loaded = [signal(f"x_loaded{s}", 16) for s in range(S)]
        c_loaded = [signal(f"c_loaded{s}", 16) for s in range(S)]
        ct_stored = [signal(f"ct_stored{s}", 16) for s in range(S)]
        written = {("Q", s): signal(f"q_written{s}", 16) for s in range(S)}
        written.update({("K", s, k): signal(f"k_written{s}_{k}", 16) for s in range(S) for k in range(2)})
        q_stacked = [signal(f"q_stacked{s}", 16) for s in range(S)]
        k_stacked = [signal(f"k_stacked{s}", 16) for s in range(S)]
        y_stored = [signal(f"y_stored{s}", 16) for s in range(S)]
        spread_ready = signal("spread_ready")
        rstd_ready = signal("rstd_ready")
        norm_ready = signal("norm_ready")
        d_full = signal("d_full")
        d_out = [signal(f"d_out{i}") for i in range(2)]
        hi_ready = signal("hi_ready")
        lo_ready = signal("lo_ready")
        parts_ready = signal("parts_ready")
        mask_hi_ready = signal("mask_hi_ready")
        mask_lo_ready = signal("mask_lo_ready")
        a_full = signal("a_full")
        a_out = signal("a_out")
        m_ready = signal("m_ready")
        b_full = signal("b_full")
        b_out = signal("b_out")
        hid_hi_ready = signal("hid_hi_ready")
        hid_lo_ready = signal("hid_lo_ready")
        hid_used = signal("hid_used")
        y_ready = signal("y_ready")
        scaled = signal("scaled")
        step = Steps(ctx.enter_context(nc.semaphore("vector_step")))

        def finish(passes):
            for g in signals:
                if g.keys:
                    g.finish(passes)
            step.finish(passes)

        def f32(ap):
            return ap.bitcast(F32)

        def repeat(ap, n):
            return ap.unsqueeze(1).broadcast_to([ap.shape[0], n, ap.shape[1]])

        with nc.Block() as block:
            @block.sync
            def _(sp):
                for g in signals + [step]:
                    sp.sem_inc(g.sem, CREDIT)

        eye_ready.plan(["zero", "half", "eye"])
        const_ready.plan(["eye_b", "eye_r", "select", "no_max", "mask_f", "count", "bias0", "bias1", "inverse",
                          "ok", "factors"])
        tanh_ready.plan(["gate"])
        const_loaded.plan(["u8", "i32", "gate"])
        bias_stored.plan(["bias", "ok"])
        factor_loaded.plan(["ok"])
        with nc.Block() as block:
            @block.sync
            def _(sp):
                sp.dma_start(mask_u8[:], ins["mask_BxS2_bf1"]).then_inc(*const_loaded.rise("u8"))
                sp.dma_start(mask_i32[:], ins["mask_BxS2_ik0"]).then_inc(*const_loaded.rise("i32"))
                sp.dma_start(gate[:, 0:1], ins["L3_xattn_gate"].partition_broadcast(128)).then_inc(
                    *const_loaded.rise("gate"))
                sp.wait_ge(const_ready.sem, const_ready.at(0, "ok"))
                sp.dma_start(bias_dram.rearrange("m (b t) -> b m t", b=B), mask_b[:]).then_inc(
                    *bias_stored.rise("bias"))
                sp.dma_start(ok_dram.unsqueeze(1), key_ok[:, 0:1]).then_inc(*bias_stored.rise("ok"))
                sp.wait_ge(bias_stored.sem, bias_stored.at(0, "ok"))
                sp.dma_start(gate[:, 2:2 + B], ok_dram.partition_broadcast(128)).then_inc(
                    *factor_loaded.rise("ok"))

            @block.gpsimd
            def _(pool):
                nc.gpsimd.memset(ident[:], 0.0).then_inc(*eye_ready.rise("zero"))
                nc.gpsimd.memset(minus_half[:], -0.5).then_inc(*eye_ready.rise("half"))
                pool.wait_ge(eye_ready.sem, eye_ready.at(0, "half"))
                nc.gpsimd.affine_select(out=ident[:], in_=ident[:], compare_op=ALU.not_equal, fill=1.0, base=0,
                                        pattern=[[-1, 128]], channel_multiplier=1).then_inc(
                    *eye_ready.rise("eye"))

            @block.vector
            def _(dve):
                dve.wait_ge(eye_ready.sem, eye_ready.at(0, "eye"))
                nc.vector.tensor_copy(ident_b[:], ident[:]).then_inc(*const_ready.rise("eye_b"))
                nc.vector.tensor_copy(ident_r[:], ident[:]).then_inc(*const_ready.rise("eye_r"))
                nc.vector.tensor_tensor(
                    out=select[:], in0=ident[:, 0:8].unsqueeze(2).broadcast_to([128, 8, 128]),
                    in1=ident[:, 8:16].unsqueeze(2).broadcast_to([128, 8, 128]), op=ALU.add).then_inc(
                    *const_ready.rise("select"))
                nc.vector.memset(m_parts[:], 0.0).then_inc(*const_ready.rise("no_max"))
                dve.wait_ge(const_loaded.sem, const_loaded.at(0, "gate"))
                nc.vector.tensor_copy(mask_f[:], mask_u8[:]).then_inc(*const_ready.rise("mask_f"))
                dve.wait_ge(const_ready.sem, const_ready.at(0, "mask_f"))
                nc.vector.tensor_reduce(out=key_ok[:, 1:2], in_=mask_f[:], axis=AX.X, op=ALU.add).then_inc(
                    *const_ready.rise("count"))
                nc.vector.tensor_scalar(mask_b[:, 0, :], mask_f[:], 0.0, -BIG, ALU.is_equal,
                                        ALU.mult).then_inc(*const_ready.rise("bias0"))
                nc.vector.tensor_scalar(mask_b[:, 1, :], mask_i32[:], 0.0, -BIG, ALU.is_equal,
                                        ALU.mult).then_inc(*const_ready.rise("bias1"))
                dve.wait_ge(const_ready.sem, const_ready.at(0, "bias1"))
                nc.vector.reciprocal(key_ok[:, 2:3], key_ok[:, 1:2]).then_inc(*const_ready.rise("inverse"))
                dve.wait_ge(const_ready.sem, const_ready.at(0, "inverse"))
                nc.vector.tensor_scalar(key_ok[:, 0:1], key_ok[:, 2:3], 0.0, 1.0, ALU.mult,
                                        ALU.add).then_inc(*const_ready.rise("ok"))
                dve.wait_ge(factor_loaded.sem, factor_loaded.at(0, "ok"))
                dve.wait_ge(tanh_ready.sem, tanh_ready.at(0, "gate"))
                nc.vector.tensor_scalar(gate[:, 2:2 + B], gate[:, 2:2 + B], gate[:, 1:2], None,
                                        ALU.mult).then_inc(*const_ready.rise("factors"))

            @block.scalar
            def _(act):
                act.wait_ge(const_loaded.sem, const_loaded.at(0, "gate"))
                nc.scalar.activation(gate[:, 1:2], gate[:, 0:1], ACT.Tanh).then_inc(*tanh_ready.rise("gate"))
        finish(1)

        for index, L in enumerate(LAYERS):
            name = L.name + "_xattn_"
            H, HD, KV, KT, U = L.heads, L.head, L.kv_heads, L.key_tiles, L.unit
            kc = KV * HD
            k_rows, k_tiles = min(kc, 128), -(-kc // 128)
            whi, wlo = w_hi[L.slot], w_lo[L.slot]

            place, first = {}, 0
            for key, tiles, width in [("q", DT, D), ("k", DT, kc), ("v", DT, kc), ("o", DT, D)] + (
                    [("f", DT, INNER), ("m", FT, D)] if L.mlp else []):
                place[key] = (first, tiles, width)
                first += tiles * width

            def weight(t, key):
                start, tiles, width = place[key]
                return t[:, start:start + tiles * width].rearrange("p (k n) -> p k n", k=tiles)

            def both(key):
                return weight(whi, key), weight(wlo, key)

            matrices = {
                "L0": dict(q="q_w", k="k_w", v="v_w", o="cproj_w", f="fc_w", m="proj_w"),
                "L1": dict(q="Wq", k="Wk", v="Wv", o="Wo"),
                "L2": dict(q="q_w", kv="kv_w", o="out_w", f="mlp_w1", m="mlp_w2"),
                "L3": dict(q="Wq", k="Wk", v="Wv", o="Wo"),
            }[L.name]
            vectors = {
                "L0": dict(q="q_b", k="k_b", v="v_b", o="cproj_b", w1="ln1_w", b1="ln1_b", w2="ln2_w",
                           b2="ln2_b", f="fc_b", m="proj_b"),
                "L1": dict(q="bq", k="bk", v="bv", o="bo", gamma="gamma", beta="beta"),
                "L2": dict(q="q_b", kv="kv_b", o="out_b", w2="postnorm_w", f="mlp_b1", m="mlp_b2"),
                "L3": dict(w1="ln_gamma", b1="ln_beta"),
            }[L.name]

            chunks = []
            for key, w in matrices.items():
                tall, broad = ins[name + w].shape
                for tile in range(tall // 128):
                    for c0 in range(0, broad, 512):
                        chunks.append((key, tile, c0, min(512, broad - c0)))

            def by_dimension(ap, heads):
                return ap.rearrange("p (d h) -> p h d", h=heads)

            def by_head(ap):
                return ap.rearrange("p (h d) -> p h d", d=HD)

            def homes(t, raw, key, tile, c0, width):
                if key == "kv":
                    two = raw.rearrange("p (h d e) -> p h d e", d=HD, e=2)
                    return [(two[:, :, :, 0], by_dimension(weight(t, "k")[:, tile, :], KV)),
                            (two[:, :, :, 1], by_head(weight(t, "v")[:, tile, :]))]
                if key in ("q", "k"):
                    return [(by_head(raw), by_dimension(weight(t, key)[:, tile, :], H if key == "q" else KV))]
                return [(raw, weight(t, key)[:, tile, c0:c0 + width])]

            def turned_homes(t, bank, key, tile):
                found = []
                for into in range(DT):
                    raw = bank[:, 128 * into:128 * into + 128]
                    if key in ("q", "k"):
                        n_heads = 128 // HD
                        home = by_dimension(weight(t, key)[:, into, :], H)
                        found.append((by_head(raw), home[:, n_heads * tile:n_heads * (tile + 1), :]))
                    else:
                        found.append((raw, weight(t, key)[:, into, 128 * tile:128 * tile + 128]))
                return found

            loads = []
            if "q" in vectors:
                q_bias = ins[name + vectors["q"]].rearrange("(h d) -> d h", d=HD)
                per = 128 // H
                for t in range(DT):
                    loads.append((cols[:, Q_COL + t:Q_COL + t + 1], q_bias[per * t:per * t + per, :].unsqueeze(2)))
                if "kv" in vectors:
                    k_bias = ins[name + "kv_b"].rearrange("(h d e) -> e d h", d=HD, e=2)[0]
                    loads.append((t32[0][:].rearrange("p a b -> p (a b)"), ins[name + "kv_b"].partition_broadcast(128)))
                else:
                    k_bias = ins[name + vectors["k"]].rearrange("(h d) -> d h", d=HD)
                    loads.append((rows[:, V_BIAS, 0:kc], ins[name + vectors["v"]].partition_broadcast(128)))
                per = k_rows // KV
                for t in range(k_tiles):
                    loads.append((cols[0:k_rows, K_COL + t:K_COL + t + 1],
                                  k_bias[per * t:per * t + per, :].unsqueeze(2)))
            for key, row in (("o", O_BIAS), ("m", M_BIAS), ("gamma", GAMMA), ("beta", BETA)):
                if key in vectors:
                    loads.append((rows[:, row, :], ins[name + vectors[key]].partition_broadcast(128)))
            for key, col in (("w1", W1_COL), ("b1", B1_COL), ("w2", W2_COL), ("b2", B2_COL), ("f", F_COL)):
                if key in vectors:
                    v = ins[name + vectors[key]].rearrange("(c p) -> p c", p=128)
                    loads.append((cols[:, col:col + v.shape[1]], v))

            q_stack = [arena[s][:, 0:H * GT].rearrange("p (h t) -> p h t", t=GT) for s in range(S)]
            k_stack = [arena[s][:, H * GT:(H + KT * KV) * GT].rearrange("p (k h t) -> p k h t", k=KT, t=GT)
                       for s in range(S)]
            value = [values[s][:, 0:G * KT * KV * 32].rearrange("p (g h e) -> p g h e", g=G * KT, e=32)
                     for s in range(S)]

            for i in range(4):
                raw_loaded[i].plan(range((len(chunks) - i + 3) // 4))
            raw_split.plan(range(len(chunks)))
            if L.name == "L3":
                raw_turned.plan(range(len(chunks)))
            vectors_loaded.plan(range(len(loads)))
            if "q" in vectors:
                vectors_ready.plan(["q"] + (["v"] if "kv" in vectors else []))
            stacks_clear.plan([(s, k) for s in range(S) for k in (
                ("all", "values") if L.float_mask else ("all", "values", "one")) + ("sum",)])
            with nc.Block() as block:
                @block.sync
                def _(sp):
                    for i, (key, tile, c0, width) in enumerate(chunks):
                        if i >= 4:
                            sp.wait_ge(raw_split.sem, raw_split.at(0, i - 4))
                        sp.dma_start(probs[:, i % 4, 0:width],
                                     ins[name + matrices[key]][128 * tile:128 * tile + 128, c0:c0 + width]).then_inc(
                            *raw_loaded[i % 4].rise(i // 4))

                @block.scalar
                def _(act):
                    for i, (to, of) in enumerate(loads):
                        with nc.allow_non_contiguous_dma(reason="a few hundred elements, once in a layer"):
                            act.dma_start(to, of).then_inc(*vectors_loaded.rise(i))
                    act.wait_ge(vectors_loaded.sem, vectors_loaded.at(0, len(loads) - 1))

                @block.gpsimd
                def _(pool):
                    for s in range(S):
                        nc.gpsimd.memset(f32(arena[s][:]), 0.0).then_inc(*stacks_clear.rise((s, "all")))
                        nc.gpsimd.memset(values[s][:], 0.0).then_inc(*stacks_clear.rise((s, "values")))
                        pool.wait_ge(stacks_clear.sem, stacks_clear.at(0, (s, "values")))
                        if not L.float_mask:
                            nc.gpsimd.memset(q_stack[s][PR:PR + 1, :, :], 1.0).then_inc(
                                *stacks_clear.rise((s, "one")))
                            pool.wait_ge(stacks_clear.sem, stacks_clear.at(0, (s, "one")))
                        nc.gpsimd.memset(value[s][:, :, :, HD:HD + 1], 1.0).then_inc(
                            *stacks_clear.rise((s, "sum")))

                @block.tensor
                def _(pe):
                    if L.name == "L3":
                        for i, (key, tile, c0, width) in enumerate(chunks):
                            pe.wait_ge(raw_loaded[i % 4].sem, raw_loaded[i % 4].at(0, i // 4))
                            if i >= 2:
                                pe.wait_ge(raw_split.sem, raw_split.at(0, i - 2))
                            for into in range(DT):
                                last = nc.tensor.transpose(ps_d[i % 2][:, 128 * into:128 * into + 128],
                                                           probs[:, i % 4, 128 * into:128 * into + 128], ident[:])
                            last.then_inc(*raw_turned.rise(i))

                @block.vector
                def _(dve):
                    for i, (key, tile, c0, width) in enumerate(chunks):
                        if L.name == "L3":
                            dve.wait_ge(raw_turned.sem, raw_turned.at(0, i))
                            hi_homes = turned_homes(whi, ps_d[i % 2], key, tile)
                            lo_homes = turned_homes(wlo, ps_d[i % 2], key, tile)
                        else:
                            dve.wait_ge(raw_loaded[i % 4].sem, raw_loaded[i % 4].at(0, i // 4))
                            raw = probs[:, i % 4, 0:width]
                            hi_homes = homes(whi, raw, key, tile, c0, width)
                            lo_homes = homes(wlo, raw, key, tile, c0, width)
                        for of, to in hi_homes:
                            nc.vector.tensor_copy(to, of).then_inc(*step.tick())
                        dve.wait_ge(step.sem, step.now(0))
                        for (of, hi), (_, lo) in zip(hi_homes[:-1], lo_homes[:-1]):
                            nc.vector.tensor_tensor(out=lo, in0=of, in1=f32(hi), op=ALU.subtract).then_inc(
                                *step.tick())
                        of, lo = lo_homes[-1]
                        nc.vector.tensor_tensor(out=lo, in0=of, in1=f32(hi_homes[-1][1]), op=ALU.subtract).then_inc(
                            *raw_split.rise(i))
                    if "q" in vectors:
                        dve.wait_ge(vectors_loaded.sem, vectors_loaded.at(0, len(loads) - 1))
                        nc.vector.tensor_scalar(cols[:, Q_COL:Q_COL + DT], cols[:, Q_COL:Q_COL + DT], L.scale, None,
                                                ALU.mult).then_inc(*vectors_ready.rise("q"))
                        if "kv" in vectors:
                            nc.vector.tensor_copy(
                                rows[:, V_BIAS, :],
                                t32[0][:].rearrange("p a b -> p (a b)").rearrange("p (n e) -> p n e", e=2)[:, :, 1]
                            ).then_inc(*vectors_ready.rise("v"))
            finish(1)

            N = len(L.units)
            last_unit = [N // 2 - 1, N - 1]
            chunks_f = range(FT // 2)
            uses = []
            for s in range(S):
                uses.append(("TX", s))
                if not L.load_ct:
                    uses.append(("TC", s))
            for s in range(S):
                uses.append(("Q", s))
                uses += [("K", s, k) for k in range(KT)]
            uses += [("V", s, k) for s in range(S) for k in range(KT)]
            for n in range(N + 1):
                uses += [("MT", n)] if n < N else []
                uses += [("PV", n - 1), ("OT", n - 1)] if n else []
            uses += [("TO", s) for s in range(S)] + [("O", s) for s in range(S)]
            if L.mlp:
                uses += [("TL", s) for s in range(S)] + [("F", s, c) for s in range(S) for c in chunks_f]
            assert len(uses) % 2 == 0
            bank_of = {key: i % 2 for i, key in enumerate(uses)}
            turned = [u for u in uses if u[0] in ("TX", "TC", "TO", "TL")]
            projected = [u for u in uses if u[0] in ("Q", "K")]
            assert len(turned) % 2 == 0 and len(projected) % 2 == 0
            halves = [(n, f) for n in range(N) for f in range(2)]
            k_loads = [(k, i) for k in range(KT) for i in range(3)] + ([] if L.float_mask else ["bias"])
            normed = [("in", s) for s in range(S)] if L.ln_x or L.ln_c else []
            normed += [("mid", s) for s in range(S)] if L.name != "L3" else []

            d_full.plan(uses)
            for i in range(2):
                d_out[i].plan([u for u in uses if bank_of[u] == i])
            hi_ready.plan(turned)
            lo_ready.plan(turned)
            parts_ready.plan(projected)
            for key in projected:
                written[key].plan(["parts"])
            a_full.plan(range(N))
            a_out.plan(list(range(N)) + ([("M", s) for s in range(S)] if L.mlp else []))
            m_ready.plan(range(N))
            b_full.plan(halves)
            b_out.plan(halves)
            spread_ready.plan(normed)
            rstd_ready.plan(normed)
            norm_ready.plan(normed)
            if L.name != "L3":
                y_ready.plan(range(S))
            if L.mlp:
                for g in (hid_hi_ready, hid_lo_ready, hid_used):
                    g.plan([(s, c) for s in range(S) for c in chunks_f])
            if L.float_mask:
                mask_hi_ready.plan(range(S))
                mask_lo_ready.plan(range(S))
                scaled.plan(range(S))
            for s in range(S):
                x_loaded[s].plan(["x"])
                c_loaded[s].plan(["hi", "lo", "mask"] if L.float_mask else ["hi", "lo"] if L.load_ct else ["c"])
                if L.store_ct:
                    ct_stored[s].plan(["hi", "lo"])
                q_stacked[s].plan(range(3))
                k_stacked[s].plan(k_loads)
                y_stored[s].plan(["y"])
            step.plan(L.name)

            def bank(key):
                return ps_d[bank_of[key]]

            def out_of(key):
                return d_out[bank_of[key]]

            src, dst = x_dram[index], x_dram[index + 1]
            y_tile = norm if L.float_mask else heads_out

            def tok_rows(dram_ap, it, s):
                return dram_ap[bass.ds(it * (G * S) + s * G, G), :, :].rearrange("b t d -> t b d")

            with nc.Block() as block:
                @block.sync
                def _(sp):
                    with sp.Fori(0, PASSES) as it:
                        for s in range(S):
                            if L.name == "L2":
                                sp.wait_ge(a_out.sem, a_out.prev(it, ("M", s)))
                            else:
                                sp.wait_ge(out_of(("O", s)).sem, out_of(("O", s)).prev(it, ("O", s)))
                            sp.dma_start(x_tok[s][:], tok_rows(src, it, s)).then_inc(*x_loaded[s].rise("x"))
                            if L.load_ct:
                                sp.wait_ge(d_full.sem, d_full.prev(it, ("V", s, 0)))
                                sp.dma_start(f32(c_hi[s][:]).rearrange("p k t -> p (k t)"),
                                             ct_dram[bass.ds(it, 1), s, 0, :, :].rearrange("i p n -> (i p) n")).then_inc(
                                    *c_loaded[s].rise("hi"))
                                sp.dma_start(f32(c_lo[s][:]).rearrange("p k t -> p (k t)"),
                                             ct_dram[bass.ds(it, 1), s, 1, :, :].rearrange("i p n -> (i p) n")).then_inc(
                                    *c_loaded[s].rise("lo"))
                                if L.float_mask:
                                    sp.wait_ge(mask_lo_ready.sem, mask_lo_ready.prev(it, s))
                                    sp.dma_start(
                                        c_tok[s][:, :, 0:T],
                                        ins["mask_Bx1xSxS2_ff0"].rearrange("b o q k -> b (o q) k")[
                                            bass.ds(it * (G * S) + s * G, G), :, :].rearrange("b q k -> q b k")
                                    ).then_inc(*c_loaded[s].rise("mask"))
                            else:
                                if L.ln_c:
                                    sp.wait_ge(norm_ready.sem, norm_ready.prev(it, ("in", s)))
                                else:
                                    sp.wait_ge(d_full.sem, d_full.prev(it, ("TC", s)))
                                sp.dma_start(c_tok[s][:], tok_rows(ins["ctx_2048"], it, s)).then_inc(
                                    *c_loaded[s].rise("c"))
                        for s in range(S):
                            sp.wait_ge(parts_ready.sem, parts_ready.at(it, ("Q", s)))
                            i = projected.index(("Q", s)) % 2
                            sp.dma_start(q_dram[s].rearrange("(n r k) -> r n k", r=128, k=GT),
                                         parts[i][:].rearrange("r p t k -> r (p t) k")).then_inc(
                                *written["Q", s].rise("parts"))
                            for k in range(KT):
                                sp.wait_ge(parts_ready.sem, parts_ready.at(it, ("K", s, k)))
                                i = projected.index(("K", s, k)) % 2
                                n = 3 * k_tiles
                                of = parts[i][:].rearrange("r p t k -> r (p t) k") if k_tiles == DT else \
                                    parts[i][0:k_rows, :, 0, :]
                                sp.dma_start(k_dram[s][k][0:n * k_rows * GT].rearrange("(n r k) -> r n k", r=k_rows, k=GT),
                                             of).then_inc(
                                    *written["K", s, k].rise("parts"))
                            sp.wait_ge(b_full.sem, b_full.prev(it, (last_unit[s], 1)))
                            sp.wait_ge(written["Q", s].sem, written["Q", s].at(it, "parts"))
                            part = HD * H * GT
                            for i, (p0, slot, n, rep) in enumerate(Q_SLOTS):
                                sp.dma_start(q_stack[s][slot * HD:(slot + n) * HD, :, :],
                                             q_dram[s][p0 * part:(p0 + n) * part].rearrange(
                                                 "(r h k) -> r h k", h=H, k=GT)).then_inc(*q_stacked[s].rise(i))
                            part = HD * KV * GT
                            for k in range(KT):
                                sp.wait_ge(written["K", s, k].sem, written["K", s, k].at(it, "parts"))
                                for i, (p0, slot, n, rep) in enumerate(K_SLOTS):
                                    of = k_dram[s][k][p0 * part:(p0 + 1) * part]
                                    of = of.rearrange("(o r n) -> o r n", o=1, r=HD).broadcast_to([rep, HD, KV * GT])
                                    sp.dma_start(
                                        k_stack[s][slot * HD:(slot + rep) * HD, k, :, :].rearrange("p h t -> p (h t)"),
                                        of).then_inc(*k_stacked[s].rise((k, i)))
                            if not L.float_mask:
                                row = bias_dram[1 if KT == 2 else 0, bass.ds((it * (G * S) + s * G) * T, GT)]
                                sp.dma_start(k_stack[s][PR:PR + 1, 0, :, :],
                                             row.rearrange("(o h t) -> o h t", o=1, h=1).broadcast_to([1, KV, GT])
                                             ).then_inc(*k_stacked[s].rise("bias"))
                            if L.store_ct:
                                sp.wait_ge(lo_ready.sem, lo_ready.at(it, ("TC", s)))
                                for i, t in enumerate((c_hi[s], c_lo[s])):
                                    sp.dma_start(ct_dram[bass.ds(it, 1), s, i, :, :].rearrange("i p n -> (i p) n"),
                                                 f32(t[:]).rearrange("p k t -> p (k t)")).then_inc(
                                        *ct_stored[s].rise(("hi", "lo")[i]))
                        for s in range(S):
                            g, key = (out_of(("O", s)), ("O", s)) if L.name == "L3" else (y_ready, s)
                            sp.wait_ge(g.sem, g.at(it, key))
                            sp.dma_start(tok_rows(dst, it, s), y_tile[s][:]).then_inc(*y_stored[s].rise("y"))
                    for s in range(S):
                        sp.wait_ge(y_stored[s].sem, y_stored[s].at(PASSES - 1, "y"))
                        if L.store_ct:
                            sp.wait_ge(ct_stored[s].sem, ct_stored[s].at(PASSES - 1, "lo"))

                @block.tensor
                def _(pe):
                    def split_product(dst_ap, lhs, rhs, start=True, stop=True):
                        n = len(lhs)
                        for i, (a, b) in enumerate(zip(lhs, rhs)):
                            for j, (x, w) in enumerate(((a[0], b[0]), (a[0], b[1]), (a[1], b[0]))):
                                last = nc.tensor.matmul(dst_ap, x, w, start=start and i == 0 and j == 0,
                                                        stop=stop and i == n - 1 and j == 2)
                        return last

                    with pe.Fori(0, PASSES) as it:
                        def take(key):
                            pe.wait_ge(out_of(key).sem, out_of(key).back(it, key, 1))
                            return bank(key)

                        def turn(key, source):
                            d = take(key)
                            for kt in range(DT):
                                for b in range(G):
                                    last = nc.tensor.transpose(d[:, kt * GT + b * T:kt * GT + b * T + T],
                                                               source[:, b, 128 * kt:128 * kt + 128], ident[:])
                            last.then_inc(*d_full.rise(key))

                        for s in range(S):
                            if L.ln_x:
                                pe.wait_ge(norm_ready.sem, norm_ready.at(it, ("in", s)))
                                turn(("TX", s), norm[s])
                            else:
                                pe.wait_ge(x_loaded[s].sem, x_loaded[s].at(it, "x"))
                                turn(("TX", s), x_tok[s])
                            if not L.load_ct:
                                if L.ln_c:
                                    pe.wait_ge(norm_ready.sem, norm_ready.at(it, ("in", s)))
                                    turn(("TC", s), norm[s])
                                else:
                                    pe.wait_ge(c_loaded[s].sem, c_loaded[s].at(it, "c"))
                                    turn(("TC", s), c_tok[s])

                        def transposed_projection(key, w, source, tiles, rows_n):
                            d = take(key)
                            hi, lo = both(w)
                            for t in range(tiles):
                                cut = slice(rows_n * t, rows_n * t + rows_n)
                                last = split_product(
                                    d[0:rows_n, t * GT:t * GT + GT],
                                    [(hi[:, kt, cut], lo[:, kt, cut]) for kt in range(DT)],
                                    [(source[0][:, kt, :], source[1][:, kt, :]) for kt in range(DT)])
                            last.then_inc(*d_full.rise(key))

                        def projection(key, w, source, width):
                            d = take(key)
                            hi, lo = both(w)
                            for b in range(G):
                                cut = slice(b * T, b * T + T)
                                last = split_product(
                                    d[:, b * width:(b + 1) * width],
                                    [(source[0][:, kt, cut], source[1][:, kt, cut]) for kt in range(DT)],
                                    [(hi[:, kt, :], lo[:, kt, :]) for kt in range(DT)])
                            last.then_inc(*d_full.rise(key))

                        xs = [(x_hi[s], x_lo[s]) for s in range(S)]
                        cs = [(c_hi[s], c_lo[s]) for s in range(S)]
                        for s in range(S):
                            pe.wait_ge(lo_ready.sem, lo_ready.at(it, ("TX", s)))
                            transposed_projection(("Q", s), "q", xs[s], DT, 128)
                            if L.load_ct:
                                pe.wait_ge(c_loaded[s].sem, c_loaded[s].at(it, c_loaded[s].keys[-1]))
                            else:
                                pe.wait_ge(lo_ready.sem, lo_ready.at(it, ("TC", s)))
                            for k in range(KT):
                                transposed_projection(("K", s, k), "k", (cs, xs)[k][s], k_tiles, k_rows)
                        for s in range(S):
                            for k in range(KT):
                                projection(("V", s, k), "v", (cs, xs)[k][s], kc)

                        def scores_for_maxima(n):
                            s, b, h0 = L.units[n]
                            if n % (N // 2) == 0:
                                pe.wait_ge(q_stacked[s].sem, q_stacked[s].at(it, 2))
                                pe.wait_ge(k_stacked[s].sem, k_stacked[s].at(it, k_loads[-1]))
                                if L.float_mask:
                                    pe.wait_ge(mask_lo_ready.sem, mask_lo_ready.at(it, s))
                            pe.wait_ge(a_out.sem, a_out.back(it, n, 2))
                            a = ps_a[n % 2]
                            cut = slice(b * T, b * T + T)
                            for i in range(U):
                                if L.float_mask and i % 4 == 0:
                                    for j, m in enumerate((hid_hi[s], hid_lo[s])):
                                        nc.tensor.matmul(a[:, i * T:(i + 4) * T], ident_r[:],
                                                         repeat(m[:].rearrange("p a b -> p (a b)")[:, cut], 4),
                                                         start=j == 0, stop=False, skip_group_check=True)
                                last = nc.tensor.matmul(
                                    a[:, i * KT * T:(i + 1) * KT * T], q_stack[s][:, h0 + i, cut],
                                    k_stack[s][:, :, (h0 + i) // L.group, cut] if KT == 2 else
                                    k_stack[s][:, 0, (h0 + i) // L.group, cut],
                                    start=not L.float_mask, stop=True, skip_group_check=L.float_mask)
                            last.then_inc(*a_full.rise(n))

                        def turn_maxima(n):
                            pe.wait_ge(m_ready.sem, m_ready.at(it, n))
                            d = take(("MT", n))
                            nc.tensor.transpose(d[:, 0:64].bitcast(BF16), m_parts[:, n % 2, :], ident_b[:]).then_inc(
                                *d_full.rise(("MT", n)))

                        def scores_less_maxima(n):
                            s, b, h0 = L.units[n]
                            pe.wait_ge(out_of(("MT", n)).sem, out_of(("MT", n)).at(it, ("MT", n)))
                            cut = slice(b * T, b * T + T)
                            for f in range(2):
                                pe.wait_ge(b_out.sem, b_out.back(it, (n, f), 2))
                                d = ps_b[f]
                                if L.float_mask:
                                    for j, m in enumerate((hid_hi[s], hid_lo[s])):
                                        nc.tensor.matmul(d[:], m[:].rearrange("p a b -> p (a b)")[:, cut],
                                                         repeat(ident_r[:], 4), start=j == 0, stop=False,
                                                         skip_group_check=True)
                                for j in range(4):
                                    i, k = (j, f) if KT == 2 else (4 * f + j, 0)
                                    to = d[:, j * T:(j + 1) * T]
                                    nc.tensor.matmul(to, k_stack[s][:, k, (h0 + i) // L.group, cut],
                                                     q_stack[s][:, h0 + i, cut], start=not L.float_mask, stop=False,
                                                     skip_group_check=L.float_mask)
                                    last = nc.tensor.matmul(to, select[:, i, :], m_rows[:, n % 2, :], start=False,
                                                            stop=True, skip_group_check=L.float_mask)
                                last.then_inc(*b_full.rise((n, f)))

                        def weighted_values(n):
                            s, b, h0 = L.units[n]
                            if n % (N // 2) == 0:
                                for k in range(KT):
                                    v = out_of(("V", s, k))
                                    pe.wait_ge(v.sem, v.at(it, ("V", s, k)))
                            pe.wait_ge(b_out.sem, b_out.at(it, (n, 1)))
                            d = take(("PV", n))
                            for k in range(KT):
                                for i in range(U):
                                    half, j = (k, i) if KT == 2 else (i // 4, i % 4)
                                    p = probs[:, (2 * n + half) % 4, j * T:(j + 1) * T]
                                    last = nc.tensor.matmul(
                                        d[32 * (i % 4):32 * (i % 4) + 32, (i // 4) * T:(i // 4) * T + T],
                                        value[s][:, b * KT + k, (h0 + i) // L.group, :], p, start=k == 0,
                                        stop=k == KT - 1)
                            last.then_inc(*d_full.rise(("PV", n)))

                        def turn_outputs(n):
                            pv = out_of(("PV", n))
                            pe.wait_ge(pv.sem, pv.at(it, ("PV", n)))
                            d = take(("OT", n))
                            for i in range(U // 4):
                                last = nc.tensor.transpose(d[:, i * T:(i + 1) * T], o_t[:, i * T:(i + 1) * T], ident[:])
                            last.then_inc(*d_full.rise(("OT", n)))

                        scores_for_maxima(0)
                        scores_for_maxima(1)
                        for n in range(N + 1):
                            if n < N:
                                turn_maxima(n)
                            if n + 2 < N:
                                scores_for_maxima(n + 2)
                            if n:
                                weighted_values(n - 1)
                            if n < N:
                                scores_less_maxima(n)
                            if n:
                                turn_outputs(n - 1)

                        for s in range(S):
                            ot = ("OT", last_unit[s])
                            pe.wait_ge(out_of(ot).sem, out_of(ot).at(it, ot))
                            turn(("TO", s), heads_out[s])
                        for s in range(S):
                            pe.wait_ge(lo_ready.sem, lo_ready.at(it, ("TO", s)))
                            projection(("O", s), "o", xs[s], D)
                        if L.mlp:
                            for s in range(S):
                                pe.wait_ge(norm_ready.sem, norm_ready.at(it, ("mid", s)))
                                turn(("TL", s), norm[s])
                            f_hi, f_lo = both("f")
                            g_hi, g_lo = both("m")

                            def hidden(s, c):
                                d = take(("F", s, c))
                                for j in range(2):
                                    cut = slice((2 * c + j) * 128, (2 * c + j) * 128 + 128)
                                    last = split_product(
                                        d[:, j * GT:(j + 1) * GT],
                                        [(f_hi[:, kt, cut], f_lo[:, kt, cut]) for kt in range(DT)],
                                        [(x_hi[s][:, kt, :], x_lo[s][:, kt, :]) for kt in range(DT)])
                                last.then_inc(*d_full.rise(("F", s, c)))

                            def mlp_out(s, c):
                                pe.wait_ge(hid_lo_ready.sem, hid_lo_ready.at(it, (s, c)))
                                if c == 0:
                                    pe.wait_ge(a_out.sem, a_out.back(it, ("M", s), 2))
                                hi, lo = hid_hi[c % 2], hid_lo[c % 2]
                                for b in range(G):
                                    cut = slice(b * T, b * T + T)
                                    last = split_product(
                                        ps_a[s][:, 512 * b:512 * b + D],
                                        [(hi[:, j, cut], lo[:, j, cut]) for j in range(2)],
                                        [(g_hi[:, 2 * c + j, :], g_lo[:, 2 * c + j, :]) for j in range(2)],
                                        start=c == 0, stop=c == FT // 2 - 1)
                                last.then_inc(*hid_used.rise((s, c)))

                            for s in range(S):
                                pe.wait_ge(lo_ready.sem, lo_ready.at(it, ("TL", s)))
                                hidden(s, 0)
                                for c in range(1, FT // 2):
                                    hidden(s, c)
                                    mlp_out(s, c - 1)
                                mlp_out(s, FT // 2 - 1)

                @block.scalar
                def _(act):
                    with act.Fori(0, PASSES) as it:
                        def full(key):
                            act.wait_ge(d_full.sem, d_full.at(it, key))
                            return bank(key)

                        def turned_out(key, w_col=None, b_col=None):
                            i = turned.index(key)
                            d = full(key)
                            act.wait_ge(lo_ready.sem, lo_ready.back(it, key, 2))
                            if w_col is None:
                                nc.scalar.activation(t32[i % 2][:].rearrange("p a b -> p (a b)"), d[:],
                                                     ACT.Copy).then_inc(*out_of(key).rise(key))
                                return
                            for kt in range(DT):
                                last = nc.scalar.activation(
                                    t32[i % 2][:, kt, :], d[:, kt * GT:kt * GT + GT], ACT.Identity,
                                    scale=cols[:, w_col + kt:w_col + kt + 1],
                                    bias=cols[:, b_col + kt:b_col + kt + 1] if b_col is not None else 0.0)
                            last.then_inc(*out_of(key).rise(key))

                        for s in range(S):
                            turned_out(("TX", s), *((W1_COL, B1_COL) if L.ln_x else ()))
                            if not L.load_ct:
                                turned_out(("TC", s), *((W1_COL, B1_COL) if L.ln_c else ()))
                        for key in projected:
                            i = projected.index(key)
                            d = full(key)
                            act.wait_ge(parts_ready.sem, parts_ready.back(it, key, 2))
                            is_q = key[0] == "Q"
                            p, tiles = (128, DT) if is_q else (k_rows, k_tiles)
                            for t in range(tiles):
                                col = (Q_COL if is_q else K_COL) + t
                                last = nc.scalar.activation(
                                    qk32[i % 2][0:p, t, :], d[0:p, t * GT:t * GT + GT], ACT.Identity,
                                    scale=L.scale if is_q else 1.0,
                                    bias=cols[0:p, col:col + 1] if "q" in vectors else 0.0)
                            last.then_inc(*out_of(key).rise(key))

                        for n in range(N + 1):
                            if n < N:
                                d = full(("MT", n))
                                nc.scalar.activation(m_rows[:, n % 2, :], d[:, 0:64].bitcast(BF16), ACT.Copy).then_inc(
                                    *out_of(("MT", n)).rise(("MT", n)))
                            if n:
                                d = full(("PV", n - 1))
                                if n == 1:
                                    act.wait_ge(d_full.sem, d_full.prev(it, ("OT", N - 1)))
                                else:
                                    act.wait_ge(d_full.sem, d_full.at(it, ("OT", n - 2)))
                                nc.scalar.activation(o_t[:, 0:U * 32], d[:, 0:U * 32], ACT.Copy).then_inc(
                                    *out_of(("PV", n - 1)).rise(("PV", n - 1)))
                            if n < N:
                                for f in range(2):
                                    act.wait_ge(b_full.sem, b_full.at(it, (n, f)))
                                    nc.scalar.activation(probs[:, (2 * n + f) % 4, :], ps_b[f][:], ACT.Exp).then_inc(
                                        *b_out.rise((n, f)))

                        for s in range(S):
                            turned_out(("TO", s))
                        if L.mlp:
                            for s in range(S):
                                turned_out(("TL", s), W2_COL, B2_COL if "b2" in vectors else None)
                            for s in range(S):
                                for c in chunks_f:
                                    d = full(("F", s, c))
                                    act.wait_ge(hid_lo_ready.sem, hid_lo_ready.back(it, (s, c), 2))
                                    for j in range(2):
                                        col = F_COL + 2 * c + j
                                        last = nc.scalar.activation(hid32[c % 2][:, j, :], d[:, j * GT:(j + 1) * GT],
                                                                    ACT.Gelu_apprx_tanh, bias=cols[:, col:col + 1])
                                    last.then_inc(*out_of(("F", s, c)).rise(("F", s, c)))

                @block.vector
                def _(dve):
                    with dve.Fori(0, PASSES) as it:
                        def full(key):
                            dve.wait_ge(d_full.sem, d_full.at(it, key))
                            return bank(key)

                        def here():
                            dve.wait_ge(step.sem, step.now(it))

                        def norm_stats(which, s, source):
                            for b in range(G):
                                nc.vector.bn_stats(out=stats[:, s, b, :], in_=source[:, b, :]).then_inc(*step.tick())
                            here()
                            nc.vector.tensor_copy(spare[:], minus_half[:, 0:1])
                            for b in range(G):
                                nc.vector.bn_aggr(out=moments[:, s, b, :], in_=stats[:, s, b, :]).then_inc(*step.tick())
                            here()
                            if L.name == "L2":
                                nc.vector.tensor_tensor(out=spread[:, s, :], in0=moments[:, s, :, 0],
                                                        in1=moments[:, s, :, 0], op=ALU.mult).then_inc(*step.tick())
                                here()
                                nc.vector.scalar_tensor_tensor(
                                    out=spread[:, s, :], in0=moments[:, s, :, 1], scalar=L.eps, in1=spread[:, s, :],
                                    op0=ALU.add, op1=ALU.add).then_inc(*spread_ready.rise((which, s)))
                            else:
                                nc.vector.tensor_scalar(spread[:, s, :], moments[:, s, :, 1], L.eps, None,
                                                        ALU.add).then_inc(*spread_ready.rise((which, s)))

                        def normalise(which, s, source):
                            dve.wait_ge(rstd_ready.sem, rstd_ready.at(it, (which, s)))
                            for b in range(G):
                                if L.name == "L2":
                                    last = nc.vector.tensor_scalar(norm[s][:, b, :], source[:, b, :],
                                                                   rstd[:, s, b:b + 1], None, ALU.mult)
                                else:
                                    last = nc.vector.tensor_scalar(norm[s][:, b, :], source[:, b, :],
                                                                   moments[:, s, b, 0:1], rstd[:, s, b:b + 1],
                                                                   ALU.subtract, ALU.mult)
                            last.then_inc(*norm_ready.rise((which, s)))

                        def hi_half(key):
                            s = key[1]
                            to = c_hi[s] if key[0] == "TC" else x_hi[s]
                            dve.wait_ge(out_of(key).sem, out_of(key).at(it, key))
                            if key[0] == "TC" and L.store_ct:
                                dve.wait_ge(ct_stored[s].sem, ct_stored[s].prev(it, "lo"))
                            nc.vector.tensor_copy(to[:], t32[turned.index(key) % 2][:]).then_inc(*hi_ready.rise(key))

                        if L.ln_x or L.ln_c:
                            tok = x_tok if L.ln_x else c_tok
                            for s in range(S):
                                g = x_loaded[s] if L.ln_x else c_loaded[s]
                                dve.wait_ge(g.sem, g.at(it, g.keys[-1]))
                                norm_stats("in", s, tok[s])
                            for s in range(S):
                                dve.wait_ge(d_full.sem, d_full.prev(it, ("TL" if L.mlp else "TC", s)))
                                normalise("in", s, tok[s])
                        for s in range(S):
                            hi_half(("TX", s))
                            if not L.load_ct:
                                hi_half(("TC", s))
                        if L.float_mask:
                            for s in range(S):
                                dve.wait_ge(c_loaded[s].sem, c_loaded[s].at(it, "mask"))
                                dve.wait_ge(b_full.sem, b_full.prev(it, (last_unit[s], 1)))
                                nc.vector.tensor_copy(hid_hi[s][:].rearrange("p a b -> p (a b)")[:, 0:GT],
                                                      c_tok[s][:, :, 0:T]).then_inc(*mask_hi_ready.rise(s))

                        for n, key in enumerate(projected):
                            dve.wait_ge(out_of(key).sem, out_of(key).at(it, key))
                            g = written[projected[n - 2]]
                            dve.wait_ge(g.sem, g.at(it, "parts") if n >= 2 else g.prev(it, "parts"))
                            p, tiles = (128, DT) if key[0] == "Q" else (k_rows, k_tiles)
                            rest = qk32[n % 2][0:p, 0:tiles, :]
                            part = [parts[n % 2][0:p, i, 0:tiles, :] for i in range(3)]
                            nc.vector.tensor_copy(part[0], rest).then_inc(*step.tick())
                            here()
                            nc.vector.tensor_tensor(out=rest, in0=rest, in1=part[0], op=ALU.subtract).then_inc(
                                *step.tick())
                            here()
                            nc.vector.tensor_copy(part[1], rest).then_inc(*step.tick())
                            here()
                            nc.vector.tensor_tensor(out=part[2], in0=rest, in1=part[1], op=ALU.subtract).then_inc(
                                *parts_ready.rise(key))

                        for s in range(S):
                            for k in range(KT):
                                d = full(("V", s, k))
                                for b in range(G):
                                    to = value[s][:, b * KT + k, :, 0:HD]
                                    of = by_head(d[:, b * kc:(b + 1) * kc])
                                    if "q" in vectors:
                                        last = nc.vector.tensor_tensor(out=to, in0=of,
                                                                       in1=by_head(rows[:, V_BIAS, 0:kc]), op=ALU.add)
                                    else:
                                        last = nc.vector.tensor_copy(to, of)
                                last.then_inc(*out_of(("V", s, k)).rise(("V", s, k)))

                        def maxima(n):
                            dve.wait_ge(a_full.sem, a_full.at(it, n))
                            nc.vector.tensor_reduce(out=m_neg[:, n % 2, 0:U],
                                                    in_=ps_a[n % 2][:].rearrange("p (h k) -> p h k", h=U), axis=AX.X,
                                                    op=ALU.max, negate=True).then_inc(*a_out.rise(n))
                            dve.wait_ge(a_out.sem, a_out.at(it, n))
                            nc.vector.tensor_copy(m_parts[:, n % 2, 0:U], m_neg[:, n % 2, 0:U]).then_inc(*step.tick())
                            here()
                            nc.vector.tensor_tensor(out=m_parts[:, n % 2, 8:8 + U], in0=m_neg[:, n % 2, 0:U],
                                                    in1=m_parts[:, n % 2, 0:U], op=ALU.subtract).then_inc(
                                *m_ready.rise(n))

                        def divide(n):
                            s, b, h0 = L.units[n]
                            if n % (N // 2) == 0:
                                dve.wait_ge(y_stored[s].sem, y_stored[s].prev(it, "y"))
                            key = ("OT", n)
                            d = full(key)[:, 0:U * 32].rearrange("p (h e) -> p h e", e=32)
                            nc.vector.reciprocal(r_inv[:, n % 2, 0:U].unsqueeze(2), d[:, :, HD:HD + 1]).then_inc(
                                *step.tick())
                            here()
                            nc.vector.tensor_tensor(
                                out=by_head(heads_out[s][:, b, h0 * HD:(h0 + U) * HD]), in0=d[:, :, 0:HD],
                                in1=r_inv[:, n % 2, 0:U].unsqueeze(2).broadcast_to([128, U, HD]),
                                op=ALU.mult).then_inc(*out_of(key).rise(key))

                        for n in range(N + 3):
                            if n < N:
                                maxima(n)
                            if n >= 3:
                                divide(n - 3)

                        for s in range(S):
                            hi_half(("TO", s))
                        for s in range(S):
                            d = full(("O", s))
                            h = heads_out[s][:].rearrange("p b d -> p (b d)")
                            if L.name == "L3":
                                for b in range(G):
                                    last = nc.vector.scalar_tensor_tensor(
                                        out=heads_out[s][:, b, :], in0=d[:, b * D:(b + 1) * D],
                                        scalar=gate[:, bass.ds(it * (G * S) + (2 + s * G + b), 1)],
                                        in1=x_tok[s][:, b, :], op0=ALU.mult, op1=ALU.add)
                                last.then_inc(*out_of(("O", s)).rise(("O", s)))
                                continue
                            nc.vector.tensor_tensor(out=h, in0=d[:], in1=x_tok[s][:].rearrange("p b d -> p (b d)"),
                                                    op=ALU.add).then_inc(*out_of(("O", s)).rise(("O", s)))
                            dve.wait_ge(out_of(("O", s)).sem, out_of(("O", s)).at(it, ("O", s)))
                            nc.vector.tensor_tensor(out=heads_out[s][:], in0=heads_out[s][:],
                                                    in1=repeat(rows[:, O_BIAS, :], G), op=ALU.add).then_inc(*step.tick())
                            here()
                            norm_stats("mid", s, heads_out[s])
                        if L.name != "L3":
                            for s in range(S):
                                if L.float_mask:
                                    dve.wait_ge(y_stored[s].sem, y_stored[s].prev(it, "y"))
                                normalise("mid", s, heads_out[s])
                        if L.mlp:
                            for s in range(S):
                                hi_half(("TL", s))
                            for s in range(S):
                                for c in chunks_f:
                                    f = out_of(("F", s, c))
                                    dve.wait_ge(f.sem, f.at(it, ("F", s, c)))
                                    dve.wait_ge(hid_used.sem, hid_used.back(it, (s, c), 2))
                                    nc.vector.tensor_copy(hid_hi[c % 2][:], hid32[c % 2][:]).then_inc(
                                        *hid_hi_ready.rise((s, c)))
                                dve.wait_ge(hid_used.sem, hid_used.at(it, (s, FT // 2 - 1)))
                                nc.vector.tensor_tensor(
                                    out=heads_out[s][:], in0=ps_a[s][:].rearrange("p (b n) -> p b n", b=G)[:, :, 0:D],
                                    in1=(x_tok if L.name == "L2" else heads_out)[s][:], op=ALU.add).then_inc(
                                    *a_out.rise(("M", s)))
                                dve.wait_ge(a_out.sem, a_out.at(it, ("M", s)))
                                nc.vector.tensor_tensor(out=heads_out[s][:], in0=heads_out[s][:],
                                                        in1=repeat(rows[:, M_BIAS, :], G), op=ALU.add).then_inc(
                                    *y_ready.rise(s))

                @block.gpsimd
                def _(pool):
                    with pool.Fori(0, PASSES) as it:
                        def power(key):
                            pool.wait_ge(spread_ready.sem, spread_ready.at(it, key))
                            nc.gpsimd.tensor_tensor(out=rstd[:, key[1], :], in0=spread[:, key[1], :],
                                                    in1=minus_half[:], op=ALU.pow).then_inc(*rstd_ready.rise(key))

                        def lo_half(key):
                            s = key[1]
                            hi, lo = (c_hi[s], c_lo[s]) if key[0] == "TC" else (x_hi[s], x_lo[s])
                            pool.wait_ge(hi_ready.sem, hi_ready.at(it, key))
                            nc.gpsimd.tensor_tensor(out=lo[:], in0=t32[turned.index(key) % 2][:], in1=f32(hi[:]),
                                                    op=ALU.subtract).then_inc(*lo_ready.rise(key))

                        if L.ln_x or L.ln_c:
                            for s in range(S):
                                power(("in", s))
                        for s in range(S):
                            lo_half(("TX", s))
                            if not L.load_ct:
                                lo_half(("TC", s))
                        if L.float_mask:
                            for s in range(S):
                                pool.wait_ge(mask_hi_ready.sem, mask_hi_ready.at(it, s))
                                nc.gpsimd.tensor_tensor(
                                    out=hid_lo[s][:].rearrange("p a b -> p (a b)")[:, 0:GT].rearrange(
                                        "p (b k) -> p b k", b=G),
                                    in0=c_tok[s][:, :, 0:T],
                                    in1=f32(hid_hi[s][:].rearrange("p a b -> p (a b)")[:, 0:GT]).rearrange(
                                        "p (b k) -> p b k", b=G), op=ALU.subtract).then_inc(*mask_lo_ready.rise(s))
                        for s in range(S):
                            lo_half(("TO", s))
                        if L.name != "L3":
                            for s in range(S):
                                power(("mid", s))
                        if L.float_mask:
                            for s in range(S):
                                pool.wait_ge(norm_ready.sem, norm_ready.at(it, ("mid", s)))
                                nc.gpsimd.tensor_tensor(out=norm[s][:], in0=norm[s][:], in1=repeat(rows[:, GAMMA, :], G),
                                                        op=ALU.mult).then_inc(*scaled.rise(s))
                                pool.wait_ge(scaled.sem, scaled.at(it, s))
                                nc.gpsimd.tensor_tensor(out=norm[s][:], in0=norm[s][:], in1=repeat(rows[:, BETA, :], G),
                                                        op=ALU.add).then_inc(*y_ready.rise(s))
                        if L.mlp:
                            for s in range(S):
                                lo_half(("TL", s))
                            for s in range(S):
                                for c in chunks_f:
                                    pool.wait_ge(hid_hi_ready.sem, hid_hi_ready.at(it, (s, c)))
                                    nc.gpsimd.tensor_tensor(out=hid_lo[c % 2][:], in0=hid32[c % 2][:],
                                                            in1=f32(hid_hi[c % 2][:]), op=ALU.subtract).then_inc(
                                        *hid_lo_ready.rise((s, c)))
            finish(PASSES)


def kernel(**inputs):
    import numpy as _np
    import concourse.bacc as _bacc
    from concourse import mybir as _mybir
    from concourse.bass_utils import run_bass_kernel_spmd as _run

    nc = _bacc.Bacc("TRN2", target_bir_lowering=False, num_devices=1)
    arrays, ins = {}, {}
    for name, a in inputs.items():
        a = _np.ascontiguousarray(a)
        if a.dtype == _np.bool_:
            a = a.view(_np.uint8)
        arrays[f"in_{name}_dram"] = a
        ins[name] = nc.dram_tensor(f"in_{name}_dram", a.shape, _mybir.dt.from_np(a.dtype), kind="ExternalInput").ap()
    out = nc.dram_tensor("out_dram", (B, T, D), _mybir.dt.float32, kind="ExternalOutput").ap()
    xattn_program(nc, ins, out)
    r = _run(nc, [arrays], core_ids=[0])
    return r.results[0]["out_dram"]
```

```python
from contextlib import ExitStack

import concourse.bass as bass
from concourse import mybir

B = 16
T = 128
D = 256
DT = D // 128
INNER = 4 * D
FT = INNER // 128
G = 2
S = 2
GT = G * T
PASSES = B // (G * S)
BIG = 3.0e38
CREDIT = 256
PR = 96

Q_SLOTS = ((0, 0, 3, 1), (0, 3, 2, 1), (0, 5, 1, 1))
K_SLOTS = ((0, 0, 1, 3), (1, 3, 1, 2), (2, 5, 1, 1))


class Layer:
    def __init__(self, name, heads, head, kv_heads, key_tiles, unit, scale, eps, ln_x=False, ln_c=False,
                 load_ct=False, store_ct=False, mlp=False, float_mask=False):
        self.name, self.heads, self.head, self.kv_heads = name, heads, head, kv_heads
        self.key_tiles, self.unit, self.scale, self.eps = key_tiles, unit, scale, eps
        self.ln_x, self.ln_c, self.load_ct, self.store_ct = ln_x, ln_c, load_ct, store_ct
        self.mlp, self.float_mask = mlp, float_mask
        self.group = heads // kv_heads
        self.kcols = kv_heads * head
        self.units = [(s, b, h) for s in range(S) for b in range(G) for h in range(0, heads, unit)]


LAYERS = [
    Layer("L0", 16, 16, 16, 1, 8, 0.25, 1e-5, ln_x=True, store_ct=True, mlp=True),
    Layer("L1", 32, 8, 8, 1, 8, float(8.0 ** -0.5), 1e-6, load_ct=True, float_mask=True),
    Layer("L2", 16, 16, 16, 2, 4, 1.0 / 16, 1e-6, load_ct=True, mlp=True),
    Layer("L3", 16, 16, 16, 1, 8, 0.25, 1e-5, ln_c=True),
]


class Signal:

    def __init__(self, sem, step=1):
        self.sem, self.step, self.total, self.keys, self.risen = sem, step, CREDIT, [], set()

    def plan(self, keys):
        self.keys, self.risen = list(keys), set()
        assert self.step * len(self.keys) < CREDIT, (self.sem, len(self.keys))

    def rise(self, key):
        assert key in self.keys, (self.sem, key)
        self.risen.add(key)
        return self.sem, self.step

    def at(self, it, key):
        return self.total + self.step * (it * len(self.keys) + self.keys.index(key) + 1)

    def prev(self, it, key):
        return self.total + self.step * ((it - 1) * len(self.keys) + self.keys.index(key) + 1)

    def back(self, it, key, n):
        return self.total + self.step * (it * len(self.keys) + self.keys.index(key) + 1 - n)

    def finish(self, passes):
        assert len(self.risen) == len(self.keys), (self.sem, set(self.keys) - self.risen)
        self.total += self.step * len(self.keys) * passes
        self.keys, self.risen = [], set()


class Steps:

    def __init__(self, sem):
        self.sem, self.total, self.it, self.per, self.n = sem, CREDIT, None, 0, 0

    def enter(self, it, per):
        self.total, self.it, self.per, self.n = self.total + self.n, it, per, 0

    def leave(self, layer, passes):
        assert self.n == self.per, f"STEPS {layer} {self.n}"
        self.total, self.it, self.n = self.total + self.per * passes, None, 0

    def tick(self):
        self.n += 1
        return self.sem, 1

    def now(self):
        return self.total + self.n + (0 if self.it is None else self.it * self.per)


STEPS = {"L0": 46, "L1": 54, "L2": 62, "L3": 36}


def xattn_program(nc, ins, out):
    F32, F32R, BF16 = mybir.dt.float32, mybir.dt.float32r, mybir.dt.bfloat16
    ALU, ACT, AX = mybir.AluOpType, mybir.ActivationFunctionType, mybir.AxisListType

    ctx = ExitStack()
    with ctx:
        def sb(name, shape, dt=F32):
            return ctx.enter_context(nc.sbuf_tensor(name, shape, dt))

        def dram(name, shape, dt=F32):
            return nc.dram_tensor(name, shape, dt, kind="Internal").ap()

        signals = []
        PHASES = ("prep", "att", "post")

        def signal(name, step=1):
            signals.append(Signal(ctx.enter_context(nc.semaphore(name)), step))
            return signals[-1]

        W_COLS = 4 * DT * D + 2 * DT * INNER
        whi = sb("weights_hi", [128, W_COLS], F32R)
        wlo = sb("weights_lo", [128, W_COLS], F32R)
        ARENA = 48 * GT
        arena = [sb(f"stacks{s}", [128, ARENA], BF16) for s in range(S)]
        values = [sb(f"values{s}", [128, G * 2 * 16 * 32]) for s in range(S)]
        probs = sb("probs", [128, 4, 512])
        x_in = [sb(f"x_in{s}", [128, G, D]) for s in range(S)]
        x_tok = [sb(f"x_tok{s}", [128, G, D]) for s in range(S)]
        c_tok = [sb(f"c_tok{s}", [128, G, D]) for s in range(S)]
        norm = [sb(f"norm{s}", [128, G, D]) for s in range(S)]
        heads_out = [sb(f"heads_out{s}", [128, G, D]) for s in range(S)]
        t32 = [sb(f"t32_{i}", [128, DT, GT]) for i in range(2)]
        x_hi = [sb(f"x_hi{s}", [128, DT, GT], F32R) for s in range(S)]
        x_lo = [sb(f"x_lo{s}", [128, DT, GT], F32R) for s in range(S)]
        p_hi = [sb(f"p_hi{s}", [128, DT, GT], F32R) for s in range(S)]
        p_lo = [sb(f"p_lo{s}", [128, DT, GT], F32R) for s in range(S)]
        c_hi = [sb(f"c_hi{s}", [128, DT, GT], F32R) for s in range(S)]
        c_lo = [sb(f"c_lo{s}", [128, DT, GT], F32R) for s in range(S)]
        qk32 = [sb(f"qk32_{i}", [128, DT, GT]) for i in range(2)]
        parts = [sb(f"parts{i}", [128, 3, DT, GT], BF16) for i in range(2)]
        hid32 = [sb(f"hid32_{i}", [128, 2, GT]) for i in range(2)]
        hid_hi = [sb(f"hid_hi{i}", [128, 2, GT], F32R) for i in range(2)]
        hid_lo = [sb(f"hid_lo{i}", [128, 2, GT], F32R) for i in range(2)]
        o_t = sb("o_t", [128, 256])
        m_neg = sb("m_neg", [128, 2, 8])
        m_parts = sb("m_parts", [128, 2, 128], BF16)
        m_rows = sb("m_rows", [128, 2, 128], BF16)
        r_inv = sb("r_inv", [128, 2, 8])
        stats = sb("stats", [128, S, G, 6])
        moments = sb("moments", [128, S, G, 2])
        spread = sb("spread", [128, S, G])
        rstd = sb("rstd", [128, S, G])
        minus_half = sb("minus_half", [128, G])
        spare = sb("spare", [128, 1])
        ident = sb("ident", [128, 128])
        ident_r = sb("ident_r", [128, 128], F32R)
        ident_b = sb("ident_b", [128, 128], BF16)
        select = sb("select", [128, 8, 128], BF16)
        rows = sb("rows", [128, 5, D])
        V_BIAS, O_BIAS, M_BIAS, GAMMA, BETA = range(5)
        cols = sb("cols", [128, 12 + FT])
        Q_COL, K_COL, W1_COL, B1_COL, W2_COL, B2_COL, F_COL = 0, 2, 4, 6, 8, 10, 12
        mask_f = sb("mask_f", [B, T])
        mask_u8 = sb("mask_u8", [B, T], mybir.dt.uint8)
        mask_i32 = sb("mask_i32", [B, T], mybir.dt.int32)
        mask_b = sb("mask_b", [B, 2, T], BF16)
        key_ok = sb("key_ok", [B, 3])
        gate = sb("gate", [128, 2 + B])

        ps_a = [ctx.enter_context(nc.psum_tensor(f"ps_a{i}", [128, 1024], F32)) for i in range(2)]
        ps_b = [ctx.enter_context(nc.psum_tensor(f"ps_b{i}", [128, 512], F32)) for i in range(2)]
        ps_d = [ctx.enter_context(nc.psum_tensor(f"ps_d{i}", [128, 512], F32)) for i in range(2)]

        x_dram = [ins["x"]] + [dram(f"x_after{i}", [B, T, D]) for i in range(3)] + [out]
        ct_dram = dram("ct", [PASSES, S, 2, 128, DT * GT])
        bias_dram = dram("key_bias", [2, B * T], BF16)
        ok_dram = dram("key_ok_rows", [B])
        q_dram = [dram(f"q_parts{s}", [3 * D * GT], BF16) for s in range(S)]
        k_dram = [[dram(f"k_parts{s}_{k}", [3 * D * GT], BF16) for k in range(2)] for s in range(S)]

        eye_ready = signal("eye_ready")
        const_ready = signal("const_ready")
        tanh_ready = signal("tanh_ready")
        const_loaded = signal("const_loaded", 16)
        bias_stored = signal("bias_stored", 16)
        factor_loaded = signal("factor_loaded", 16)
        raw_loaded = [signal(f"raw_loaded{i}", 16) for i in range(4)]
        raw_split = signal("raw_split")
        raw_turned = signal("raw_turned")
        vectors_loaded = signal("vectors_loaded", 16)
        vectors_ready = signal("vectors_ready")
        stacks_clear = signal("stacks_clear")
        x_loaded = [signal(f"x_loaded{s}", 16) for s in range(S)]
        residual_loaded = [signal(f"residual_loaded{s}", 16) for s in range(S)]
        c_loaded = [signal(f"c_loaded{s}", 16) for s in range(S)]
        ct_stored = [signal(f"ct_stored{s}", 16) for s in range(S)]
        written = {("Q", s): signal(f"q_written{s}", 16) for s in range(S)}
        written.update({("K", s, k): signal(f"k_written{s}_{k}", 16) for s in range(S) for k in range(2)})
        q_stacked = [signal(f"q_stacked{s}", 16) for s in range(S)]
        k_stacked = [signal(f"k_stacked{s}", 16) for s in range(S)]
        y_stored = [signal(f"y_stored{s}", 16) for s in range(S)]
        spread_ready = {f: signal(f"spread_ready_{f}") for f in ("prep", "post")}
        rstd_ready = {f: signal(f"rstd_ready_{f}") for f in ("prep", "post")}
        norm_ready = {f: signal(f"norm_ready_{f}") for f in ("prep", "post")}
        d_full = {f: signal(f"d_full_{f}") for f in PHASES}
        d_out = {f: [signal(f"d_out{i}_{f}") for i in range(2)] for f in PHASES}
        hi_ready = {f: signal(f"hi_ready_{f}") for f in ("prep", "post")}
        lo_ready = {f: signal(f"lo_ready_{f}") for f in ("prep", "post")}
        parts_ready = signal("parts_ready")
        mask_hi_ready = signal("mask_hi_ready")
        mask_lo_ready = signal("mask_lo_ready")
        a_full = signal("a_full")
        a_out = signal("a_out")
        m_ready = signal("m_ready")
        b_full = signal("b_full")
        b_out = signal("b_out")
        hid_hi_ready = signal("hid_hi_ready")
        hid_lo_ready = signal("hid_lo_ready")
        hid_used = signal("hid_used")
        y_ready = signal("y_ready")
        scaled = signal("scaled")
        step = Steps(ctx.enter_context(nc.semaphore("vector_step")))

        def finish(passes):
            for g in signals:
                if g.keys:
                    g.finish(passes)

        def f32(ap):
            return ap.bitcast(F32)

        def repeat(ap, n):
            return ap.unsqueeze(1).broadcast_to([ap.shape[0], n, ap.shape[1]])

        with nc.Block() as block:
            @block.sync
            def _(sp):
                for g in signals + [step]:
                    sp.sem_inc(g.sem, CREDIT)

        eye_ready.plan(["zero", "half", "eye"])
        const_ready.plan(["eye_b", "eye_r", "select", "no_max", "mask_f", "count", "bias0", "bias1", "inverse",
                          "ok", "factors"])
        tanh_ready.plan(["gate"])
        const_loaded.plan(["u8", "i32", "gate"])
        bias_stored.plan(["bias", "ok"])
        factor_loaded.plan(["ok"])
        with nc.Block() as block:
            @block.sync
            def _(sp):
                sp.dma_start(mask_u8[:], ins["mask_BxS2_bf1"]).then_inc(*const_loaded.rise("u8"))
                sp.dma_start(mask_i32[:], ins["mask_BxS2_ik0"]).then_inc(*const_loaded.rise("i32"))
                sp.dma_start(gate[:, 0:1], ins["L3_xattn_gate"].partition_broadcast(128)).then_inc(
                    *const_loaded.rise("gate"))
                sp.wait_ge(const_ready.sem, const_ready.at(0, "ok"))
                sp.dma_start(bias_dram.rearrange("m (b t) -> b m t", b=B), mask_b[:]).then_inc(
                    *bias_stored.rise("bias"))
                sp.dma_start(ok_dram.unsqueeze(1), key_ok[:, 0:1]).then_inc(*bias_stored.rise("ok"))
                sp.wait_ge(bias_stored.sem, bias_stored.at(0, "ok"))
                sp.dma_start(gate[:, 2:2 + B], ok_dram.partition_broadcast(128)).then_inc(
                    *factor_loaded.rise("ok"))

            @block.gpsimd
            def _(pool):
                nc.gpsimd.memset(ident[:], 0.0).then_inc(*eye_ready.rise("zero"))
                nc.gpsimd.memset(minus_half[:], -0.5).then_inc(*eye_ready.rise("half"))
                pool.wait_ge(eye_ready.sem, eye_ready.at(0, "half"))
                nc.gpsimd.affine_select(out=ident[:], in_=ident[:], compare_op=ALU.not_equal, fill=1.0, base=0,
                                        pattern=[[-1, 128]], channel_multiplier=1).then_inc(
                    *eye_ready.rise("eye"))

            @block.vector
            def _(dve):
                dve.wait_ge(eye_ready.sem, eye_ready.at(0, "eye"))
                nc.vector.tensor_copy(ident_b[:], ident[:]).then_inc(*const_ready.rise("eye_b"))
                nc.vector.tensor_copy(ident_r[:], ident[:]).then_inc(*const_ready.rise("eye_r"))
                nc.vector.tensor_tensor(
                    out=select[:], in0=ident[:, 0:8].unsqueeze(2).broadcast_to([128, 8, 128]),
                    in1=ident[:, 8:16].unsqueeze(2).broadcast_to([128, 8, 128]), op=ALU.add).then_inc(
                    *const_ready.rise("select"))
                nc.vector.memset(m_parts[:], 0.0).then_inc(*const_ready.rise("no_max"))
                dve.wait_ge(const_loaded.sem, const_loaded.at(0, "gate"))
                nc.vector.tensor_copy(mask_f[:], mask_u8[:]).then_inc(*const_ready.rise("mask_f"))
                dve.wait_ge(const_ready.sem, const_ready.at(0, "mask_f"))
                nc.vector.tensor_reduce(out=key_ok[:, 1:2], in_=mask_f[:], axis=AX.X, op=ALU.add).then_inc(
                    *const_ready.rise("count"))
                nc.vector.tensor_scalar(mask_b[:, 0, :], mask_f[:], 0.0, -BIG, ALU.is_equal,
                                        ALU.mult).then_inc(*const_ready.rise("bias0"))
                nc.vector.tensor_scalar(mask_b[:, 1, :], mask_i32[:], 0.0, -BIG, ALU.is_equal,
                                        ALU.mult).then_inc(*const_ready.rise("bias1"))
                dve.wait_ge(const_ready.sem, const_ready.at(0, "bias1"))
                nc.vector.reciprocal(key_ok[:, 2:3], key_ok[:, 1:2]).then_inc(*const_ready.rise("inverse"))
                dve.wait_ge(const_ready.sem, const_ready.at(0, "inverse"))
                nc.vector.tensor_scalar(key_ok[:, 0:1], key_ok[:, 2:3], 0.0, 1.0, ALU.mult,
                                        ALU.add).then_inc(*const_ready.rise("ok"))
                dve.wait_ge(factor_loaded.sem, factor_loaded.at(0, "ok"))
                dve.wait_ge(tanh_ready.sem, tanh_ready.at(0, "gate"))
                nc.vector.tensor_scalar(gate[:, 2:2 + B], gate[:, 2:2 + B], gate[:, 1:2], None,
                                        ALU.mult).then_inc(*const_ready.rise("factors"))

            @block.scalar
            def _(act):
                act.wait_ge(const_loaded.sem, const_loaded.at(0, "gate"))
                nc.scalar.activation(gate[:, 1:2], gate[:, 0:1], ACT.Tanh).then_inc(*tanh_ready.rise("gate"))
        finish(1)

        for index, L in enumerate(LAYERS):
            name = L.name + "_xattn_"
            H, HD, KV, KT, U = L.heads, L.head, L.kv_heads, L.key_tiles, L.unit
            kc = KV * HD
            k_rows, k_tiles = min(kc, 128), -(-kc // 128)

            place, first = {}, 0
            for key, tiles, width in [("q", DT, D), ("k", DT, kc), ("v", DT, kc), ("o", DT, D)] + (
                    [("f", DT, INNER), ("m", FT, D)] if L.mlp else []):
                place[key] = (first, tiles, width)
                first += tiles * width

            def weight(t, key):
                start, tiles, width = place[key]
                return t[:, start:start + tiles * width].rearrange("p (k n) -> p k n", k=tiles)

            def both(key):
                return weight(whi, key), weight(wlo, key)

            matrices = {
                "L0": dict(q="q_w", k="k_w", v="v_w", o="cproj_w", f="fc_w", m="proj_w"),
                "L1": dict(q="Wq", k="Wk", v="Wv", o="Wo"),
                "L2": dict(q="q_w", kv="kv_w", o="out_w", f="mlp_w1", m="mlp_w2"),
                "L3": dict(q="Wq", k="Wk", v="Wv", o="Wo"),
            }[L.name]
            vectors = {
                "L0": dict(q="q_b", k="k_b", v="v_b", o="cproj_b", w1="ln1_w", b1="ln1_b", w2="ln2_w",
                           b2="ln2_b", f="fc_b", m="proj_b"),
                "L1": dict(q="bq", k="bk", v="bv", o="bo", gamma="gamma", beta="beta"),
                "L2": dict(q="q_b", kv="kv_b", o="out_b", w2="postnorm_w", f="mlp_b1", m="mlp_b2"),
                "L3": dict(w1="ln_gamma", b1="ln_beta"),
            }[L.name]

            chunks = []
            for key, w in matrices.items():
                tall, broad = ins[name + w].shape
                for tile in range(tall // 128):
                    for c0 in range(0, broad, 512):
                        chunks.append((key, tile, c0, min(512, broad - c0)))

            def by_dimension(ap, heads):
                return ap.rearrange("p (d h) -> p h d", h=heads)

            def by_head(ap):
                return ap.rearrange("p (h d) -> p h d", d=HD)

            def homes(t, raw, key, tile, c0, width):
                if key == "kv":
                    two = raw.rearrange("p (h d e) -> p h d e", d=HD, e=2)
                    return [(two[:, :, :, 0], by_dimension(weight(t, "k")[:, tile, :], KV)),
                            (two[:, :, :, 1], by_head(weight(t, "v")[:, tile, :]))]
                if key in ("q", "k"):
                    return [(by_head(raw), by_dimension(weight(t, key)[:, tile, :], H if key == "q" else KV))]
                return [(raw, weight(t, key)[:, tile, c0:c0 + width])]

            def turned_homes(t, bank, key, tile):
                found = []
                for into in range(DT):
                    raw = bank[:, 128 * into:128 * into + 128]
                    if key in ("q", "k"):
                        n_heads = 128 // HD
                        home = by_dimension(weight(t, key)[:, into, :], H)
                        found.append((by_head(raw), home[:, n_heads * tile:n_heads * (tile + 1), :]))
                    else:
                        found.append((raw, weight(t, key)[:, into, 128 * tile:128 * tile + 128]))
                return found

            loads = []
            if "q" in vectors:
                q_bias = ins[name + vectors["q"]].rearrange("(h d) -> d h", d=HD)
                per = 128 // H
                for t in range(DT):
                    loads.append((cols[:, Q_COL + t:Q_COL + t + 1], q_bias[per * t:per * t + per, :].unsqueeze(2)))
                if "kv" in vectors:
                    k_bias = ins[name + "kv_b"].rearrange("(h d e) -> e d h", d=HD, e=2)[0]
                    loads.append((t32[0][:].rearrange("p a b -> p (a b)"), ins[name + "kv_b"].partition_broadcast(128)))
                else:
                    k_bias = ins[name + vectors["k"]].rearrange("(h d) -> d h", d=HD)
                    loads.append((rows[:, V_BIAS, 0:kc], ins[name + vectors["v"]].partition_broadcast(128)))
                per = k_rows // KV
                for t in range(k_tiles):
                    loads.append((cols[0:k_rows, K_COL + t:K_COL + t + 1],
                                  k_bias[per * t:per * t + per, :].unsqueeze(2)))
            for key, row in (("o", O_BIAS), ("m", M_BIAS), ("gamma", GAMMA), ("beta", BETA)):
                if key in vectors:
                    loads.append((rows[:, row, :], ins[name + vectors[key]].partition_broadcast(128)))
            for key, col in (("w1", W1_COL), ("b1", B1_COL), ("w2", W2_COL), ("b2", B2_COL), ("f", F_COL)):
                if key in vectors:
                    v = ins[name + vectors[key]].rearrange("(c p) -> p c", p=128)
                    loads.append((cols[:, col:col + v.shape[1]], v))

            q_stack = [arena[s][:, 0:H * GT].rearrange("p (h t) -> p h t", t=GT) for s in range(S)]
            k_stack = [arena[s][:, H * GT:(H + KT * KV) * GT].rearrange("p (k h t) -> p k h t", k=KT, t=GT)
                       for s in range(S)]
            value = [values[s][:, 0:G * KT * KV * 32].rearrange("p (g h e) -> p g h e", g=G * KT, e=32)
                     for s in range(S)]

            for i in range(4):
                raw_loaded[i].plan(range((len(chunks) - i + 3) // 4))
            raw_split.plan(range(len(chunks)))
            if L.name == "L3":
                raw_turned.plan(range(len(chunks)))
            vectors_loaded.plan(range(len(loads)))
            if "q" in vectors:
                vectors_ready.plan(["q"] + (["v"] if "kv" in vectors else []))
            stacks_clear.plan([(s, k) for s in range(S) for k in (
                ("all", "values") if L.float_mask else ("all", "values", "one")) + ("sum",)])
            with nc.Block() as block:
                @block.sync
                def _(sp):
                    for i, (key, tile, c0, width) in enumerate(chunks):
                        if i >= 4:
                            sp.wait_ge(raw_split.sem, raw_split.at(0, i - 4))
                        sp.dma_start(probs[:, i % 4, 0:width],
                                     ins[name + matrices[key]][128 * tile:128 * tile + 128, c0:c0 + width]).then_inc(
                            *raw_loaded[i % 4].rise(i // 4))

                @block.scalar
                def _(act):
                    for i, (to, of) in enumerate(loads):
                        with nc.allow_non_contiguous_dma(reason="a few hundred elements, once in a layer"):
                            act.dma_start(to, of).then_inc(*vectors_loaded.rise(i))
                    act.wait_ge(vectors_loaded.sem, vectors_loaded.at(0, len(loads) - 1))

                @block.gpsimd
                def _(pool):
                    for s in range(S):
                        nc.gpsimd.memset(f32(arena[s][:]), 0.0).then_inc(*stacks_clear.rise((s, "all")))
                        nc.gpsimd.memset(values[s][:], 0.0).then_inc(*stacks_clear.rise((s, "values")))
                        pool.wait_ge(stacks_clear.sem, stacks_clear.at(0, (s, "values")))
                        if not L.float_mask:
                            nc.gpsimd.memset(q_stack[s][PR:PR + 1, :, :], 1.0).then_inc(
                                *stacks_clear.rise((s, "one")))
                            pool.wait_ge(stacks_clear.sem, stacks_clear.at(0, (s, "one")))
                        nc.gpsimd.memset(value[s][:, :, :, HD:HD + 1], 1.0).then_inc(
                            *stacks_clear.rise((s, "sum")))

                @block.tensor
                def _(pe):
                    if L.name == "L3":
                        for i, (key, tile, c0, width) in enumerate(chunks):
                            pe.wait_ge(raw_loaded[i % 4].sem, raw_loaded[i % 4].at(0, i // 4))
                            if i >= 2:
                                pe.wait_ge(raw_split.sem, raw_split.at(0, i - 2))
                            for into in range(DT):
                                last = nc.tensor.transpose(ps_d[i % 2][:, 128 * into:128 * into + 128],
                                                           probs[:, i % 4, 128 * into:128 * into + 128], ident[:])
                            last.then_inc(*raw_turned.rise(i))

                @block.vector
                def _(dve):
                    for i, (key, tile, c0, width) in enumerate(chunks):
                        if L.name == "L3":
                            dve.wait_ge(raw_turned.sem, raw_turned.at(0, i))
                            hi_homes = turned_homes(whi, ps_d[i % 2], key, tile)
                            lo_homes = turned_homes(wlo, ps_d[i % 2], key, tile)
                        else:
                            dve.wait_ge(raw_loaded[i % 4].sem, raw_loaded[i % 4].at(0, i // 4))
                            raw = probs[:, i % 4, 0:width]
                            hi_homes = homes(whi, raw, key, tile, c0, width)
                            lo_homes = homes(wlo, raw, key, tile, c0, width)
                        for of, to in hi_homes:
                            nc.vector.tensor_copy(to, of).then_inc(*step.tick())
                        dve.wait_ge(step.sem, step.now())
                        for (of, hi), (_, lo) in zip(hi_homes[:-1], lo_homes[:-1]):
                            nc.vector.tensor_tensor(out=lo, in0=of, in1=f32(hi), op=ALU.subtract).then_inc(
                                *step.tick())
                        of, lo = lo_homes[-1]
                        nc.vector.tensor_tensor(out=lo, in0=of, in1=f32(hi_homes[-1][1]), op=ALU.subtract).then_inc(
                            *raw_split.rise(i))
                    if "q" in vectors:
                        dve.wait_ge(vectors_loaded.sem, vectors_loaded.at(0, len(loads) - 1))
                        nc.vector.tensor_scalar(cols[:, Q_COL:Q_COL + DT], cols[:, Q_COL:Q_COL + DT], L.scale, None,
                                                ALU.mult).then_inc(*vectors_ready.rise("q"))
                        if "kv" in vectors:
                            nc.vector.tensor_copy(
                                rows[:, V_BIAS, :],
                                t32[0][:].rearrange("p a b -> p (a b)").rearrange("p (n e) -> p n e", e=2)[:, :, 1]
                            ).then_inc(*vectors_ready.rise("v"))
            finish(1)

            N = len(L.units)
            last_unit = [N // 2 - 1, N - 1]
            chunks_f = range(FT // 2)
            turned = [(k, s) for s in range(S) for k in (("TX",) if L.load_ct else ("TX", "TC"))]
            projected = [("Q", s) if k is None else ("K", s, k) for s in range(S) for k in (None, *range(KT))]
            first_half = len(projected) // 2
            outputs = [("V", s, k) for s in range(S) for k in range(KT)]
            att_uses, mixed = [], []
            for n in range(N + 1):
                att_uses += [("MT", n)] if n < N else []
                att_uses += [("PV", n - 1), ("OT", n - 1)] if n else []
            mixed += turned + [("TO", s) for s in range(S)] + projected[:first_half]
            mixed += [("O", s) for s in range(S)] + projected[first_half:]
            mixed += [("TL", s) for s in range(S)] if L.mlp else []
            mixed += outputs
            mixed += [("F", s, c) for s in range(S) for c in chunks_f] if L.mlp else []
            phase_of = {key: "att" for key in att_uses}
            phase_of.update({key: "post" if key[0] in ("TO", "O", "TL", "F") else "prep" for key in mixed})
            body_uses = att_uses + mixed
            bank_of = {key: i % 2 for i, key in enumerate(body_uses)}
            halves = [(n, f) for n in range(N) for f in range(2)]
            k_loads = [(k, i) for k in range(KT) for i in range(3)] + ([] if L.float_mask else ["bias"])
            turned_post = [("TO", s) for s in range(S)] + ([("TL", s) for s in range(S)] if L.mlp else [])
            normed = {"prep": range(S) if L.ln_x or L.ln_c else (), "post": range(S) if L.name != "L3" else ()}

            for phase in PHASES:
                keys = [u for u in body_uses if phase_of[u] == phase]
                d_full[phase].plan(keys)
                for i in range(2):
                    d_out[phase][i].plan([u for u in keys if bank_of[u] == i])
            for phase, keys in (("prep", turned), ("post", turned_post)):
                hi_ready[phase].plan(keys)
                lo_ready[phase].plan(keys)
                for g in (spread_ready, rstd_ready, norm_ready):
                    g[phase].plan(normed[phase])
            parts_ready.plan(projected)
            for key in projected:
                written[key].plan(["parts"])
            a_full.plan(range(N))
            a_out.plan(list(range(N)) + ([("M", s) for s in range(S)] if L.mlp else []))
            m_ready.plan(range(N))
            b_full.plan(halves)
            b_out.plan(halves)
            if L.name != "L3":
                y_ready.plan(range(S))
            if L.mlp:
                for g in (hid_hi_ready, hid_lo_ready, hid_used):
                    g.plan([(s, c) for s in range(S) for c in chunks_f])
            if L.float_mask:
                mask_hi_ready.plan(range(S))
                mask_lo_ready.plan(range(S))
                scaled.plan(range(S))
            for s in range(S):
                x_loaded[s].plan(["x"])
                residual_loaded[s].plan(["x"])
                c_loaded[s].plan(["hi", "lo", "mask"] if L.float_mask else ["hi", "lo"] if L.load_ct else ["c"])
                if L.store_ct:
                    ct_stored[s].plan(["hi", "lo"])
                q_stacked[s].plan(range(3))
                k_stacked[s].plan(k_loads)
                y_stored[s].plan(["y"])

            def bank(key):
                return ps_d[bank_of[key]]

            def filled(key):
                return d_full[phase_of[key]]

            def out_of(key):
                return d_out[phase_of[key]][bank_of[key]]

            src, dst = x_dram[index], x_dram[index + 1]
            y_tile = norm if L.float_mask else heads_out

            def tok_rows(dram_ap, it, s):
                return dram_ap[bass.ds(it * (G * S) + s * G, G), :, :].rearrange("b t d -> t b d")

            def passes(engine, body):
                body(-1, prep=True, rest=False)
                with engine.Fori(0, PASSES - 1) as p:
                    body(p, prep=True, rest=True)
                body(PASSES - 1, prep=False, rest=True)

            with nc.Block() as block:
                @block.sync
                def _(sp):
                    def body(p, prep, rest):
                        it = p + 1
                        for s in range(S):
                            if prep:
                                sp.wait_ge(d_full["prep"].sem, d_full["prep"].prev(it, ("TX", s)))
                                sp.dma_start(x_in[s][:], tok_rows(src, it, s)).then_inc(*x_loaded[s].rise("x"))
                            if prep and L.load_ct:
                                sp.wait_ge(d_full["prep"].sem, d_full["prep"].prev(it, ("V", s, 0)))
                                sp.dma_start(f32(c_hi[s][:]).rearrange("p k t -> p (k t)"),
                                             ct_dram[bass.ds(it, 1), s, 0, :, :].rearrange("i p n -> (i p) n")).then_inc(
                                    *c_loaded[s].rise("hi"))
                                sp.dma_start(f32(c_lo[s][:]).rearrange("p k t -> p (k t)"),
                                             ct_dram[bass.ds(it, 1), s, 1, :, :].rearrange("i p n -> (i p) n")).then_inc(
                                    *c_loaded[s].rise("lo"))
                                if L.float_mask:
                                    sp.wait_ge(mask_lo_ready.sem, mask_lo_ready.prev(it, s))
                                    sp.dma_start(
                                        c_tok[s][:, :, 0:T],
                                        ins["mask_Bx1xSxS2_ff0"].rearrange("b o q k -> b (o q) k")[
                                            bass.ds(it * (G * S) + s * G, G), :, :].rearrange("b q k -> q b k")
                                    ).then_inc(*c_loaded[s].rise("mask"))
                            elif prep:
                                sp.wait_ge(d_full["prep"].sem, d_full["prep"].prev(it, ("TC", s)))
                                sp.dma_start(c_tok[s][:], tok_rows(ins["ctx_2048"], it, s)).then_inc(
                                    *c_loaded[s].rise("c"))
                        for s in range(S):
                            if rest:
                                if L.name == "L2":
                                    sp.wait_ge(a_out.sem, a_out.prev(p, ("M", s)))
                                else:
                                    sp.wait_ge(out_of(("O", s)).sem, out_of(("O", s)).prev(p, ("O", s)))
                                sp.dma_start(x_tok[s][:], tok_rows(src, p, s)).then_inc(*residual_loaded[s].rise("x"))
                        for s in range(S if prep else 0):
                            sp.wait_ge(parts_ready.sem, parts_ready.at(it, ("Q", s)))
                            i = projected.index(("Q", s)) % 2
                            sp.dma_start(q_dram[s].rearrange("(n r k) -> r n k", r=128, k=GT),
                                         parts[i][:].rearrange("r p t k -> r (p t) k")).then_inc(
                                *written["Q", s].rise("parts"))
                            for k in range(KT):
                                sp.wait_ge(parts_ready.sem, parts_ready.at(it, ("K", s, k)))
                                i = projected.index(("K", s, k)) % 2
                                n = 3 * k_tiles
                                of = parts[i][:].rearrange("r p t k -> r (p t) k") if k_tiles == DT else \
                                    parts[i][0:k_rows, :, 0, :]
                                sp.dma_start(k_dram[s][k][0:n * k_rows * GT].rearrange("(n r k) -> r n k", r=k_rows, k=GT),
                                             of).then_inc(*written["K", s, k].rise("parts"))
                            sp.wait_ge(b_full.sem, b_full.prev(it, (last_unit[s], 1)))
                            sp.wait_ge(written["Q", s].sem, written["Q", s].at(it, "parts"))
                            part = HD * H * GT
                            for i, (p0, slot, n, rep) in enumerate(Q_SLOTS):
                                sp.dma_start(q_stack[s][slot * HD:(slot + n) * HD, :, :],
                                             q_dram[s][p0 * part:(p0 + n) * part].rearrange(
                                                 "(r h k) -> r h k", h=H, k=GT)).then_inc(*q_stacked[s].rise(i))
                            part = HD * KV * GT
                            for k in range(KT):
                                sp.wait_ge(written["K", s, k].sem, written["K", s, k].at(it, "parts"))
                                for i, (p0, slot, n, rep) in enumerate(K_SLOTS):
                                    of = k_dram[s][k][p0 * part:(p0 + 1) * part]
                                    of = of.rearrange("(o r n) -> o r n", o=1, r=HD).broadcast_to([rep, HD, KV * GT])
                                    sp.dma_start(
                                        k_stack[s][slot * HD:(slot + rep) * HD, k, :, :].rearrange("p h t -> p (h t)"),
                                        of).then_inc(*k_stacked[s].rise((k, i)))
                            if not L.float_mask:
                                row = bias_dram[1 if KT == 2 else 0, bass.ds((it * (G * S) + s * G) * T, GT)]
                                sp.dma_start(k_stack[s][PR:PR + 1, 0, :, :],
                                             row.rearrange("(o h t) -> o h t", o=1, h=1).broadcast_to([1, KV, GT])
                                             ).then_inc(*k_stacked[s].rise("bias"))
                            if L.store_ct:
                                sp.wait_ge(lo_ready["prep"].sem, lo_ready["prep"].at(it, ("TC", s)))
                                for i, t in enumerate((c_hi[s], c_lo[s])):
                                    sp.dma_start(ct_dram[bass.ds(it, 1), s, i, :, :].rearrange("i p n -> (i p) n"),
                                                 f32(t[:]).rearrange("p k t -> p (k t)")).then_inc(
                                        *ct_stored[s].rise(("hi", "lo")[i]))
                        for s in range(S if rest else 0):
                            g, key = (out_of(("O", s)), ("O", s)) if L.name == "L3" else (y_ready, s)
                            sp.wait_ge(g.sem, g.at(p, key))
                            sp.dma_start(tok_rows(dst, p, s), y_tile[s][:]).then_inc(*y_stored[s].rise("y"))

                    passes(sp, body)
                    for s in range(S):
                        sp.wait_ge(y_stored[s].sem, y_stored[s].at(PASSES - 1, "y"))
                        if L.store_ct:
                            sp.wait_ge(ct_stored[s].sem, ct_stored[s].at(PASSES - 1, "lo"))

                @block.tensor
                def _(pe):
                    def split_product(dst_ap, lhs, rhs, start=True, stop=True):
                        n = len(lhs)
                        for i, (a, b) in enumerate(zip(lhs, rhs)):
                            for j, (x, w) in enumerate(((a[0], b[0]), (a[0], b[1]), (a[1], b[0]))):
                                last = nc.tensor.matmul(dst_ap, x, w, start=start and i == 0 and j == 0,
                                                        stop=stop and i == n - 1 and j == 2)
                        return last

                    def body(p, prep, rest):
                        it = p + 1
                        order = [u for u in body_uses if (prep if phase_of[u] == "prep" else rest)]

                        def pass_of(key):
                            return it if phase_of[key] == "prep" else p

                        def take(key):
                            before = [u for u in order[:order.index(key)] if bank_of[u] == bank_of[key]]
                            if before:
                                u = before[-1]
                                pe.wait_ge(out_of(u).sem, out_of(u).at(pass_of(u), u))
                            elif rest:
                                for phase in ("post", "prep"):
                                    u = [u for u in body_uses if bank_of[u] == bank_of[key] and phase_of[u] == phase]
                                    if u:
                                        g = out_of(u[-1])
                                        pe.wait_ge(g.sem, g.prev(p, u[-1]) if phase == "post" else g.at(p, u[-1]))
                            return bank(key)

                        def turn(key, source):
                            d = take(key)
                            for kt in range(DT):
                                for b in range(G):
                                    last = nc.tensor.transpose(d[:, kt * GT + b * T:kt * GT + b * T + T],
                                                               source[:, b, 128 * kt:128 * kt + 128], ident[:])
                            last.then_inc(*filled(key).rise(key))

                        def turn_inputs():
                            for key in turned:
                                s = key[1]
                                ready, loaded = norm_ready["prep"], (x_loaded if key[0] == "TX" else c_loaded)[s]
                                if L.ln_x if key[0] == "TX" else L.ln_c:
                                    pe.wait_ge(ready.sem, ready.at(it, s))
                                else:
                                    pe.wait_ge(loaded.sem, loaded.at(it, loaded.keys[-1]))
                                turn(key, x_in[s] if key[0] == "TX" else c_tok[s])

                        def transposed_projection(key, w, source, tiles, rows_n):
                            d = take(key)
                            hi, lo = both(w)
                            for t in range(tiles):
                                cut = slice(rows_n * t, rows_n * t + rows_n)
                                last = split_product(
                                    d[0:rows_n, t * GT:t * GT + GT],
                                    [(hi[:, kt, cut], lo[:, kt, cut]) for kt in range(DT)],
                                    [(source[0][:, kt, :], source[1][:, kt, :]) for kt in range(DT)])
                            last.then_inc(*filled(key).rise(key))

                        def projection(key, w, source, width):
                            d = take(key)
                            hi, lo = both(w)
                            for b in range(G):
                                cut = slice(b * T, b * T + T)
                                last = split_product(
                                    d[:, b * width:(b + 1) * width],
                                    [(source[0][:, kt, cut], source[1][:, kt, cut]) for kt in range(DT)],
                                    [(hi[:, kt, :], lo[:, kt, :]) for kt in range(DT)])
                            last.then_inc(*filled(key).rise(key))

                        xs = [(x_hi[s], x_lo[s]) for s in range(S)]
                        cs = [(c_hi[s], c_lo[s]) for s in range(S)]
                        ps = [(p_hi[s], p_lo[s]) for s in range(S)]

                        def queries_and_keys(s):
                            lo = lo_ready["prep"]
                            pe.wait_ge(lo.sem, lo.at(it, ("TX", s)))
                            transposed_projection(("Q", s), "q", xs[s], DT, 128)
                            if L.load_ct:
                                pe.wait_ge(c_loaded[s].sem, c_loaded[s].at(it, c_loaded[s].keys[-1]))
                            else:
                                pe.wait_ge(lo.sem, lo.at(it, ("TC", s)))
                            for k in range(KT):
                                transposed_projection(("K", s, k), "k", (cs, xs)[k][s], k_tiles, k_rows)

                        def scores_for_maxima(n):
                            s, b, h0 = L.units[n]
                            if n % (N // 2) == 0:
                                pe.wait_ge(q_stacked[s].sem, q_stacked[s].at(p, 2))
                                pe.wait_ge(k_stacked[s].sem, k_stacked[s].at(p, k_loads[-1]))
                                if L.float_mask:
                                    pe.wait_ge(mask_lo_ready.sem, mask_lo_ready.at(p, s))
                            pe.wait_ge(a_out.sem, a_out.back(p, n, 2))
                            a = ps_a[n % 2]
                            cut = slice(b * T, b * T + T)
                            for i in range(U):
                                if L.float_mask and i % 4 == 0:
                                    for j, m in enumerate((hid_hi[s], hid_lo[s])):
                                        nc.tensor.matmul(a[:, i * T:(i + 4) * T], ident_r[:],
                                                         repeat(m[:].rearrange("p a b -> p (a b)")[:, cut], 4),
                                                         start=j == 0, stop=False, skip_group_check=True)
                                last = nc.tensor.matmul(
                                    a[:, i * KT * T:(i + 1) * KT * T], q_stack[s][:, h0 + i, cut],
                                    k_stack[s][:, :, (h0 + i) // L.group, cut] if KT == 2 else
                                    k_stack[s][:, 0, (h0 + i) // L.group, cut],
                                    start=not L.float_mask, stop=True, skip_group_check=L.float_mask)
                            last.then_inc(*a_full.rise(n))

                        def turn_maxima(n):
                            pe.wait_ge(m_ready.sem, m_ready.at(p, n))
                            d = take(("MT", n))
                            nc.tensor.transpose(d[:, 0:64].bitcast(BF16), m_parts[:, n % 2, :], ident_b[:]).then_inc(
                                *filled(("MT", n)).rise(("MT", n)))

                        def scores_less_maxima(n):
                            s, b, h0 = L.units[n]
                            pe.wait_ge(out_of(("MT", n)).sem, out_of(("MT", n)).at(p, ("MT", n)))
                            cut = slice(b * T, b * T + T)
                            for f in range(2):
                                pe.wait_ge(b_out.sem, b_out.back(p, (n, f), 2))
                                d = ps_b[f]
                                if L.float_mask:
                                    for j, m in enumerate((hid_hi[s], hid_lo[s])):
                                        nc.tensor.matmul(d[:], m[:].rearrange("p a b -> p (a b)")[:, cut],
                                                         repeat(ident_r[:], 4), start=j == 0, stop=False,
                                                         skip_group_check=True)
                                for j in range(4):
                                    i, k = (j, f) if KT == 2 else (4 * f + j, 0)
                                    to = d[:, j * T:(j + 1) * T]
                                    nc.tensor.matmul(to, k_stack[s][:, k, (h0 + i) // L.group, cut],
                                                     q_stack[s][:, h0 + i, cut], start=not L.float_mask, stop=False,
                                                     skip_group_check=L.float_mask)
                                    last = nc.tensor.matmul(to, select[:, i, :], m_rows[:, n % 2, :], start=False,
                                                            stop=True, skip_group_check=L.float_mask)
                                last.then_inc(*b_full.rise((n, f)))

                        def weighted_values(n):
                            s, b, h0 = L.units[n]
                            if n % (N // 2) == 0:
                                for k in range(KT):
                                    v = out_of(("V", s, k))
                                    pe.wait_ge(v.sem, v.at(p, ("V", s, k)))
                            pe.wait_ge(b_out.sem, b_out.at(p, (n, 1)))
                            d = take(("PV", n))
                            for k in range(KT):
                                for i in range(U):
                                    half, j = (k, i) if KT == 2 else (i // 4, i % 4)
                                    e = probs[:, (2 * n + half) % 4, j * T:(j + 1) * T]
                                    last = nc.tensor.matmul(
                                        d[32 * (i % 4):32 * (i % 4) + 32, (i // 4) * T:(i // 4) * T + T],
                                        value[s][:, b * KT + k, (h0 + i) // L.group, :], e, start=k == 0,
                                        stop=k == KT - 1)
                            last.then_inc(*filled(("PV", n)).rise(("PV", n)))

                        def turn_outputs(n):
                            pv = out_of(("PV", n))
                            pe.wait_ge(pv.sem, pv.at(p, ("PV", n)))
                            d = take(("OT", n))
                            for i in range(U // 4):
                                last = nc.tensor.transpose(d[:, i * T:(i + 1) * T], o_t[:, i * T:(i + 1) * T], ident[:])
                            last.then_inc(*filled(("OT", n)).rise(("OT", n)))

                        if rest:
                            scores_for_maxima(0)
                            scores_for_maxima(1)
                            for n in range(N + 1):
                                if n < N:
                                    turn_maxima(n)
                                if n + 2 < N:
                                    scores_for_maxima(n + 2)
                                if n:
                                    weighted_values(n - 1)
                                if n < N:
                                    scores_less_maxima(n)
                                if n:
                                    turn_outputs(n - 1)

                        if prep:
                            turn_inputs()
                        if rest:
                            for s in range(S):
                                ot = ("OT", last_unit[s])
                                pe.wait_ge(out_of(ot).sem, out_of(ot).at(p, ot))
                                turn(("TO", s), heads_out[s])
                        if prep:
                            queries_and_keys(0)
                        if rest:
                            for s in range(S):
                                pe.wait_ge(lo_ready["post"].sem, lo_ready["post"].at(p, ("TO", s)))
                                projection(("O", s), "o", ps[s], D)
                        if prep:
                            queries_and_keys(1)
                        if rest and L.mlp:
                            for s in range(S):
                                pe.wait_ge(norm_ready["post"].sem, norm_ready["post"].at(p, s))
                                turn(("TL", s), norm[s])
                        if prep:
                            for key in outputs:
                                projection(key, "v", (cs, xs)[key[2]][key[1]], kc)

                        if rest and L.mlp:
                            f_hi, f_lo = both("f")
                            g_hi, g_lo = both("m")

                            def hidden(s, c):
                                d = take(("F", s, c))
                                for j in range(2):
                                    cut = slice((2 * c + j) * 128, (2 * c + j) * 128 + 128)
                                    last = split_product(
                                        d[:, j * GT:(j + 1) * GT],
                                        [(f_hi[:, kt, cut], f_lo[:, kt, cut]) for kt in range(DT)],
                                        [(p_hi[s][:, kt, :], p_lo[s][:, kt, :]) for kt in range(DT)])
                                last.then_inc(*filled(("F", s, c)).rise(("F", s, c)))

                            def mlp_out(s, c):
                                pe.wait_ge(hid_lo_ready.sem, hid_lo_ready.at(p, (s, c)))
                                if c == 0:
                                    pe.wait_ge(a_out.sem, a_out.back(p, ("M", s), 2))
                                hi, lo = hid_hi[c % 2], hid_lo[c % 2]
                                for b in range(G):
                                    cut = slice(b * T, b * T + T)
                                    last = split_product(
                                        ps_a[s][:, 512 * b:512 * b + D],
                                        [(hi[:, j, cut], lo[:, j, cut]) for j in range(2)],
                                        [(g_hi[:, 2 * c + j, :], g_lo[:, 2 * c + j, :]) for j in range(2)],
                                        start=c == 0, stop=c == FT // 2 - 1)
                                last.then_inc(*hid_used.rise((s, c)))

                            all_chunks = [(s, c) for s in range(S) for c in chunks_f]
                            for i, (s, c) in enumerate(all_chunks):
                                if c == 0:
                                    pe.wait_ge(lo_ready["post"].sem, lo_ready["post"].at(p, ("TL", s)))
                                hidden(s, c)
                                if i:
                                    mlp_out(*all_chunks[i - 1])
                            mlp_out(*all_chunks[-1])

                    passes(pe, body)

                @block.scalar
                def _(act):
                    def body(p, prep, rest):
                        it = p + 1

                        def full(key):
                            act.wait_ge(filled(key).sem, filled(key).at(it if phase_of[key] == "prep" else p, key))
                            return bank(key)

                        def turned_out(key, to, w_col=None, b_col=None):
                            d = full(key)
                            if w_col is None:
                                nc.scalar.activation(to[:].rearrange("p a b -> p (a b)"), d[:],
                                                     ACT.Copy).then_inc(*out_of(key).rise(key))
                                return
                            for kt in range(DT):
                                last = nc.scalar.activation(
                                    to[:, kt, :], d[:, kt * GT:kt * GT + GT], ACT.Identity,
                                    scale=cols[:, w_col + kt:w_col + kt + 1],
                                    bias=cols[:, b_col + kt:b_col + kt + 1] if b_col is not None else 0.0)
                            last.then_inc(*out_of(key).rise(key))

                        def projected_out(key):
                            i = projected.index(key)
                            d = full(key)
                            act.wait_ge(parts_ready.sem, parts_ready.back(it, key, 2))
                            is_q = key[0] == "Q"
                            rows_n, tiles = (128, DT) if is_q else (k_rows, k_tiles)
                            for t in range(tiles):
                                col = (Q_COL if is_q else K_COL) + t
                                last = nc.scalar.activation(
                                    qk32[i % 2][0:rows_n, t, :], d[0:rows_n, t * GT:t * GT + GT], ACT.Identity,
                                    scale=L.scale if is_q else 1.0,
                                    bias=cols[0:rows_n, col:col + 1] if "q" in vectors else 0.0)
                            last.then_inc(*out_of(key).rise(key))

                        for n in range(N + 1 if rest else 0):
                            if n < N:
                                d = full(("MT", n))
                                nc.scalar.activation(m_rows[:, n % 2, :], d[:, 0:64].bitcast(BF16), ACT.Copy).then_inc(
                                    *out_of(("MT", n)).rise(("MT", n)))
                            if n:
                                d = full(("PV", n - 1))
                                ot = d_full["att"]
                                act.wait_ge(ot.sem, ot.prev(p, ("OT", N - 1)) if n == 1 else ot.at(p, ("OT", n - 2)))
                                nc.scalar.activation(o_t[:, 0:U * 32], d[:, 0:U * 32], ACT.Copy).then_inc(
                                    *out_of(("PV", n - 1)).rise(("PV", n - 1)))
                            if n < N:
                                for f in range(2):
                                    act.wait_ge(b_full.sem, b_full.at(p, (n, f)))
                                    nc.scalar.activation(probs[:, (2 * n + f) % 4, :], ps_b[f][:], ACT.Exp).then_inc(
                                        *b_out.rise((n, f)))

                        if prep:
                            for i, key in enumerate(turned):
                                lo = lo_ready["prep"]
                                act.wait_ge(lo.sem, lo.back(it, key, 2))
                                norm_cols = (W1_COL, B1_COL) if (L.ln_x if key[0] == "TX" else L.ln_c) else ()
                                turned_out(key, t32[i % 2], *norm_cols)
                        if rest:
                            for s in range(S):
                                if L.mlp:
                                    act.wait_ge(hid_lo_ready.sem, hid_lo_ready.prev(p, (S - 1, FT // 2 - 2 + s)))
                                else:
                                    act.wait_ge(lo_ready["post"].sem, lo_ready["post"].prev(p, ("TO", s)))
                                turned_out(("TO", s), hid32[s])
                        if prep:
                            for key in projected:
                                projected_out(key)
                        if rest and L.mlp:
                            for s in range(S):
                                act.wait_ge(lo_ready["post"].sem, lo_ready["post"].at(p, ("TO", s)))
                                turned_out(("TL", s), hid32[s], W2_COL, B2_COL if "b2" in vectors else None)
                            for s in range(S):
                                for c in chunks_f:
                                    d = full(("F", s, c))
                                    if (s, c) in ((0, 0), (0, 1)):
                                        act.wait_ge(lo_ready["post"].sem, lo_ready["post"].at(p, ("TL", c)))
                                    else:
                                        act.wait_ge(hid_lo_ready.sem, hid_lo_ready.back(p, (s, c), 2))
                                    for j in range(2):
                                        col = F_COL + 2 * c + j
                                        last = nc.scalar.activation(hid32[c % 2][:, j, :], d[:, j * GT:(j + 1) * GT],
                                                                    ACT.Gelu_apprx_tanh, bias=cols[:, col:col + 1])
                                    last.then_inc(*out_of(("F", s, c)).rise(("F", s, c)))

                    passes(act, body)

                @block.vector
                def _(dve):
                    def body(p, prep, rest):
                        it = p + 1

                        def full(key):
                            dve.wait_ge(filled(key).sem, filled(key).at(it if phase_of[key] == "prep" else p, key))
                            return bank(key)

                        def in_sbuf(key):
                            dve.wait_ge(out_of(key).sem, out_of(key).at(it if phase_of[key] == "prep" else p, key))

                        def here():
                            dve.wait_ge(step.sem, step.now())

                        def norm_stats(phase, s, source):
                            for b in range(G):
                                nc.vector.bn_stats(out=stats[:, s, b, :], in_=source[:, b, :]).then_inc(*step.tick())
                            here()
                            nc.vector.tensor_copy(spare[:], minus_half[:, 0:1])
                            for b in range(G):
                                nc.vector.bn_aggr(out=moments[:, s, b, :], in_=stats[:, s, b, :]).then_inc(*step.tick())
                            here()
                            if L.name == "L2":
                                nc.vector.tensor_tensor(out=spread[:, s, :], in0=moments[:, s, :, 0],
                                                        in1=moments[:, s, :, 0], op=ALU.mult).then_inc(*step.tick())
                                here()
                                nc.vector.scalar_tensor_tensor(
                                    out=spread[:, s, :], in0=moments[:, s, :, 1], scalar=L.eps, in1=spread[:, s, :],
                                    op0=ALU.add, op1=ALU.add).then_inc(*spread_ready[phase].rise(s))
                            else:
                                nc.vector.tensor_scalar(spread[:, s, :], moments[:, s, :, 1], L.eps, None,
                                                        ALU.add).then_inc(*spread_ready[phase].rise(s))

                        def normalise(phase, s, source, to):
                            g = rstd_ready[phase]
                            dve.wait_ge(g.sem, g.at(it if phase == "prep" else p, s))
                            for b in range(G):
                                if L.name == "L2":
                                    last = nc.vector.tensor_scalar(to[:, b, :], source[:, b, :],
                                                                   rstd[:, s, b:b + 1], None, ALU.mult)
                                else:
                                    last = nc.vector.tensor_scalar(to[:, b, :], source[:, b, :],
                                                                   moments[:, s, b, 0:1], rstd[:, s, b:b + 1],
                                                                   ALU.subtract, ALU.mult)
                            last.then_inc(*norm_ready[phase].rise(s))

                        def hi_half(key, to, of):
                            in_sbuf(key)
                            if key[0] == "TC" and L.store_ct:
                                g = ct_stored[key[1]]
                                dve.wait_ge(g.sem, g.prev(it, "lo"))
                            nc.vector.tensor_copy(to[:], of[:]).then_inc(*hi_ready[phase_of[key]].rise(key))

                        def three_parts(n):
                            key = projected[n]
                            in_sbuf(key)
                            g = written[projected[n - 2]]
                            dve.wait_ge(g.sem, g.at(it, "parts") if n >= 2 else g.prev(it, "parts"))
                            rows_n, tiles = (128, DT) if key[0] == "Q" else (k_rows, k_tiles)
                            rest_of = qk32[n % 2][0:rows_n, 0:tiles, :]
                            part = [parts[n % 2][0:rows_n, i, 0:tiles, :] for i in range(3)]
                            nc.vector.tensor_copy(part[0], rest_of).then_inc(*step.tick())
                            here()
                            nc.vector.tensor_tensor(out=rest_of, in0=rest_of, in1=part[0], op=ALU.subtract).then_inc(
                                *step.tick())
                            here()
                            nc.vector.tensor_copy(part[1], rest_of).then_inc(*step.tick())
                            here()
                            nc.vector.tensor_tensor(out=part[2], in0=rest_of, in1=part[1], op=ALU.subtract).then_inc(
                                *parts_ready.rise(key))

                        def values_out(key):
                            s, k = key[1:]
                            d = full(key)
                            for b in range(G):
                                to = value[s][:, b * KT + k, :, 0:HD]
                                of = by_head(d[:, b * kc:(b + 1) * kc])
                                if "q" in vectors:
                                    last = nc.vector.tensor_tensor(out=to, in0=of, in1=by_head(rows[:, V_BIAS, 0:kc]),
                                                                   op=ALU.add)
                                else:
                                    last = nc.vector.tensor_copy(to, of)
                            last.then_inc(*out_of(key).rise(key))

                        def maxima(n):
                            dve.wait_ge(a_full.sem, a_full.at(p, n))
                            nc.vector.tensor_reduce(out=m_neg[:, n % 2, 0:U],
                                                    in_=ps_a[n % 2][:].rearrange("p (h k) -> p h k", h=U), axis=AX.X,
                                                    op=ALU.max, negate=True).then_inc(*a_out.rise(n))
                            dve.wait_ge(a_out.sem, a_out.at(p, n))
                            nc.vector.tensor_copy(m_parts[:, n % 2, 0:U], m_neg[:, n % 2, 0:U]).then_inc(*step.tick())
                            here()
                            nc.vector.tensor_tensor(out=m_parts[:, n % 2, 8:8 + U], in0=m_neg[:, n % 2, 0:U],
                                                    in1=m_parts[:, n % 2, 0:U], op=ALU.subtract).then_inc(
                                *m_ready.rise(n))

                        def divide(n):
                            s, b, h0 = L.units[n]
                            if n % (N // 2) == 0:
                                dve.wait_ge(y_stored[s].sem, y_stored[s].prev(p, "y"))
                            key = ("OT", n)
                            d = full(key)[:, 0:U * 32].rearrange("p (h e) -> p h e", e=32)
                            nc.vector.reciprocal(r_inv[:, n % 2, 0:U].unsqueeze(2), d[:, :, HD:HD + 1]).then_inc(
                                *step.tick())
                            here()
                            nc.vector.tensor_tensor(
                                out=by_head(heads_out[s][:, b, h0 * HD:(h0 + U) * HD]), in0=d[:, :, 0:HD],
                                in1=r_inv[:, n % 2, 0:U].unsqueeze(2).broadcast_to([128, U, HD]),
                                op=ALU.mult).then_inc(*out_of(key).rise(key))

                        in_tok, in_loaded = (x_in, x_loaded) if L.ln_x else (c_tok, c_loaded)

                        def input_stats():
                            for s in normed["prep"]:
                                g = in_loaded[s]
                                dve.wait_ge(g.sem, g.at(it, g.keys[-1]))
                                norm_stats("prep", s, in_tok[s])

                        def normalise_inputs():
                            for s in normed["prep"]:
                                normalise("prep", s, in_tok[s], in_tok[s])

                        if not rest:
                            input_stats()
                            normalise_inputs()
                        for n in range(N + 3 if rest else 0):
                            if n < N:
                                maxima(n)
                            if prep and n == N:
                                input_stats()
                            if n >= 3:
                                divide(n - 3)
                            if prep and n == N:
                                normalise_inputs()

                        if prep:
                            for i, key in enumerate(turned):
                                s = key[1]
                                hi_half(key, c_hi[s] if key[0] == "TC" else x_hi[s], t32[i % 2])
                            if L.float_mask:
                                for s in range(S):
                                    dve.wait_ge(c_loaded[s].sem, c_loaded[s].at(it, "mask"))
                                    dve.wait_ge(b_full.sem, b_full.prev(it, (last_unit[s], 1)))
                                    nc.vector.tensor_copy(hid_hi[s][:].rearrange("p a b -> p (a b)")[:, 0:GT],
                                                          c_tok[s][:, :, 0:T]).then_inc(*mask_hi_ready.rise(s))
                        if rest:
                            for s in range(S):
                                hi_half(("TO", s), p_hi[s], hid32[s])
                        if prep:
                            for n in range(first_half):
                                three_parts(n)
                        for s in range(S if rest else 0):
                            d = full(("O", s))
                            dve.wait_ge(residual_loaded[s].sem, residual_loaded[s].at(p, "x"))
                            h = heads_out[s][:].rearrange("p b d -> p (b d)")
                            if L.name == "L3":
                                for b in range(G):
                                    last = nc.vector.scalar_tensor_tensor(
                                        out=heads_out[s][:, b, :], in0=d[:, b * D:(b + 1) * D],
                                        scalar=gate[:, bass.ds(p * (G * S) + (2 + s * G + b), 1)],
                                        in1=x_tok[s][:, b, :], op0=ALU.mult, op1=ALU.add)
                                last.then_inc(*out_of(("O", s)).rise(("O", s)))
                                continue
                            nc.vector.tensor_tensor(out=h, in0=d[:], in1=x_tok[s][:].rearrange("p b d -> p (b d)"),
                                                    op=ALU.add).then_inc(*out_of(("O", s)).rise(("O", s)))
                            dve.wait_ge(out_of(("O", s)).sem, out_of(("O", s)).at(p, ("O", s)))
                            nc.vector.tensor_tensor(out=heads_out[s][:], in0=heads_out[s][:],
                                                    in1=repeat(rows[:, O_BIAS, :], G), op=ALU.add).then_inc(*step.tick())
                            here()
                            norm_stats("post", s, heads_out[s])
                        if rest and L.name != "L3":
                            for s in range(S):
                                if L.float_mask:
                                    dve.wait_ge(y_stored[s].sem, y_stored[s].prev(p, "y"))
                                normalise("post", s, heads_out[s], norm[s])
                        last_parts = list(range(first_half, len(projected)))
                        if prep:
                            while len(last_parts) > (2 if rest and L.mlp else 0):
                                three_parts(last_parts.pop(0))
                        if rest and L.mlp:
                            for s in range(S):
                                hi_half(("TL", s), p_hi[s], hid32[s])
                        if prep:
                            for key in outputs:
                                values_out(key)
                        if rest and L.mlp:
                            for s in range(S):
                                for c in chunks_f:
                                    in_sbuf(("F", s, c))
                                    dve.wait_ge(hid_used.sem, hid_used.back(p, (s, c), 2))
                                    nc.vector.tensor_copy(hid_hi[c % 2][:], hid32[c % 2][:]).then_inc(
                                        *hid_hi_ready.rise((s, c)))
                                    if prep and last_parts:
                                        three_parts(last_parts.pop(0))
                                dve.wait_ge(hid_used.sem, hid_used.at(p, (s, FT // 2 - 1)))
                                nc.vector.tensor_tensor(
                                    out=heads_out[s][:], in0=ps_a[s][:].rearrange("p (b n) -> p b n", b=G)[:, :, 0:D],
                                    in1=(x_tok if L.name == "L2" else heads_out)[s][:], op=ALU.add).then_inc(
                                    *a_out.rise(("M", s)))
                                dve.wait_ge(a_out.sem, a_out.at(p, ("M", s)))
                                nc.vector.tensor_tensor(out=heads_out[s][:], in0=heads_out[s][:],
                                                        in1=repeat(rows[:, M_BIAS, :], G), op=ALU.add).then_inc(
                                    *y_ready.rise(s))

                    body(-1, prep=True, rest=False)
                    with dve.Fori(0, PASSES - 1) as p:
                        step.enter(p, STEPS[L.name])
                        body(p, prep=True, rest=True)
                    step.leave(L.name, PASSES - 1)
                    body(PASSES - 1, prep=False, rest=True)

                @block.gpsimd
                def _(pool):
                    def body(p, prep, rest):
                        it = p + 1

                        def power(phase, s):
                            g = spread_ready[phase]
                            pool.wait_ge(g.sem, g.at(it if phase == "prep" else p, s))
                            nc.gpsimd.tensor_tensor(out=rstd[:, s, :], in0=spread[:, s, :],
                                                    in1=minus_half[:], op=ALU.pow).then_inc(*rstd_ready[phase].rise(s))

                        def lo_half(key, of, hi, lo):
                            g = hi_ready[phase_of[key]]
                            pool.wait_ge(g.sem, g.at(it if phase_of[key] == "prep" else p, key))
                            nc.gpsimd.tensor_tensor(out=lo[:], in0=of[:], in1=f32(hi[:]),
                                                    op=ALU.subtract).then_inc(*lo_ready[phase_of[key]].rise(key))

                        if prep:
                            for s in normed["prep"]:
                                power("prep", s)
                            for i, key in enumerate(turned):
                                s = key[1]
                                lo_half(key, t32[i % 2], *((c_hi[s], c_lo[s]) if key[0] == "TC" else (x_hi[s], x_lo[s])))
                            if L.float_mask:
                                for s in range(S):
                                    pool.wait_ge(mask_hi_ready.sem, mask_hi_ready.at(it, s))
                                    nc.gpsimd.tensor_tensor(
                                        out=hid_lo[s][:].rearrange("p a b -> p (a b)")[:, 0:GT].rearrange(
                                            "p (b k) -> p b k", b=G),
                                        in0=c_tok[s][:, :, 0:T],
                                        in1=f32(hid_hi[s][:].rearrange("p a b -> p (a b)")[:, 0:GT]).rearrange(
                                            "p (b k) -> p b k", b=G), op=ALU.subtract).then_inc(*mask_lo_ready.rise(s))
                        if rest:
                            for s in range(S):
                                lo_half(("TO", s), hid32[s], p_hi[s], p_lo[s])
                            for s in normed["post"]:
                                power("post", s)
                        if rest and L.float_mask:
                            for s in range(S):
                                pool.wait_ge(norm_ready["post"].sem, norm_ready["post"].at(p, s))
                                nc.gpsimd.tensor_tensor(out=norm[s][:], in0=norm[s][:], in1=repeat(rows[:, GAMMA, :], G),
                                                        op=ALU.mult).then_inc(*scaled.rise(s))
                                pool.wait_ge(scaled.sem, scaled.at(p, s))
                                nc.gpsimd.tensor_tensor(out=norm[s][:], in0=norm[s][:], in1=repeat(rows[:, BETA, :], G),
                                                        op=ALU.add).then_inc(*y_ready.rise(s))
                        if rest and L.mlp:
                            for s in range(S):
                                lo_half(("TL", s), hid32[s], p_hi[s], p_lo[s])
                            for s in range(S):
                                for c in chunks_f:
                                    pool.wait_ge(hid_hi_ready.sem, hid_hi_ready.at(p, (s, c)))
                                    nc.gpsimd.tensor_tensor(out=hid_lo[c % 2][:], in0=hid32[c % 2][:],
                                                            in1=f32(hid_hi[c % 2][:]), op=ALU.subtract).then_inc(
                                        *hid_lo_ready.rise((s, c)))

                    passes(pool, body)
            finish(PASSES)


def kernel(**inputs):
    import numpy as _np
    import concourse.bacc as _bacc
    from concourse import mybir as _mybir
    from concourse.bass_utils import run_bass_kernel_spmd as _run

    nc = _bacc.Bacc("TRN2", target_bir_lowering=False, num_devices=1)
    arrays, ins = {}, {}
    for name, a in inputs.items():
        a = _np.ascontiguousarray(a)
        if a.dtype == _np.bool_:
            a = a.view(_np.uint8)
        arrays[f"in_{name}_dram"] = a
        ins[name] = nc.dram_tensor(f"in_{name}_dram", a.shape, _mybir.dt.from_np(a.dtype), kind="ExternalInput").ap()
    out = nc.dram_tensor("out_dram", (B, T, D), _mybir.dt.float32, kind="ExternalOutput").ap()
    xattn_program(nc, ins, out)
    r = _run(nc, [arrays], core_ids=[0])
    return r.results[0]["out_dram"]
```

```python
from contextlib import ExitStack

import numpy as np

import concourse.bass as bass
from concourse import mybir

B = 16
T = 128
D = 256
DT = D // 128
INNER = 4 * D
FT = INNER // 128
G = 2
S = 2
GT = G * T
PASSES = B // (G * S)
BIG = 3.0e38
LARGEST = float(np.finfo(np.float32).max)
CREDIT = 256
PR = 96

Q_SLOTS = ((0, 0, 3, 1), (0, 3, 2, 1), (0, 5, 1, 1))
K_SLOTS = ((0, 0, 1, 3), (1, 3, 1, 2), (2, 5, 1, 1))


class Layer:
    def __init__(self, name, heads, head, kv_heads, key_tiles, unit, scale, eps, ln_x=False, ln_c=False,
                 load_ct=False, store_ct=False, mlp=False, float_mask=False):
        self.name, self.heads, self.head, self.kv_heads = name, heads, head, kv_heads
        self.key_tiles, self.unit, self.scale, self.eps = key_tiles, unit, scale, eps
        self.ln_x, self.ln_c, self.load_ct, self.store_ct = ln_x, ln_c, load_ct, store_ct
        self.mlp, self.float_mask = mlp, float_mask
        self.group = heads // kv_heads
        self.kcols = kv_heads * head
        self.units = [(s, b, h) for s in range(S) for b in range(G) for h in range(0, heads, unit)]


LAYERS = [
    Layer("L0", 16, 16, 16, 1, 8, 0.25, 1e-5, ln_x=True, store_ct=True, mlp=True),
    Layer("L1", 32, 8, 8, 1, 8, float(8.0 ** -0.5), 1e-6, load_ct=True, float_mask=True),
    Layer("L2", 16, 16, 16, 2, 4, 1.0 / 16, 1e-6, load_ct=True, mlp=True),
    Layer("L3", 16, 16, 16, 1, 8, 0.25, 1e-5, ln_c=True),
]


class Signal:

    def __init__(self, sem, step=1):
        self.sem, self.step, self.total, self.keys, self.risen = sem, step, CREDIT, [], set()

    def plan(self, keys, passes=1):
        self.keys, self.risen, self.passes = list(keys), set(), passes
        assert self.step * len(self.keys) < CREDIT, (self.sem, len(self.keys))

    def rise(self, key):
        assert key in self.keys, (self.sem, key)
        self.risen.add(key)
        return self.sem, self.step

    def at(self, it, key):
        return self.total + self.step * (it * len(self.keys) + self.keys.index(key) + 1)

    def prev(self, it, key):
        return self.total + self.step * ((it - 1) * len(self.keys) + self.keys.index(key) + 1)

    def back(self, it, key, n):
        return self.total + self.step * (it * len(self.keys) + self.keys.index(key) + 1 - n)

    def finish(self):
        assert len(self.risen) == len(self.keys), (self.sem, set(self.keys) - self.risen)
        self.total += self.step * len(self.keys) * self.passes
        self.keys, self.risen = [], set()


class Steps:

    def __init__(self, sem):
        self.sem, self.total, self.it, self.per, self.n = sem, CREDIT, None, 0, 0

    def enter(self, it, per):
        self.total, self.it, self.per, self.n = self.total + self.n, it, per, 0

    def leave(self, layer, passes):
        assert self.n == self.per, f"STEPS {layer} {self.n}"
        self.total, self.it, self.n = self.total + self.per * passes, None, 0

    def tick(self):
        self.n += 1
        return self.sem, 1

    def now(self):
        return self.total + self.n + (0 if self.it is None else self.it * self.per)


STEPS = {"L0": 46, "L1": 168, "L2": 62, "L3": 36}


def xattn_program(nc, ins, out):
    F32, F32R, BF16 = mybir.dt.float32, mybir.dt.float32r, mybir.dt.bfloat16
    ALU, ACT, AX = mybir.AluOpType, mybir.ActivationFunctionType, mybir.AxisListType

    ctx = ExitStack()
    with ctx:
        def sb(name, shape, dt=F32):
            return ctx.enter_context(nc.sbuf_tensor(name, shape, dt))

        def dram(name, shape, dt=F32):
            return nc.dram_tensor(name, shape, dt, kind="Internal").ap()

        signals = []
        PHASES = ("prep", "att", "post")

        def signal(name, step=1):
            signals.append(Signal(ctx.enter_context(nc.semaphore(name)), step))
            return signals[-1]

        W_COLS = 4 * DT * D + 2 * DT * INNER
        whi = sb("weights_hi", [128, W_COLS], F32R)
        wlo = sb("weights_lo", [128, W_COLS], F32R)
        ARENA = 48 * GT
        arena = [sb(f"stacks{s}", [128, ARENA], BF16) for s in range(S)]
        values = [sb(f"values{s}", [128, G * 2 * 16 * 32]) for s in range(S)]
        probs = sb("probs", [128, 4, 512])
        x_in = [sb(f"x_in{s}", [128, G, D]) for s in range(S)]
        x_tok = [sb(f"x_tok{s}", [128, G, D]) for s in range(S)]
        c_tok = [sb(f"c_tok{s}", [128, G, D]) for s in range(S)]
        norm = [sb(f"norm{s}", [128, G, D]) for s in range(S)]
        heads_out = [sb(f"heads_out{s}", [128, G, D]) for s in range(S)]
        t32 = [sb(f"t32_{i}", [128, DT, GT]) for i in range(2)]
        x_hi = [sb(f"x_hi{s}", [128, DT, GT], F32R) for s in range(S)]
        x_lo = [sb(f"x_lo{s}", [128, DT, GT], F32R) for s in range(S)]
        p_hi = [sb(f"p_hi{s}", [128, DT, GT], F32R) for s in range(S)]
        p_lo = [sb(f"p_lo{s}", [128, DT, GT], F32R) for s in range(S)]
        c_hi = [sb(f"c_hi{s}", [128, DT, GT], F32R) for s in range(S)]
        c_lo = [sb(f"c_lo{s}", [128, DT, GT], F32R) for s in range(S)]
        qk32 = [sb(f"qk32_{i}", [128, DT, GT]) for i in range(2)]
        parts = [sb(f"parts{i}", [128, 3, DT, GT], BF16) for i in range(2)]
        hid32 = [sb(f"hid32_{i}", [128, 2, GT]) for i in range(2)]
        hid_hi = [sb(f"hid_hi{i}", [128, 2, GT], F32R) for i in range(2)]
        hid_lo = [sb(f"hid_lo{i}", [128, 2, GT], F32R) for i in range(2)]
        o_t = sb("o_t", [128, 256])
        m_neg = sb("m_neg", [128, 2, 8])
        m_parts = sb("m_parts", [128, 2, 128], BF16)
        m_rows = sb("m_rows", [128, 2, 128], BF16)
        r_inv = sb("r_inv", [128, 2, 8])
        stats = sb("stats", [128, S, G, 6])
        moments = sb("moments", [128, S, G, 2])
        spread = sb("spread", [128, S, G])
        rstd = sb("rstd", [128, S, G])
        minus_half = sb("minus_half", [128, G])
        spare = sb("spare", [128, 1])
        act_spare = sb("act_spare", [128, 2])
        ident = sb("ident", [128, 128])
        ident_r = sb("ident_r", [128, 128], F32R)
        ident_b = sb("ident_b", [128, 128], BF16)
        select = sb("select", [128, 8, 128], BF16)
        rows = sb("rows", [128, 5, D])
        V_BIAS, O_BIAS, M_BIAS, GAMMA, BETA = range(5)
        cols = sb("cols", [128, 12 + FT])
        Q_COL, K_COL, W1_COL, B1_COL, W2_COL, B2_COL, F_COL = 0, 2, 4, 6, 8, 10, 12
        mask_f = sb("mask_f", [B, T])
        mask_u8 = sb("mask_u8", [B, T], mybir.dt.uint8)
        mask_i32 = sb("mask_i32", [B, T], mybir.dt.int32)
        mask_b = sb("mask_b", [B, 2, T], BF16)
        key_ok = sb("key_ok", [B, 3])
        gate = sb("gate", [128, 2 + B])

        ps_a = [ctx.enter_context(nc.psum_tensor(f"ps_a{i}", [128, 1024], F32)) for i in range(2)]
        ps_b = [ctx.enter_context(nc.psum_tensor(f"ps_b{i}", [128, 512], F32)) for i in range(2)]
        ps_d = [ctx.enter_context(nc.psum_tensor(f"ps_d{i}", [128, 512], F32)) for i in range(2)]

        x_dram = [ins["x"]] + [dram(f"x_after{i}", [B, T, D]) for i in range(3)] + [out]
        ct_dram = dram("ct", [PASSES, S, 2, 128, DT * GT])
        bias_dram = dram("key_bias", [2, B * T], BF16)
        ok_dram = dram("key_ok_rows", [B])
        q_dram = [dram(f"q_parts{s}", [3 * D * GT], BF16) for s in range(S)]
        k_dram = [[dram(f"k_parts{s}_{k}", [3 * D * GT], BF16) for k in range(2)] for s in range(S)]

        eye_ready = signal("eye_ready")
        const_ready = signal("const_ready")
        tanh_ready = signal("tanh_ready")
        const_loaded = signal("const_loaded", 16)
        bias_stored = signal("bias_stored", 16)
        factor_loaded = signal("factor_loaded", 16)
        raw_loaded = [signal(f"raw_loaded{i}", 16) for i in range(4)]
        raw_split = signal("raw_split")
        late_loaded = [signal(f"late_loaded{i}", 16) for i in range(FT + 4)]
        late_rounded = signal("late_rounded")
        late_split = signal("late_split")
        raw_turned = signal("raw_turned")
        vectors_loaded = signal("vectors_loaded", 16)
        vectors_ready = signal("vectors_ready")
        stacks_clear = signal("stacks_clear")
        values_clear = signal("values_clear")
        x_loaded = [signal(f"x_loaded{s}", 16) for s in range(S)]
        residual_loaded = [signal(f"residual_loaded{s}", 16) for s in range(S)]
        c_loaded = [signal(f"c_loaded{s}", 16) for s in range(S)]
        ct_stored = [signal(f"ct_stored{s}", 16) for s in range(S)]
        written = {("Q", s): signal(f"q_written{s}", 16) for s in range(S)}
        written.update({("K", s, k): signal(f"k_written{s}_{k}", 16) for s in range(S) for k in range(2)})
        q_stacked = [signal(f"q_stacked{s}", 16) for s in range(S)]
        k_stacked = [signal(f"k_stacked{s}", 16) for s in range(S)]
        y_stored = [signal(f"y_stored{s}", 16) for s in range(S)]
        spread_ready = {f: signal(f"spread_ready_{f}") for f in ("prep", "post")}
        rstd_ready = {f: signal(f"rstd_ready_{f}") for f in ("prep", "post")}
        norm_ready = {f: signal(f"norm_ready_{f}") for f in ("prep", "post")}
        d_full = {f: signal(f"d_full_{f}") for f in PHASES}
        d_out = {f: [signal(f"d_out{i}_{f}") for i in range(2)] for f in PHASES}
        hi_ready = {f: signal(f"hi_ready_{f}") for f in ("prep", "post")}
        lo_ready = {f: signal(f"lo_ready_{f}") for f in ("prep", "post")}
        parts_ready = signal("parts_ready")
        mask_hi_ready = signal("mask_hi_ready")
        mask_lo_ready = signal("mask_lo_ready")
        a_full = signal("a_full")
        a_out = signal("a_out")
        m_ready = signal("m_ready")
        b_full = signal("b_full")
        b_out = signal("b_out")
        hid_hi_ready = signal("hid_hi_ready")
        hid_lo_ready = signal("hid_lo_ready")
        hid_used = signal("hid_used")
        y_ready = signal("y_ready")
        scaled = signal("scaled")
        step = Steps(ctx.enter_context(nc.semaphore("vector_step")))

        def finish():
            for g in signals:
                if g.keys:
                    g.finish()

        def f32(ap):
            return ap.bitcast(F32)

        def repeat(ap, n):
            return ap.unsqueeze(1).broadcast_to([ap.shape[0], n, ap.shape[1]])

        with nc.Block() as block:
            @block.sync
            def _(sp):
                for g in signals + [step]:
                    sp.sem_inc(g.sem, CREDIT)

        eye_ready.plan(["zero", "half", "eye"])
        const_ready.plan(["eye_b", "eye_r", "select", "no_max", "mask_f", "count", "bias0", "bias1", "inverse",
                          "ok", "factors"])
        tanh_ready.plan(["gate"])
        const_loaded.plan(["u8", "i32", "gate"])
        bias_stored.plan(["bias", "ok"])
        factor_loaded.plan(["ok"])
        with nc.Block() as block:
            @block.sync
            def _(sp):
                sp.dma_start(mask_u8[:], ins["mask_BxS2_bf1"]).then_inc(*const_loaded.rise("u8"))
                sp.dma_start(mask_i32[:], ins["mask_BxS2_ik0"]).then_inc(*const_loaded.rise("i32"))
                sp.dma_start(gate[:, 0:1], ins["L3_xattn_gate"].partition_broadcast(128)).then_inc(
                    *const_loaded.rise("gate"))
                sp.wait_ge(const_ready.sem, const_ready.at(0, "ok"))
                sp.dma_start(bias_dram.rearrange("m (b t) -> b m t", b=B), mask_b[:]).then_inc(
                    *bias_stored.rise("bias"))
                sp.dma_start(ok_dram.unsqueeze(1), key_ok[:, 0:1]).then_inc(*bias_stored.rise("ok"))
                sp.wait_ge(bias_stored.sem, bias_stored.at(0, "ok"))
                sp.dma_start(gate[:, 2:2 + B], ok_dram.partition_broadcast(128)).then_inc(
                    *factor_loaded.rise("ok"))

            @block.gpsimd
            def _(pool):
                nc.gpsimd.memset(ident[:], 0.0).then_inc(*eye_ready.rise("zero"))
                nc.gpsimd.memset(minus_half[:], -0.5).then_inc(*eye_ready.rise("half"))
                pool.wait_ge(eye_ready.sem, eye_ready.at(0, "half"))
                nc.gpsimd.affine_select(out=ident[:], in_=ident[:], compare_op=ALU.not_equal, fill=1.0, base=0,
                                        pattern=[[-1, 128]], channel_multiplier=1).then_inc(
                    *eye_ready.rise("eye"))

            @block.vector
            def _(dve):
                dve.wait_ge(eye_ready.sem, eye_ready.at(0, "eye"))
                nc.vector.tensor_copy(ident_b[:], ident[:]).then_inc(*const_ready.rise("eye_b"))
                nc.vector.tensor_copy(ident_r[:], ident[:]).then_inc(*const_ready.rise("eye_r"))
                nc.vector.tensor_tensor(
                    out=select[:], in0=ident[:, 0:8].unsqueeze(2).broadcast_to([128, 8, 128]),
                    in1=ident[:, 8:16].unsqueeze(2).broadcast_to([128, 8, 128]), op=ALU.add).then_inc(
                    *const_ready.rise("select"))
                nc.vector.memset(m_parts[:], 0.0).then_inc(*const_ready.rise("no_max"))
                dve.wait_ge(const_loaded.sem, const_loaded.at(0, "gate"))
                nc.vector.tensor_copy(mask_f[:], mask_u8[:]).then_inc(*const_ready.rise("mask_f"))
                dve.wait_ge(const_ready.sem, const_ready.at(0, "mask_f"))
                nc.vector.tensor_reduce(out=key_ok[:, 1:2], in_=mask_f[:], axis=AX.X, op=ALU.add).then_inc(
                    *const_ready.rise("count"))
                nc.vector.tensor_scalar(mask_b[:, 0, :], mask_f[:], 0.0, -BIG, ALU.is_equal,
                                        ALU.mult).then_inc(*const_ready.rise("bias0"))
                nc.vector.tensor_scalar(mask_b[:, 1, :], mask_i32[:], 0.0, -BIG, ALU.is_equal,
                                        ALU.mult).then_inc(*const_ready.rise("bias1"))
                dve.wait_ge(const_ready.sem, const_ready.at(0, "bias1"))
                nc.vector.reciprocal(key_ok[:, 2:3], key_ok[:, 1:2]).then_inc(*const_ready.rise("inverse"))
                dve.wait_ge(const_ready.sem, const_ready.at(0, "inverse"))
                nc.vector.tensor_scalar(key_ok[:, 0:1], key_ok[:, 2:3], 0.0, 1.0, ALU.mult,
                                        ALU.add).then_inc(*const_ready.rise("ok"))
                dve.wait_ge(factor_loaded.sem, factor_loaded.at(0, "ok"))
                dve.wait_ge(tanh_ready.sem, tanh_ready.at(0, "gate"))
                nc.vector.tensor_scalar(gate[:, 2:2 + B], gate[:, 2:2 + B], gate[:, 1:2], None,
                                        ALU.mult).then_inc(*const_ready.rise("factors"))

            @block.scalar
            def _(act):
                act.wait_ge(const_loaded.sem, const_loaded.at(0, "gate"))
                nc.scalar.activation(gate[:, 1:2], gate[:, 0:1], ACT.Tanh).then_inc(*tanh_ready.rise("gate"))
        finish()

        for index, L in enumerate(LAYERS):
            name = L.name + "_xattn_"
            H, HD, KV, KT, U = L.heads, L.head, L.kv_heads, L.key_tiles, L.unit
            kc = KV * HD
            k_rows, k_tiles = min(kc, 128), -(-kc // 128)

            place, first = {}, 0
            for key, tiles, width in [("q", DT, D), ("k", DT, kc), ("v", DT, kc), ("o", DT, D)] + (
                    [("f", DT, INNER), ("m", FT, D)] if L.mlp else []):
                place[key] = (first, tiles, width)
                first += tiles * width

            def weight(t, key):
                start, tiles, width = place[key]
                return t[:, start:start + tiles * width].rearrange("p (k n) -> p k n", k=tiles)

            def both(key):
                return weight(whi, key), weight(wlo, key)

            matrices = {
                "L0": dict(q="q_w", k="k_w", v="v_w", o="cproj_w", f="fc_w", m="proj_w"),
                "L1": dict(q="Wq", k="Wk", v="Wv", o="Wo"),
                "L2": dict(q="q_w", kv="kv_w", o="out_w", f="mlp_w1", m="mlp_w2"),
                "L3": dict(q="Wq", k="Wk", v="Wv", o="Wo"),
            }[L.name]
            vectors = {
                "L0": dict(q="q_b", k="k_b", v="v_b", o="cproj_b", w1="ln1_w", b1="ln1_b", w2="ln2_w",
                           b2="ln2_b", f="fc_b", m="proj_b"),
                "L1": dict(q="bq", k="bk", v="bv", o="bo", gamma="gamma", beta="beta"),
                "L2": dict(q="q_b", kv="kv_b", o="out_b", w2="postnorm_w", f="mlp_b1", m="mlp_b2"),
                "L3": dict(w1="ln_gamma", b1="ln_beta"),
            }[L.name]

            chunks = []
            for key, w in matrices.items():
                tall, broad = ins[name + w].shape
                for tile in range(tall // 128):
                    for c0 in range(0, broad, 512):
                        chunks.append((key, tile, c0, min(512, broad - c0)))
            late = [c for c in chunks if c[0] == "m"] + [c for c in chunks if c[0] == "f"]
            chunks = [c for c in chunks if c[0] not in ("f", "m")]

            def by_dimension(ap, heads):
                return ap.rearrange("p (d h) -> p h d", h=heads)

            def by_head(ap):
                return ap.rearrange("p (h d) -> p h d", d=HD)

            def homes(t, raw, key, tile, c0, width):
                if key == "kv":
                    two = raw.rearrange("p (h d e) -> p h d e", d=HD, e=2)
                    return [(two[:, :, :, 0], by_dimension(weight(t, "k")[:, tile, :], KV)),
                            (two[:, :, :, 1], by_head(weight(t, "v")[:, tile, :]))]
                if key in ("q", "k"):
                    return [(by_head(raw), by_dimension(weight(t, key)[:, tile, :], H if key == "q" else KV))]
                return [(raw, weight(t, key)[:, tile, c0:c0 + width])]

            def turned_homes(t, bank, key, tile):
                found = []
                for into in range(DT):
                    raw = bank[:, 128 * into:128 * into + 128]
                    if key in ("q", "k"):
                        n_heads = 128 // HD
                        home = by_dimension(weight(t, key)[:, into, :], H)
                        found.append((by_head(raw), home[:, n_heads * tile:n_heads * (tile + 1), :]))
                    else:
                        found.append((raw, weight(t, key)[:, into, 128 * tile:128 * tile + 128]))
                return found

            loads = []
            if "q" in vectors:
                q_bias = ins[name + vectors["q"]].rearrange("(h d) -> d h", d=HD)
                per = 128 // H
                for t in range(DT):
                    loads.append((cols[:, Q_COL + t:Q_COL + t + 1], q_bias[per * t:per * t + per, :].unsqueeze(2)))
                if "kv" in vectors:
                    k_bias = ins[name + "kv_b"].rearrange("(h d e) -> e d h", d=HD, e=2)[0]
                    loads.append((t32[0][:].rearrange("p a b -> p (a b)"), ins[name + "kv_b"].partition_broadcast(128)))
                else:
                    k_bias = ins[name + vectors["k"]].rearrange("(h d) -> d h", d=HD)
                    loads.append((rows[:, V_BIAS, 0:kc], ins[name + vectors["v"]].partition_broadcast(128)))
                per = k_rows // KV
                for t in range(k_tiles):
                    loads.append((cols[0:k_rows, K_COL + t:K_COL + t + 1],
                                  k_bias[per * t:per * t + per, :].unsqueeze(2)))
            for key, row in (("o", O_BIAS), ("m", M_BIAS), ("gamma", GAMMA), ("beta", BETA)):
                if key in vectors:
                    loads.append((rows[:, row, :], ins[name + vectors[key]].partition_broadcast(128)))
            for key, col in (("w1", W1_COL), ("b1", B1_COL), ("w2", W2_COL), ("b2", B2_COL), ("f", F_COL)):
                if key in vectors:
                    v = ins[name + vectors[key]].rearrange("(c p) -> p c", p=128)
                    loads.append((cols[:, col:col + v.shape[1]], v))

            q_stack = [arena[s][:, 0:H * GT].rearrange("p (h t) -> p h t", t=GT) for s in range(S)]
            k_stack = [arena[s][:, H * GT:(H + KT * KV) * GT].rearrange("p (k h t) -> p k h t", k=KT, t=GT)
                       for s in range(S)]
            value = [values[s][:, 0:G * KT * KV * 32].rearrange("p (g h e) -> p g h e", g=G * KT, e=32)
                     for s in range(S)]

            for i in range(4):
                raw_loaded[i].plan(range((len(chunks) - i + 3) // 4))
            raw_split.plan(range(len(chunks)))
            for i in range(len(late)):
                late_loaded[i].plan(["chunk"])
            late_rounded.plan(range(len(late)))
            late_split.plan(range(len(late)))
            if L.name == "L3":
                raw_turned.plan(range(len(chunks)))
            vectors_loaded.plan(range(len(loads)))
            if "q" in vectors:
                vectors_ready.plan(["q"] + (["v"] if "kv" in vectors else []))
            clears = [(s, k) for k in ("all", "one", "sum") for s in range(S)
                      if not (k == "all" and L.name in ("L2", "L3") or k == "one" and L.float_mask)]
            stacks_clear.plan(clears)
            if L.name == "L0":
                values_clear.plan(range(S))
            late_place = [place_of[:, b, :] for place_of in (*heads_out, *x_tok) for b in range(G)]
            late_place += [place_of[:].rearrange("p a b -> p (a b)") for place_of in (*hid32, *norm)]

            def load_chunk(sp, i):
                key, tile, c0, width = chunks[i]
                if i >= 4:
                    sp.wait_ge(raw_split.sem, raw_split.at(0, i - 4))
                sp.dma_start(probs[:, i % 4, 0:width],
                             ins[name + matrices[key]][128 * tile:128 * tile + 128, c0:c0 + width]).then_inc(
                    *raw_loaded[i % 4].rise(i // 4))

            def load_late_chunk(sp, i):
                key, tile, c0, width = late[i]
                sp.dma_start(late_place[i][:, 0:width],
                             ins[name + matrices[key]][128 * tile:128 * tile + 128, c0:c0 + width]).then_inc(
                    *late_loaded[i].rise("chunk"))

            def load_vectors(act):
                for i, (to, of) in enumerate(loads):
                    with nc.allow_non_contiguous_dma(reason="a few hundred elements, once in a layer"):
                        act.dma_start(to, of).then_inc(*vectors_loaded.rise(i))
                act.wait_ge(vectors_loaded.sem, vectors_loaded.at(0, len(loads) - 1))
                if "q" in vectors:
                    act.wait_ge(vectors_ready.sem, vectors_ready.at(0, vectors_ready.keys[-1]))

            def round_late_chunks(act):
                for i, (key, tile, c0, width) in enumerate(late):
                    act.wait_ge(late_loaded[i].sem, late_loaded[i].at(0, "chunk"))
                    nc.scalar.activation(weight(whi, key)[:, tile, c0:c0 + width], late_place[i][:, 0:width],
                                         ACT.Copy).then_inc(*late_rounded.rise(i))

            def rest_of_late_chunks(pool):
                for i, (key, tile, c0, width) in enumerate(late):
                    pool.wait_ge(late_rounded.sem, late_rounded.at(0, i))
                    nc.gpsimd.tensor_tensor(out=weight(wlo, key)[:, tile, c0:c0 + width],
                                            in0=late_place[i][:, 0:width],
                                            in1=f32(weight(whi, key)[:, tile, c0:c0 + width]),
                                            op=ALU.subtract).then_inc(*late_split.rise(i))

            def wait_for_late_chunks(engine, last=-1):
                if late:
                    engine.wait_ge(late_split.sem, late_split.at(0, range(len(late))[last]))

            def clear_stacks(pool):
                for i, (s, what) in enumerate(clears):
                    if L.name == "L0" and (s, what) == (0, "sum"):
                        pool.wait_ge(values_clear.sem, values_clear.at(0, S - 1))
                    if i:
                        pool.wait_ge(stacks_clear.sem, stacks_clear.at(0, clears[i - 1]))
                    to, of = {
                        "all": (f32(arena[s][:]), 0.0),
                        "one": (q_stack[s][PR:PR + 1, :, :], 1.0),
                        "sum": (value[s][:, :, :, HD:HD + 1], 1.0),
                    }[what]
                    nc.gpsimd.memset(to, of).then_inc(*stacks_clear.rise((s, what)))

            def turn_chunks(pe):
                for i in range(len(chunks)):
                    pe.wait_ge(raw_loaded[i % 4].sem, raw_loaded[i % 4].at(0, i // 4))
                    if i >= 2:
                        pe.wait_ge(raw_split.sem, raw_split.at(0, i - 2))
                    for into in range(DT):
                        last = nc.tensor.transpose(ps_d[i % 2][:, 128 * into:128 * into + 128],
                                                   probs[:, i % 4, 128 * into:128 * into + 128], ident[:])
                    last.then_inc(*raw_turned.rise(i))
                pe.wait_ge(raw_split.sem, raw_split.at(0, len(chunks) - 1))

            def split_chunks(dve):
                if L.name == "L0":
                    for s in range(S):
                        nc.vector.memset(values[s][:], 0.0).then_inc(*values_clear.rise(s))
                for i, (key, tile, c0, width) in enumerate(chunks):
                    if L.name == "L3":
                        dve.wait_ge(raw_turned.sem, raw_turned.at(0, i))
                        hi_homes = turned_homes(whi, ps_d[i % 2], key, tile)
                        lo_homes = turned_homes(wlo, ps_d[i % 2], key, tile)
                    else:
                        dve.wait_ge(raw_loaded[i % 4].sem, raw_loaded[i % 4].at(0, i // 4))
                        raw = probs[:, i % 4, 0:width]
                        hi_homes = homes(whi, raw, key, tile, c0, width)
                        lo_homes = homes(wlo, raw, key, tile, c0, width)
                    for of, to in hi_homes:
                        nc.vector.tensor_copy(to, of).then_inc(*step.tick())
                    dve.wait_ge(step.sem, step.now())
                    for (of, hi), (_, lo) in zip(hi_homes[:-1], lo_homes[:-1]):
                        nc.vector.tensor_tensor(out=lo, in0=of, in1=f32(hi), op=ALU.subtract).then_inc(
                            *step.tick())
                    of, lo = lo_homes[-1]
                    nc.vector.tensor_tensor(out=lo, in0=of, in1=f32(hi_homes[-1][1]), op=ALU.subtract).then_inc(
                        *raw_split.rise(i))
                dve.wait_ge(vectors_loaded.sem, vectors_loaded.at(0, len(loads) - 1))
                if "q" in vectors:
                    nc.vector.tensor_scalar(cols[:, Q_COL:Q_COL + DT], cols[:, Q_COL:Q_COL + DT], L.scale, None,
                                            ALU.mult).then_inc(*vectors_ready.rise("q"))
                    if "kv" in vectors:
                        nc.vector.tensor_copy(
                            rows[:, V_BIAS, :],
                            t32[0][:].rearrange("p a b -> p (a b)").rearrange("p (n e) -> p n e", e=2)[:, :, 1]
                        ).then_inc(*vectors_ready.rise("v"))
                        dve.wait_ge(vectors_ready.sem, vectors_ready.at(0, "v"))

            N = len(L.units)
            last_unit = [N // 2 - 1, N - 1]
            chunks_f = range(FT // 2)
            turned = [(k, s) for s in range(S) for k in (("TX",) if L.load_ct else ("TX", "TC"))]
            projected = [("Q", s) if k is None else ("K", s, k) for s in range(S) for k in (None, *range(KT))]
            first_half = len(projected) // 2
            outputs = [("V", s, k) for s in range(S) for k in range(KT)]
            att_uses, mixed = [], []
            for n in range(N + 2):
                att_uses += [("MT", n)] if n < N else []
                att_uses += [("OT", n - 2)] if n >= 2 else []
                att_uses += [("PV", n - 1)] if 1 <= n <= N else []
            mixed += turned + [("TO", s) for s in range(S)] + projected[:first_half]
            mixed += [("O", s) for s in range(S)] + projected[first_half:]
            mixed += outputs[:KT] + ([("TL", s) for s in range(S)] if L.mlp else []) + outputs[KT:]
            mixed += [("F", s, c) for s in range(S) for c in chunks_f] if L.mlp else []
            phase_of = {key: "att" for key in att_uses}
            phase_of.update({key: "post" if key[0] in ("TO", "O", "TL", "F") else "prep" for key in mixed})
            body_uses = att_uses + mixed
            bank_of = {key: i % 2 for i, key in enumerate(body_uses)}
            halves = [(n, f) for n in range(N) for f in range(2)]
            k_loads = [(k, i) for k in range(KT) for i in range(3)] + ([] if L.float_mask else ["bias"])
            turned_post = [("TO", s) for s in range(S)] + ([("TL", s) for s in range(S)] if L.mlp else [])
            normed = {"prep": range(S) if L.ln_x or L.ln_c else (), "post": range(S) if L.name != "L3" else ()}

            for phase in PHASES:
                keys = [u for u in body_uses if phase_of[u] == phase]
                d_full[phase].plan(keys, PASSES)
                for i in range(2):
                    d_out[phase][i].plan([u for u in keys if bank_of[u] == i], PASSES)
            for phase, keys in (("prep", turned), ("post", turned_post)):
                hi_ready[phase].plan(keys, PASSES)
                lo_ready[phase].plan(keys, PASSES)
                for g in (spread_ready, rstd_ready, norm_ready):
                    g[phase].plan(normed[phase], PASSES)
            parts_ready.plan(projected, PASSES)
            for key in projected:
                written[key].plan(["parts"], PASSES)
            a_full.plan(range(N), PASSES)
            a_out.plan(list(range(N)) + ([("M", s) for s in range(S)] if L.mlp else []), PASSES)
            m_ready.plan(range(N), PASSES)
            b_full.plan(halves, PASSES)
            b_out.plan(halves, PASSES)
            if L.name != "L3":
                y_ready.plan(range(S), PASSES)
            if L.mlp:
                for g in (hid_hi_ready, hid_lo_ready, hid_used):
                    g.plan([(s, c) for s in range(S) for c in chunks_f], PASSES)
            if L.float_mask:
                mask_hi_ready.plan(range(S), PASSES)
                mask_lo_ready.plan(range(S), PASSES)
                scaled.plan(range(S), PASSES)
            for s in range(S):
                x_loaded[s].plan(["x"], PASSES)
                residual_loaded[s].plan(["x"], PASSES)
                c_loaded[s].plan(["hi", "lo", "mask"] if L.float_mask else ["hi", "lo"] if L.load_ct else ["c"], PASSES)
                if L.store_ct:
                    ct_stored[s].plan(["hi", "lo"], PASSES)
                q_stacked[s].plan(range(3), PASSES)
                k_stacked[s].plan(k_loads, PASSES)
                y_stored[s].plan(["y"], PASSES)

            def bank(key):
                return ps_d[bank_of[key]]

            def filled(key):
                return d_full[phase_of[key]]

            def out_of(key):
                return d_out[phase_of[key]][bank_of[key]]

            src, dst = x_dram[index], x_dram[index + 1]
            y_tile = norm if L.float_mask else heads_out

            def tok_rows(dram_ap, it, s):
                return dram_ap[bass.ds(it * (G * S) + s * G, G), :, :].rearrange("b t d -> t b d")

            def passes(engine, body):
                body(-1, prep=True, rest=False)
                with engine.Fori(0, PASSES - 1) as p:
                    body(p, prep=True, rest=True)
                body(PASSES - 1, prep=False, rest=True)

            with nc.Block() as block:
                @block.sync
                def _(sp):
                    def body(p, prep, rest):
                        it = p + 1
                        for i in range(0 if rest else 4):
                            load_chunk(sp, i)
                        for s in range(S):
                            if prep:
                                sp.wait_ge(d_full["prep"].sem, d_full["prep"].prev(it, ("TX", s)))
                                sp.dma_start(x_in[s][:], tok_rows(src, it, s)).then_inc(*x_loaded[s].rise("x"))
                            if prep and L.load_ct:
                                sp.wait_ge(d_full["prep"].sem, d_full["prep"].prev(it, ("V", s, 0)))
                                sp.dma_start(f32(c_hi[s][:]).rearrange("p k t -> p (k t)"),
                                             ct_dram[bass.ds(it, 1), s, 0, :, :].rearrange("i p n -> (i p) n")).then_inc(
                                    *c_loaded[s].rise("hi"))
                                sp.dma_start(f32(c_lo[s][:]).rearrange("p k t -> p (k t)"),
                                             ct_dram[bass.ds(it, 1), s, 1, :, :].rearrange("i p n -> (i p) n")).then_inc(
                                    *c_loaded[s].rise("lo"))
                                if L.float_mask:
                                    sp.wait_ge(a_out.sem, a_out.prev(it, last_unit[s]))
                                    sp.dma_start(
                                        c_tok[s][:, :, 0:T],
                                        ins["mask_Bx1xSxS2_ff0"].rearrange("b o q k -> b (o q) k")[
                                            bass.ds(it * (G * S) + s * G, G), :, :].rearrange("b q k -> q b k")
                                    ).then_inc(*c_loaded[s].rise("mask"))
                            elif prep:
                                sp.wait_ge(d_full["prep"].sem, d_full["prep"].prev(it, ("TC", s)))
                                sp.dma_start(c_tok[s][:], tok_rows(ins["ctx_2048"], it, s)).then_inc(
                                    *c_loaded[s].rise("c"))
                        if rest:
                            wait_for_late_chunks(sp, 4 * G - 1)
                        for s in range(S):
                            if rest:
                                if L.name == "L2":
                                    sp.wait_ge(a_out.sem, a_out.prev(p, ("M", s)))
                                else:
                                    sp.wait_ge(out_of(("O", s)).sem, out_of(("O", s)).prev(p, ("O", s)))
                                sp.dma_start(x_tok[s][:], tok_rows(src, p, s)).then_inc(*residual_loaded[s].rise("x"))
                        for i in range(4, 4 if rest else len(chunks)):
                            load_chunk(sp, i)
                        for i in range(0 if rest else len(late)):
                            load_late_chunk(sp, i)
                        for s in range(S if prep else 0):
                            sp.wait_ge(parts_ready.sem, parts_ready.at(it, ("Q", s)))
                            i = projected.index(("Q", s)) % 2
                            sp.dma_start(q_dram[s].rearrange("(n r k) -> r n k", r=128, k=GT),
                                         parts[i][:].rearrange("r p t k -> r (p t) k")).then_inc(
                                *written["Q", s].rise("parts"))
                            for k in range(KT):
                                sp.wait_ge(parts_ready.sem, parts_ready.at(it, ("K", s, k)))
                                i = projected.index(("K", s, k)) % 2
                                n = 3 * k_tiles
                                of = parts[i][:].rearrange("r p t k -> r (p t) k") if k_tiles == DT else \
                                    parts[i][0:k_rows, :, 0, :]
                                sp.dma_start(k_dram[s][k][0:n * k_rows * GT].rearrange("(n r k) -> r n k", r=k_rows, k=GT),
                                             of).then_inc(*written["K", s, k].rise("parts"))
                            sp.wait_ge(b_full.sem, b_full.prev(it, (last_unit[s], 1)))
                            if not rest:
                                sp.wait_ge(stacks_clear.sem, stacks_clear.at(0, clears[-1]))
                            sp.wait_ge(written["Q", s].sem, written["Q", s].at(it, "parts"))
                            part = HD * H * GT
                            for i, (p0, slot, n, rep) in enumerate(Q_SLOTS):
                                sp.dma_start(q_stack[s][slot * HD:(slot + n) * HD, :, :],
                                             q_dram[s][p0 * part:(p0 + n) * part].rearrange(
                                                 "(r h k) -> r h k", h=H, k=GT)).then_inc(*q_stacked[s].rise(i))
                            part = HD * KV * GT
                            for k in range(KT):
                                sp.wait_ge(written["K", s, k].sem, written["K", s, k].at(it, "parts"))
                                for i, (p0, slot, n, rep) in enumerate(K_SLOTS):
                                    of = k_dram[s][k][p0 * part:(p0 + 1) * part]
                                    of = of.rearrange("(o r n) -> o r n", o=1, r=HD).broadcast_to([rep, HD, KV * GT])
                                    sp.dma_start(
                                        k_stack[s][slot * HD:(slot + rep) * HD, k, :, :].rearrange("p h t -> p (h t)"),
                                        of).then_inc(*k_stacked[s].rise((k, i)))
                            if not L.float_mask:
                                row = bias_dram[1 if KT == 2 else 0, bass.ds((it * (G * S) + s * G) * T, GT)]
                                sp.dma_start(k_stack[s][PR:PR + 1, 0, :, :],
                                             row.rearrange("(o h t) -> o h t", o=1, h=1).broadcast_to([1, KV, GT])
                                             ).then_inc(*k_stacked[s].rise("bias"))
                            if L.store_ct:
                                sp.wait_ge(lo_ready["prep"].sem, lo_ready["prep"].at(it, ("TC", s)))
                                for i, t in enumerate((c_hi[s], c_lo[s])):
                                    sp.dma_start(ct_dram[bass.ds(it, 1), s, i, :, :].rearrange("i p n -> (i p) n"),
                                                 f32(t[:]).rearrange("p k t -> p (k t)")).then_inc(
                                        *ct_stored[s].rise(("hi", "lo")[i]))
                        for s in range(S if rest else 0):
                            g, key = (out_of(("O", s)), ("O", s)) if L.name == "L3" else (y_ready, s)
                            sp.wait_ge(g.sem, g.at(p, key))
                            sp.dma_start(tok_rows(dst, p, s), y_tile[s][:]).then_inc(*y_stored[s].rise("y"))

                    passes(sp, body)
                    for s in range(S):
                        sp.wait_ge(y_stored[s].sem, y_stored[s].at(PASSES - 1, "y"))
                        if L.store_ct:
                            sp.wait_ge(ct_stored[s].sem, ct_stored[s].at(PASSES - 1, "lo"))

                @block.tensor
                def _(pe):
                    def split_product(dst_ap, lhs, rhs, start=True, stop=True):
                        n = len(lhs)
                        for i, (a, b) in enumerate(zip(lhs, rhs)):
                            for j, (x, w) in enumerate(((a[0], b[0]), (a[0], b[1]), (a[1], b[0]))):
                                last = nc.tensor.matmul(dst_ap, x, w, start=start and i == 0 and j == 0,
                                                        stop=stop and i == n - 1 and j == 2)
                        return last

                    def body(p, prep, rest):
                        it = p + 1
                        order = [u for u in body_uses if (prep if phase_of[u] == "prep" else rest)]

                        def pass_of(key):
                            return it if phase_of[key] == "prep" else p

                        def take(key):
                            before = [u for u in order[:order.index(key)] if bank_of[u] == bank_of[key]]
                            if before:
                                u = before[-1]
                                pe.wait_ge(out_of(u).sem, out_of(u).at(pass_of(u), u))
                            elif rest:
                                for phase in ("post", "prep"):
                                    u = [u for u in body_uses if bank_of[u] == bank_of[key] and phase_of[u] == phase]
                                    if u:
                                        g = out_of(u[-1])
                                        pe.wait_ge(g.sem, g.prev(p, u[-1]) if phase == "post" else g.at(p, u[-1]))
                            return bank(key)

                        def turn(key, source):
                            d = take(key)
                            for kt in range(DT):
                                for b in range(G):
                                    last = nc.tensor.transpose(d[:, kt * GT + b * T:kt * GT + b * T + T],
                                                               source[:, b, 128 * kt:128 * kt + 128], ident[:])
                            last.then_inc(*filled(key).rise(key))

                        def turn_inputs():
                            for key in turned:
                                s = key[1]
                                ready, loaded = norm_ready["prep"], (x_loaded if key[0] == "TX" else c_loaded)[s]
                                if L.ln_x if key[0] == "TX" else L.ln_c:
                                    pe.wait_ge(ready.sem, ready.at(it, s))
                                else:
                                    pe.wait_ge(loaded.sem, loaded.at(it, loaded.keys[-1]))
                                turn(key, x_in[s] if key[0] == "TX" else c_tok[s])

                        def transposed_projection(key, w, source, tiles, rows_n):
                            d = take(key)
                            hi, lo = both(w)
                            for t in range(tiles):
                                cut = slice(rows_n * t, rows_n * t + rows_n)
                                last = split_product(
                                    d[0:rows_n, t * GT:t * GT + GT],
                                    [(hi[:, kt, cut], lo[:, kt, cut]) for kt in range(DT)],
                                    [(source[0][:, kt, :], source[1][:, kt, :]) for kt in range(DT)])
                            last.then_inc(*filled(key).rise(key))

                        def projection(key, w, source, width):
                            d = take(key)
                            hi, lo = both(w)
                            for b in range(G):
                                cut = slice(b * T, b * T + T)
                                last = split_product(
                                    d[:, b * width:(b + 1) * width],
                                    [(source[0][:, kt, cut], source[1][:, kt, cut]) for kt in range(DT)],
                                    [(hi[:, kt, :], lo[:, kt, :]) for kt in range(DT)])
                            last.then_inc(*filled(key).rise(key))

                        xs = [(x_hi[s], x_lo[s]) for s in range(S)]
                        cs = [(c_hi[s], c_lo[s]) for s in range(S)]
                        ps = [(p_hi[s], p_lo[s]) for s in range(S)]

                        def queries_and_keys(s):
                            lo = lo_ready["prep"]
                            if not rest:
                                pe.wait_ge(raw_split.sem, raw_split.at(0, len(chunks) - 1))
                            pe.wait_ge(lo.sem, lo.at(it, ("TX", s)))
                            transposed_projection(("Q", s), "q", xs[s], DT, 128)
                            if L.load_ct:
                                pe.wait_ge(c_loaded[s].sem, c_loaded[s].at(it, c_loaded[s].keys[-1]))
                            else:
                                pe.wait_ge(lo.sem, lo.at(it, ("TC", s)))
                            for k in range(KT):
                                transposed_projection(("K", s, k), "k", (cs, xs)[k][s], k_tiles, k_rows)

                        def scores_for_maxima(n, p=p):
                            s, b, h0 = L.units[n]
                            if n % (N // 2) == 0:
                                pe.wait_ge(q_stacked[s].sem, q_stacked[s].at(p, 2))
                                pe.wait_ge(k_stacked[s].sem, k_stacked[s].at(p, k_loads[-1]))
                                if L.float_mask:
                                    pe.wait_ge(mask_lo_ready.sem, mask_lo_ready.at(p, s))
                            pe.wait_ge(a_out.sem, a_out.back(p, n, 2))
                            a = ps_a[n % 2]
                            cut = slice(b * T, b * T + T)
                            for i in range(U):
                                last = nc.tensor.matmul(
                                    a[:, i * KT * T:(i + 1) * KT * T], q_stack[s][:, h0 + i, cut],
                                    k_stack[s][:, :, (h0 + i) // L.group, cut] if KT == 2 else
                                    k_stack[s][:, 0, (h0 + i) // L.group, cut])
                            last.then_inc(*a_full.rise(n))

                        def turn_maxima(n):
                            pe.wait_ge(m_ready.sem, m_ready.at(p, n))
                            d = take(("MT", n))
                            nc.tensor.transpose(d[:, 0:64].bitcast(BF16), m_parts[:, n % 2, :], ident_b[:]).then_inc(
                                *filled(("MT", n)).rise(("MT", n)))

                        def scores_less_maxima(n):
                            s, b, h0 = L.units[n]
                            pe.wait_ge(out_of(("MT", n)).sem, out_of(("MT", n)).at(p, ("MT", n)))
                            cut = slice(b * T, b * T + T)
                            for f in range(2):
                                pe.wait_ge(b_out.sem, b_out.back(p, (n, f), 2))
                                d = ps_b[f]
                                if L.float_mask:
                                    for j, m in enumerate((hid_hi[s], hid_lo[s])):
                                        nc.tensor.matmul(d[:], m[:].rearrange("p a b -> p (a b)")[:, cut],
                                                         repeat(ident_r[:], 4), start=j == 0, stop=False,
                                                         skip_group_check=True)
                                for j in range(4):
                                    i, k = (j, f) if KT == 2 else (4 * f + j, 0)
                                    to = d[:, j * T:(j + 1) * T]
                                    nc.tensor.matmul(to, k_stack[s][:, k, (h0 + i) // L.group, cut],
                                                     q_stack[s][:, h0 + i, cut], start=not L.float_mask, stop=False,
                                                     skip_group_check=L.float_mask)
                                    last = nc.tensor.matmul(to, select[:, i, :], m_rows[:, n % 2, :], start=False,
                                                            stop=True, skip_group_check=L.float_mask)
                                last.then_inc(*b_full.rise((n, f)))

                        def weighted_values(n):
                            s, b, h0 = L.units[n]
                            if n % (N // 2) == 0:
                                for k in range(KT):
                                    v = out_of(("V", s, k))
                                    pe.wait_ge(v.sem, v.at(p, ("V", s, k)))
                            pe.wait_ge(b_out.sem, b_out.at(p, (n, 1)))
                            d = take(("PV", n))
                            for k in range(KT):
                                for i in range(U):
                                    half, j = (k, i) if KT == 2 else (i // 4, i % 4)
                                    e = probs[:, (2 * n + half) % 4, j * T:(j + 1) * T]
                                    last = nc.tensor.matmul(
                                        d[32 * (i % 4):32 * (i % 4) + 32, (i // 4) * T:(i // 4) * T + T],
                                        value[s][:, b * KT + k, (h0 + i) // L.group, :], e, start=k == 0,
                                        stop=k == KT - 1)
                            last.then_inc(*filled(("PV", n)).rise(("PV", n)))

                        def turn_outputs(n):
                            pv = out_of(("PV", n))
                            pe.wait_ge(pv.sem, pv.at(p, ("PV", n)))
                            d = take(("OT", n))
                            for i in range(U // 4):
                                last = nc.tensor.transpose(d[:, i * T:(i + 1) * T], o_t[:, i * T:(i + 1) * T], ident[:])
                            last.then_inc(*filled(("OT", n)).rise(("OT", n)))

                        if rest:
                            scores_for_maxima(1)
                            for n in range(N + 2):
                                if n < N:
                                    turn_maxima(n)
                                if n + 2 < N:
                                    scores_for_maxima(n + 2)
                                if n >= 2:
                                    turn_outputs(n - 2)
                                if n < N:
                                    scores_less_maxima(n)
                                if 1 <= n <= N:
                                    weighted_values(n - 1)

                        if prep:
                            turn_inputs()
                        if rest:
                            for s in range(S):
                                ot = ("OT", last_unit[s])
                                pe.wait_ge(out_of(ot).sem, out_of(ot).at(p, ot))
                                turn(("TO", s), heads_out[s])
                        if prep:
                            queries_and_keys(0)
                        if rest:
                            for s in range(S):
                                pe.wait_ge(lo_ready["post"].sem, lo_ready["post"].at(p, ("TO", s)))
                                projection(("O", s), "o", ps[s], D)
                        if prep:
                            queries_and_keys(1)
                        for key in outputs[:KT] if prep else ():
                            projection(key, "v", (cs, xs)[key[2]][key[1]], kc)
                        if rest and L.mlp:
                            for s in range(S):
                                pe.wait_ge(norm_ready["post"].sem, norm_ready["post"].at(p, s))
                                turn(("TL", s), norm[s])
                        for key in outputs[KT:] if prep else ():
                            projection(key, "v", (cs, xs)[key[2]][key[1]], kc)

                        if rest and L.mlp:
                            wait_for_late_chunks(pe)
                            f_hi, f_lo = both("f")
                            g_hi, g_lo = both("m")

                            def hidden(s, c):
                                d = take(("F", s, c))
                                for j in range(2):
                                    cut = slice((2 * c + j) * 128, (2 * c + j) * 128 + 128)
                                    last = split_product(
                                        d[:, j * GT:(j + 1) * GT],
                                        [(f_hi[:, kt, cut], f_lo[:, kt, cut]) for kt in range(DT)],
                                        [(p_hi[s][:, kt, :], p_lo[s][:, kt, :]) for kt in range(DT)])
                                last.then_inc(*filled(("F", s, c)).rise(("F", s, c)))

                            def mlp_out(s, c):
                                pe.wait_ge(hid_lo_ready.sem, hid_lo_ready.at(p, (s, c)))
                                if c == 0:
                                    pe.wait_ge(a_out.sem, a_out.back(p, ("M", s), 2))
                                hi, lo = hid_hi[c % 2], hid_lo[c % 2]
                                for b in range(G):
                                    cut = slice(b * T, b * T + T)
                                    last = split_product(
                                        ps_a[s][:, 512 * b:512 * b + D],
                                        [(hi[:, j, cut], lo[:, j, cut]) for j in range(2)],
                                        [(g_hi[:, 2 * c + j, :], g_lo[:, 2 * c + j, :]) for j in range(2)],
                                        start=c == 0, stop=c == FT // 2 - 1)
                                last.then_inc(*hid_used.rise((s, c)))

                            all_chunks = [(s, c) for s in range(S) for c in chunks_f]
                            for i, (s, c) in enumerate(all_chunks):
                                if c == 0:
                                    pe.wait_ge(lo_ready["post"].sem, lo_ready["post"].at(p, ("TL", s)))
                                hidden(s, c)
                                if i:
                                    mlp_out(*all_chunks[i - 1])
                            if prep:
                                scores_for_maxima(0, it)
                            mlp_out(*all_chunks[-1])
                        elif prep:
                            scores_for_maxima(0, it)

                    if L.name == "L3":
                        turn_chunks(pe)
                    passes(pe, body)

                @block.scalar
                def _(act):
                    def body(p, prep, rest):
                        it = p + 1

                        def full(key):
                            act.wait_ge(filled(key).sem, filled(key).at(it if phase_of[key] == "prep" else p, key))
                            return bank(key)

                        def turned_out(key, to, w_col=None, b_col=None):
                            d = full(key)
                            if w_col is None:
                                nc.scalar.activation(to[:].rearrange("p a b -> p (a b)"), d[:],
                                                     ACT.Copy).then_inc(*out_of(key).rise(key))
                                return
                            for kt in range(DT):
                                last = nc.scalar.activation(
                                    to[:, kt, :], d[:, kt * GT:kt * GT + GT], ACT.Identity,
                                    scale=cols[:, w_col + kt:w_col + kt + 1],
                                    bias=cols[:, b_col + kt:b_col + kt + 1] if b_col is not None else 0.0)
                            last.then_inc(*out_of(key).rise(key))

                        def projected_out(key):
                            i = projected.index(key)
                            d = full(key)
                            act.wait_ge(parts_ready.sem, parts_ready.back(it, key, 2))
                            is_q = key[0] == "Q"
                            rows_n, tiles = (128, DT) if is_q else (k_rows, k_tiles)
                            for t in range(tiles):
                                col = (Q_COL if is_q else K_COL) + t
                                last = nc.scalar.activation(
                                    qk32[i % 2][0:rows_n, t, :], d[0:rows_n, t * GT:t * GT + GT], ACT.Identity,
                                    scale=L.scale if is_q else 1.0,
                                    bias=cols[0:rows_n, col:col + 1] if "q" in vectors else 0.0)
                            last.then_inc(*out_of(key).rise(key))

                        for n in range(N + 1 if rest else 0):
                            if n < N:
                                d = full(("MT", n))
                                nc.scalar.activation(m_rows[:, n % 2, :], d[:, 0:64].bitcast(BF16), ACT.Copy).then_inc(
                                    *out_of(("MT", n)).rise(("MT", n)))
                            if n < N:
                                for f in range(2):
                                    act.wait_ge(b_full.sem, b_full.at(p, (n, f)))
                                    nc.scalar.activation(probs[:, (2 * n + f) % 4, :], ps_b[f][:], ACT.Exp).then_inc(
                                        *b_out.rise((n, f)))
                            if n:
                                d = full(("PV", n - 1))
                                ot = d_full["att"]
                                act.wait_ge(ot.sem, ot.prev(p, ("OT", N - 1)) if n == 1 else ot.at(p, ("OT", n - 2)))
                                nc.scalar.activation(o_t[:, 0:U * 32], d[:, 0:U * 32], ACT.Copy).then_inc(
                                    *out_of(("PV", n - 1)).rise(("PV", n - 1)))

                        if prep:
                            for i, key in enumerate(turned):
                                lo = lo_ready["prep"]
                                act.wait_ge(lo.sem, lo.back(it, key, 2))
                                norm_cols = (W1_COL, B1_COL) if (L.ln_x if key[0] == "TX" else L.ln_c) else ()
                                turned_out(key, t32[i % 2], *norm_cols)
                        if rest:
                            wait_for_late_chunks(act)
                            for s in range(S):
                                if L.mlp:
                                    act.wait_ge(hid_lo_ready.sem, hid_lo_ready.prev(p, (S - 1, FT // 2 - 2 + s)))
                                else:
                                    act.wait_ge(lo_ready["post"].sem, lo_ready["post"].prev(p, ("TO", s)))
                                turned_out(("TO", s), hid32[s])
                        if prep:
                            for key in projected:
                                projected_out(key)
                        if rest and L.mlp:
                            nc.scalar.activation(act_spare[:, 0:1], minus_half[:, 0:1], ACT.Gelu_apprx_tanh)
                            for s in range(S):
                                act.wait_ge(lo_ready["post"].sem, lo_ready["post"].at(p, ("TO", s)))
                                turned_out(("TL", s), hid32[s], W2_COL, B2_COL if "b2" in vectors else None)
                            for s in range(S):
                                for c in chunks_f:
                                    d = full(("F", s, c))
                                    if (s, c) in ((0, 0), (0, 1)):
                                        act.wait_ge(lo_ready["post"].sem, lo_ready["post"].at(p, ("TL", c)))
                                    else:
                                        act.wait_ge(hid_lo_ready.sem, hid_lo_ready.back(p, (s, c), 2))
                                    for j in range(2):
                                        col = F_COL + 2 * c + j
                                        last = nc.scalar.activation(hid32[c % 2][:, j, :], d[:, j * GT:(j + 1) * GT],
                                                                    ACT.Gelu_apprx_tanh, bias=cols[:, col:col + 1])
                                    last.then_inc(*out_of(("F", s, c)).rise(("F", s, c)))
                        if not rest:
                            round_late_chunks(act)
                        if prep and (L.mlp or not rest):
                            nc.scalar.activation(act_spare[:, 1:2], minus_half[:, 0:1], ACT.Exp)

                    load_vectors(act)
                    passes(act, body)

                @block.vector
                def _(dve):
                    def body(p, prep, rest):
                        it = p + 1

                        def full(key):
                            dve.wait_ge(filled(key).sem, filled(key).at(it if phase_of[key] == "prep" else p, key))
                            return bank(key)

                        def in_sbuf(key):
                            dve.wait_ge(out_of(key).sem, out_of(key).at(it if phase_of[key] == "prep" else p, key))

                        def here():
                            dve.wait_ge(step.sem, step.now())

                        def norm_stats(phase, s, source):
                            for b in range(G):
                                nc.vector.bn_stats(out=stats[:, s, b, :], in_=source[:, b, :]).then_inc(*step.tick())
                            here()
                            nc.vector.tensor_copy(spare[:], minus_half[:, 0:1])
                            for b in range(G):
                                nc.vector.bn_aggr(out=moments[:, s, b, :], in_=stats[:, s, b, :]).then_inc(*step.tick())
                            here()
                            if L.name == "L2":
                                nc.vector.tensor_tensor(out=spread[:, s, :], in0=moments[:, s, :, 0],
                                                        in1=moments[:, s, :, 0], op=ALU.mult).then_inc(*step.tick())
                                here()
                                nc.vector.scalar_tensor_tensor(
                                    out=spread[:, s, :], in0=moments[:, s, :, 1], scalar=L.eps, in1=spread[:, s, :],
                                    op0=ALU.add, op1=ALU.add).then_inc(*spread_ready[phase].rise(s))
                            else:
                                nc.vector.tensor_scalar(spread[:, s, :], moments[:, s, :, 1], L.eps, None,
                                                        ALU.add).then_inc(*spread_ready[phase].rise(s))

                        def normalise(phase, s, source, to):
                            g = rstd_ready[phase]
                            dve.wait_ge(g.sem, g.at(it if phase == "prep" else p, s))
                            for b in range(G):
                                if L.name == "L2":
                                    last = nc.vector.tensor_scalar(to[:, b, :], source[:, b, :],
                                                                   rstd[:, s, b:b + 1], None, ALU.mult)
                                else:
                                    last = nc.vector.tensor_scalar(to[:, b, :], source[:, b, :],
                                                                   moments[:, s, b, 0:1], rstd[:, s, b:b + 1],
                                                                   ALU.subtract, ALU.mult)
                            last.then_inc(*norm_ready[phase].rise(s))

                        def hi_half(key, to, of):
                            in_sbuf(key)
                            if key[0] == "TC" and L.store_ct:
                                g = ct_stored[key[1]]
                                dve.wait_ge(g.sem, g.prev(it, "lo"))
                            nc.vector.tensor_copy(to[:], of[:]).then_inc(*hi_ready[phase_of[key]].rise(key))

                        def both_halves(key):
                            s = key[1]
                            hi_half(key, p_hi[s], hid32[s])
                            dve.wait_ge(hi_ready["post"].sem, hi_ready["post"].at(p, key))
                            nc.vector.tensor_tensor(out=p_lo[s][:], in0=hid32[s][:], in1=f32(p_hi[s][:]),
                                                    op=ALU.subtract).then_inc(*lo_ready["post"].rise(key))

                        def three_parts(n):
                            key = projected[n]
                            in_sbuf(key)
                            g = written[projected[n - 2]]
                            dve.wait_ge(g.sem, g.at(it, "parts") if n >= 2 else g.prev(it, "parts"))
                            rows_n, tiles = (128, DT) if key[0] == "Q" else (k_rows, k_tiles)
                            rest_of = qk32[n % 2][0:rows_n, 0:tiles, :]
                            part = [parts[n % 2][0:rows_n, i, 0:tiles, :] for i in range(3)]
                            nc.vector.tensor_copy(part[0], rest_of).then_inc(*step.tick())
                            here()
                            nc.vector.tensor_tensor(out=rest_of, in0=rest_of, in1=part[0], op=ALU.subtract).then_inc(
                                *step.tick())
                            here()
                            nc.vector.tensor_copy(part[1], rest_of).then_inc(*step.tick())
                            here()
                            nc.vector.tensor_tensor(out=part[2], in0=rest_of, in1=part[1], op=ALU.subtract).then_inc(
                                *parts_ready.rise(key))

                        def values_out(key):
                            s, k = key[1:]
                            d = full(key)
                            for b in range(G):
                                to = value[s][:, b * KT + k, :, 0:HD]
                                of = by_head(d[:, b * kc:(b + 1) * kc])
                                if "q" in vectors:
                                    last = nc.vector.tensor_tensor(out=to, in0=of, in1=by_head(rows[:, V_BIAS, 0:kc]),
                                                                   op=ALU.add)
                                else:
                                    last = nc.vector.tensor_copy(to, of)
                            last.then_inc(*out_of(key).rise(key))

                        def masked_maxima(n):
                            s, b, h0 = L.units[n]
                            nc.vector.tensor_copy(spare[:], minus_half[:, 0:1])
                            for i in range(U):
                                last = nc.vector.tensor_tensor_reduce(
                                    out=t32[i // 4][:].rearrange("p a b -> p (a b)")[:, i % 4 * T:(i % 4 + 1) * T],
                                    in0=ps_a[n % 2][:, i * T:(i + 1) * T], in1=c_tok[s][:, b, 0:T], scale=1.0,
                                    scalar=-LARGEST, op0=ALU.add, op1=ALU.max, accum_out=m_neg[:, n % 2, i:i + 1])
                                if i < U - 1:
                                    last.then_inc(*step.tick())
                            last.then_inc(*a_out.rise(n))
                            dve.wait_ge(a_out.sem, a_out.at(p, n))
                            nc.vector.tensor_scalar(m_parts[:, n % 2, 0:U], m_neg[:, n % 2, 0:U], -1.0, None,
                                                    ALU.mult).then_inc(*step.tick())
                            here()
                            nc.vector.scalar_tensor_tensor(
                                out=m_parts[:, n % 2, 8:8 + U], in0=m_neg[:, n % 2, 0:U], scalar=-1.0,
                                in1=m_parts[:, n % 2, 0:U], op0=ALU.mult, op1=ALU.subtract).then_inc(
                                *m_ready.rise(n))

                        def maxima(n):
                            dve.wait_ge(a_full.sem, a_full.at(p, n))
                            if L.float_mask:
                                masked_maxima(n)
                                return
                            nc.vector.tensor_reduce(out=m_neg[:, n % 2, 0:U],
                                                    in_=ps_a[n % 2][:].rearrange("p (h k) -> p h k", h=U), axis=AX.X,
                                                    op=ALU.max, negate=True).then_inc(*a_out.rise(n))
                            dve.wait_ge(a_out.sem, a_out.at(p, n))
                            nc.vector.tensor_copy(m_parts[:, n % 2, 0:U], m_neg[:, n % 2, 0:U]).then_inc(*step.tick())
                            here()
                            nc.vector.tensor_tensor(out=m_parts[:, n % 2, 8:8 + U], in0=m_neg[:, n % 2, 0:U],
                                                    in1=m_parts[:, n % 2, 0:U], op=ALU.subtract).then_inc(
                                *m_ready.rise(n))

                        def divide(n):
                            s, b, h0 = L.units[n]
                            if n == 0:
                                wait_for_late_chunks(dve, 2 * G - 1)
                            if n % (N // 2) == 0:
                                dve.wait_ge(y_stored[s].sem, y_stored[s].prev(p, "y"))
                            key = ("OT", n)
                            d = full(key)[:, 0:U * 32].rearrange("p (h e) -> p h e", e=32)
                            nc.vector.reciprocal(r_inv[:, n % 2, 0:U].unsqueeze(2), d[:, :, HD:HD + 1]).then_inc(
                                *step.tick())
                            here()
                            nc.vector.tensor_tensor(
                                out=by_head(heads_out[s][:, b, h0 * HD:(h0 + U) * HD]), in0=d[:, :, 0:HD],
                                in1=r_inv[:, n % 2, 0:U].unsqueeze(2).broadcast_to([128, U, HD]),
                                op=ALU.mult).then_inc(*out_of(key).rise(key))

                        def mlp_added(s):
                            dve.wait_ge(hid_used.sem, hid_used.at(p, (s, FT // 2 - 1)))
                            nc.vector.tensor_tensor(
                                out=heads_out[s][:], in0=ps_a[s][:].rearrange("p (b n) -> p b n", b=G)[:, :, 0:D],
                                in1=(x_tok if L.name == "L2" else heads_out)[s][:], op=ALU.add).then_inc(
                                *a_out.rise(("M", s)))
                            dve.wait_ge(a_out.sem, a_out.at(p, ("M", s)))
                            nc.vector.tensor_tensor(out=heads_out[s][:], in0=heads_out[s][:],
                                                    in1=repeat(rows[:, M_BIAS, :], G), op=ALU.add).then_inc(
                                *y_ready.rise(s))

                        in_tok, in_loaded = (x_in, x_loaded) if L.ln_x else (c_tok, c_loaded)

                        def input_stats():
                            for s in normed["prep"]:
                                g = in_loaded[s]
                                dve.wait_ge(g.sem, g.at(it, g.keys[-1]))
                                norm_stats("prep", s, in_tok[s])

                        def normalise_inputs():
                            for s in normed["prep"]:
                                normalise("prep", s, in_tok[s], in_tok[s])

                        if not rest:
                            input_stats()
                            normalise_inputs()
                        for n in range(N + 3 if rest else 0):
                            if n < N:
                                maxima(n)
                            if prep and n == N:
                                input_stats()
                            if n >= 3:
                                divide(n - 3)
                            if prep and n == N:
                                normalise_inputs()

                        if prep:
                            for i, key in enumerate(turned):
                                s = key[1]
                                hi_half(key, c_hi[s] if key[0] == "TC" else x_hi[s], t32[i % 2])
                            if L.float_mask:
                                for s in range(S):
                                    dve.wait_ge(c_loaded[s].sem, c_loaded[s].at(it, "mask"))
                                    dve.wait_ge(b_full.sem, b_full.prev(it, (last_unit[s], 1)))
                                    nc.vector.tensor_scalar(c_tok[s][:, :, 0:T], c_tok[s][:, :, 0:T], -BIG, None,
                                                            ALU.max).then_inc(*step.tick())
                                    here()
                                    nc.vector.tensor_copy(hid_hi[s][:].rearrange("p a b -> p (a b)")[:, 0:GT],
                                                          c_tok[s][:, :, 0:T]).then_inc(*mask_hi_ready.rise(s))
                        if rest:
                            for s in range(S):
                                both_halves(("TO", s))
                        if prep:
                            three_parts(0)
                        for s in range(S if rest else 0):
                            d = full(("O", s))
                            dve.wait_ge(residual_loaded[s].sem, residual_loaded[s].at(p, "x"))
                            h = heads_out[s][:].rearrange("p b d -> p (b d)")
                            if L.name == "L3":
                                for b in range(G):
                                    last = nc.vector.scalar_tensor_tensor(
                                        out=heads_out[s][:, b, :], in0=d[:, b * D:(b + 1) * D],
                                        scalar=gate[:, bass.ds(p * (G * S) + (2 + s * G + b), 1)],
                                        in1=x_tok[s][:, b, :], op0=ALU.mult, op1=ALU.add)
                                last.then_inc(*out_of(("O", s)).rise(("O", s)))
                                continue
                            nc.vector.tensor_tensor(out=h, in0=d[:], in1=x_tok[s][:].rearrange("p b d -> p (b d)"),
                                                    op=ALU.add).then_inc(*out_of(("O", s)).rise(("O", s)))
                            dve.wait_ge(out_of(("O", s)).sem, out_of(("O", s)).at(p, ("O", s)))
                            nc.vector.tensor_tensor(out=heads_out[s][:], in0=heads_out[s][:],
                                                    in1=repeat(rows[:, O_BIAS, :], G), op=ALU.add).then_inc(*step.tick())
                            here()
                            norm_stats("post", s, heads_out[s])
                        if prep:
                            for n in range(1, first_half):
                                three_parts(n)
                        if rest and L.name != "L3":
                            wait_for_late_chunks(dve)
                            for s in range(S):
                                if L.float_mask:
                                    dve.wait_ge(y_stored[s].sem, y_stored[s].prev(p, "y"))
                                normalise("post", s, heads_out[s], norm[s])
                        last_parts = list(range(first_half, len(projected)))
                        if prep:
                            while len(last_parts) > (2 if rest and L.mlp else 0):
                                three_parts(last_parts.pop(0))
                        if not rest:
                            dve.wait_ge(stacks_clear.sem, stacks_clear.at(0, clears[-1]))
                        for key in outputs[:KT] if prep else ():
                            values_out(key)
                        if rest and L.mlp:
                            for s in range(S):
                                both_halves(("TL", s))
                        for key in outputs[KT:] if prep else ():
                            values_out(key)
                        if rest and L.mlp:
                            for s in range(S):
                                for c in chunks_f:
                                    in_sbuf(("F", s, c))
                                    dve.wait_ge(hid_used.sem, hid_used.back(p, (s, c), 2))
                                    nc.vector.tensor_copy(hid_hi[c % 2][:], hid32[c % 2][:]).then_inc(
                                        *hid_hi_ready.rise((s, c)))
                                    if prep and last_parts:
                                        three_parts(last_parts.pop(0))
                                    if (s, c) == (1, 0):
                                        mlp_added(0)
                            mlp_added(1)

                    split_chunks(dve)
                    body(-1, prep=True, rest=False)
                    with dve.Fori(0, PASSES - 1) as p:
                        step.enter(p, STEPS[L.name])
                        body(p, prep=True, rest=True)
                    step.leave(L.name, PASSES - 1)
                    body(PASSES - 1, prep=False, rest=True)

                @block.gpsimd
                def _(pool):
                    def body(p, prep, rest):
                        it = p + 1

                        def power(phase, s):
                            g = spread_ready[phase]
                            pool.wait_ge(g.sem, g.at(it if phase == "prep" else p, s))
                            nc.gpsimd.tensor_tensor(out=rstd[:, s, :], in0=spread[:, s, :],
                                                    in1=minus_half[:], op=ALU.pow).then_inc(*rstd_ready[phase].rise(s))

                        def lo_half(key, of, hi, lo):
                            g = hi_ready[phase_of[key]]
                            pool.wait_ge(g.sem, g.at(it if phase_of[key] == "prep" else p, key))
                            nc.gpsimd.tensor_tensor(out=lo[:], in0=of[:], in1=f32(hi[:]),
                                                    op=ALU.subtract).then_inc(*lo_ready[phase_of[key]].rise(key))

                        if prep:
                            for s in normed["prep"]:
                                power("prep", s)
                            for i, key in enumerate(turned):
                                s = key[1]
                                lo_half(key, t32[i % 2], *((c_hi[s], c_lo[s]) if key[0] == "TC" else (x_hi[s], x_lo[s])))
                            if L.float_mask:
                                for s in range(S):
                                    pool.wait_ge(mask_hi_ready.sem, mask_hi_ready.at(it, s))
                                    nc.gpsimd.tensor_tensor(
                                        out=hid_lo[s][:].rearrange("p a b -> p (a b)")[:, 0:GT].rearrange(
                                            "p (b k) -> p b k", b=G),
                                        in0=c_tok[s][:, :, 0:T],
                                        in1=f32(hid_hi[s][:].rearrange("p a b -> p (a b)")[:, 0:GT]).rearrange(
                                            "p (b k) -> p b k", b=G), op=ALU.subtract).then_inc(*mask_lo_ready.rise(s))
                        if rest:
                            for s in normed["post"]:
                                power("post", s)
                        if rest and L.float_mask:
                            for s in range(S):
                                pool.wait_ge(norm_ready["post"].sem, norm_ready["post"].at(p, s))
                                nc.gpsimd.tensor_tensor(out=norm[s][:], in0=norm[s][:], in1=repeat(rows[:, GAMMA, :], G),
                                                        op=ALU.mult).then_inc(*scaled.rise(s))
                                pool.wait_ge(scaled.sem, scaled.at(p, s))
                                nc.gpsimd.tensor_tensor(out=norm[s][:], in0=norm[s][:], in1=repeat(rows[:, BETA, :], G),
                                                        op=ALU.add).then_inc(*y_ready.rise(s))
                        if rest and L.mlp:
                            for s in range(S):
                                for c in chunks_f:
                                    pool.wait_ge(hid_hi_ready.sem, hid_hi_ready.at(p, (s, c)))
                                    nc.gpsimd.tensor_tensor(out=hid_lo[c % 2][:], in0=hid32[c % 2][:],
                                                            in1=f32(hid_hi[c % 2][:]), op=ALU.subtract).then_inc(
                                        *hid_lo_ready.rise((s, c)))
                        if not rest:
                            rest_of_late_chunks(pool)

                    clear_stacks(pool)
                    passes(pool, body)
            finish()


def kernel(**inputs):
    import numpy as _np
    import concourse.bacc as _bacc
    from concourse import mybir as _mybir
    from concourse.bass_utils import run_bass_kernel_spmd as _run

    nc = _bacc.Bacc("TRN2", target_bir_lowering=False, num_devices=1)
    arrays, ins = {}, {}
    for name, a in inputs.items():
        a = _np.ascontiguousarray(a)
        if a.dtype == _np.bool_:
            a = a.view(_np.uint8)
        arrays[f"in_{name}_dram"] = a
        ins[name] = nc.dram_tensor(f"in_{name}_dram", a.shape, _mybir.dt.from_np(a.dtype), kind="ExternalInput").ap()
    out = nc.dram_tensor("out_dram", (B, T, D), _mybir.dt.float32, kind="ExternalOutput").ap()
    xattn_program(nc, ins, out)
    r = _run(nc, [arrays], core_ids=[0])
    return r.results[0]["out_dram"]
```
